# Optimizing a Trainium2 kernel written in Bass

```python
import numpy as np
import jax
import jax.numpy as jnp

def _softmax(x, axis=-1):
    return jax.nn.softmax(x, axis=axis)

def _gelu(x):
    return jax.nn.gelu(x, approximate=True)

def _silu(x):
    return jax.nn.silu(x)

def _sigmoid(x):
    return jax.nn.sigmoid(x)

def _layernorm(x, axis=-1, eps=1e-05):
    m = jnp.mean(x, axis=axis, keepdims=True)
    v = jnp.var(x, axis=axis, keepdims=True)
    return (x - m) / jnp.sqrt(v + eps)

def _scatter_add(tgt, idx, src, axis=0):
    return tgt.at[idx].add(src)

def _segment_sum(src, seg, n):
    return jax.ops.segment_sum(src, seg, n)
kernel_name = 'mk_xattn_ffn_d2_seqx_r8_9bd6ae'

def setup_inputs(seed: int=0):
    np.random.seed(seed)
    _w = jnp.asarray

    def _rec_inputs():
        import jax
        import jax.numpy as jnp
        _rk = jax.random.key(seed)
        x = -0.0002928 + 1 * jax.random.normal(jax.random.fold_in(_rk, 1), (16, 256, 128), jnp.float32)
        _lenS = 256 - jax.random.randint(jax.random.fold_in(_rk, 7), (16,), 0, max(1, 256 // 4) + 1, jnp.int32)
        _lenS2 = 1601 - jax.random.randint(jax.random.fold_in(_rk, 8), (16,), 0, max(1, 1601 // 4) + 1, jnp.int32)
        _ctx_1024P = jax.random.normal(jax.random.fold_in(_rk, 11), (16, 16, 128), jnp.float32)
        _ctx_1024c = jax.random.dirichlet(jax.random.fold_in(_rk, 511), 0.3 * jnp.ones((16,), jnp.float32), (16, 1601))
        _ctx_1024t = jnp.einsum('bsk,bkd->bsd', _ctx_1024c, _ctx_1024P)
        _ctx_1024t = _ctx_1024t * jax.lax.rsqrt(jnp.mean(jnp.square(_ctx_1024t)) + 1e-12) * 0.953939
        ctx_1024 = -1.39393e-06 + 0.999914 * (_ctx_1024t + 0.3 * jax.random.normal(jax.random.fold_in(_rk, 611), (16, 1601, 128), jnp.float32))
        _validS = jnp.arange(256)[None, :] < _lenS[:, None]
        _validS2 = jnp.arange(1601)[None, :] < _lenS2[:, None]
        _causal = jnp.tril(jnp.ones((256, 256), dtype=bool))
        mask_BxSxS2_ik1 = jnp.where(jnp.broadcast_to(_validS2[:, None, :], (16, 256, 1601)), 1, 0).astype(jnp.int32)
        mask_BxS_ik0 = jnp.where(jnp.broadcast_to(_validS[:, :], (16, 256)), 0, 1).astype(jnp.int32)
        return (x, ctx_1024, mask_BxSxS2_ik1, mask_BxS_ik0)
    x, ctx_1024, mask_BxSxS2_ik1, mask_BxS_ik0 = _rec_inputs()

    def _L0_xattn_setup():
        import jax, jax.numpy as jnp
        import numpy as np
        H = 16
        D_MODEL = 128
        D_K = D_MODEL // H
        B, S = (2, 256)
        SCALE = 1.0 / 8.0
        MASK_FILL = -1000000000.0
        key = jax.random.key(seed)
        ks = jax.random.split(key, 12)
        s = 1.0 / np.sqrt(D_MODEL)
        return {'query': jax.random.normal(ks[0], (B, S, D_MODEL), jnp.float32), 'key': jax.random.normal(ks[1], (B, S, D_MODEL), jnp.float32), 'value': jax.random.normal(ks[2], (B, S, D_MODEL), jnp.float32), 'mask': jax.random.randint(ks[3], (B, S, S), 0, 2, jnp.int32), 'Wq': jax.random.uniform(ks[4], (H, D_MODEL, D_K), jnp.float32, -s, s), 'bq': jax.random.uniform(ks[5], (H, D_K), jnp.float32, -s, s), 'Wk': jax.random.uniform(ks[6], (H, D_MODEL, D_K), jnp.float32, -s, s), 'bk': jax.random.uniform(ks[7], (H, D_K), jnp.float32, -s, s), 'Wv': jax.random.uniform(ks[8], (H, D_MODEL, D_K), jnp.float32, -s, s), 'bv': jax.random.uniform(ks[9], (H, D_K), jnp.float32, -s, s), 'Wo': jax.random.uniform(ks[10], (D_MODEL, D_MODEL), jnp.float32, -s, s), 'bo': jax.random.uniform(ks[11], (D_MODEL,), jnp.float32, -s, s)}
    _L0_xattn_all = _L0_xattn_setup()
    _L0_xattn_in = {k: v for k, v in _L0_xattn_all.items() if k in ('Wq', 'bq', 'Wk', 'bk', 'Wv', 'bv', 'Wo', 'bo')}
    del _L0_xattn_all

    def _L0_ffn_setup():
        import jax, jax.numpy as jnp
        import numpy as np
        D_MODEL = 128
        E = 4
        MIN_E = 1
        TH_LO = 0.5
        TH_HI = 2.0
        key = jax.random.key(seed)
        ks = jax.random.split(key, 12)
        B, N, D, H = (4, 256, D_MODEL, 2 * D_MODEL)
        s = 0.02
        return {'x': jax.random.normal(ks[0], (B, N, D), dtype=jnp.float32), 'gate_w': jax.random.normal(ks[1], (D, E), dtype=jnp.float32) * s, 'gate_b': jnp.zeros((E,), dtype=jnp.float32), 'dp_w1': jax.random.normal(ks[2], (D, D // 2), dtype=jnp.float32) * s, 'dp_b1': jnp.zeros((D // 2,), dtype=jnp.float32), 'dp_w2': jax.random.normal(ks[3], (D // 2, 1), dtype=jnp.float32) * s, 'dp_b2': jnp.zeros((1,), dtype=jnp.float32), 'ew1': jax.random.normal(ks[4], (E, D, H), dtype=jnp.float32) * s, 'eb1': jnp.zeros((E, H), dtype=jnp.float32), 'ew2': jax.random.normal(ks[5], (E, H, D), dtype=jnp.float32) * s, 'eb2': jnp.zeros((E, D), dtype=jnp.float32)}
    _L0_ffn_all = _L0_ffn_setup()
    _L0_ffn_in = {k: v for k, v in _L0_ffn_all.items() if k in ('gate_w', 'gate_b', 'dp_w1', 'dp_b1', 'dp_w2', 'dp_b2', 'ew1', 'eb1', 'ew2', 'eb2')}
    del _L0_ffn_all

    def _L1_xattn_setup():
        import jax, jax.numpy as jnp
        import numpy as np
        HEADS = 16
        DIM_HEAD = 64
        SCALE = DIM_HEAD ** (-0.5)
        MASK_NEG = 1000000.0

        def _split_heads(t):
            b, n, _ = t.shape
            return t.reshape(b, n, HEADS, DIM_HEAD).transpose(0, 2, 1, 3)
        key = jax.random.key(seed)
        ks = jax.random.split(key, 6)
        B, N, M, D = (2, 256, 256, 128)
        inner = HEADS * DIM_HEAD
        x = jax.random.normal(ks[0], (B, N, D), dtype=jnp.float32)
        context = jax.random.normal(ks[1], (B, M, D), dtype=jnp.float32)
        mask = jax.random.randint(ks[2], (B, N), 0, 2, dtype=jnp.int32)
        Wq = jax.random.normal(ks[3], (D, inner), dtype=jnp.float32) * D ** (-0.5)
        Wkv = jax.random.normal(ks[4], (D, 2 * inner), dtype=jnp.float32) * D ** (-0.5)
        Wout = jax.random.normal(ks[5], (inner, D), dtype=jnp.float32) * inner ** (-0.5)
        bout = jnp.zeros((D,), dtype=jnp.float32)
        return {'x': x, 'context': context, 'mask': mask, 'Wq': Wq, 'Wkv': Wkv, 'Wout': Wout, 'bout': bout}
    _L1_xattn_all = _L1_xattn_setup()
    _L1_xattn_in = {k: v for k, v in _L1_xattn_all.items() if k in ('Wq', 'Wkv', 'Wout', 'bout')}
    del _L1_xattn_all

    def _L1_ffn_setup():
        import jax, jax.numpy as jnp
        import numpy as np
        B, S, D = (2, 256, 128)
        E, K, F = (16, 2, 64)
        FS = 128
        key = jax.random.key(seed)
        ks = jax.random.split(key, 8)

        def w(k, shape, fan_in):
            return jax.random.normal(k, shape, jnp.float32) / np.sqrt(fan_in).astype(np.float32)
        return {'x': jax.random.normal(ks[0], (B, S, D), jnp.float32), 'Wr': w(ks[1], (D, E), D), 'Wg': w(ks[2], (E, D, F), D), 'Wu': w(ks[3], (E, D, F), D), 'Wd': w(ks[4], (E, F, D), F), 'Sg': w(ks[5], (D, FS), D), 'Su': w(ks[6], (D, FS), D), 'Sd': w(ks[7], (FS, D), FS)}
    _L1_ffn_all = _L1_ffn_setup()
    _L1_ffn_in = {k: v for k, v in _L1_ffn_all.items() if k in ('Wr', 'Wg', 'Wu', 'Wd', 'Sg', 'Su', 'Sd')}
    del _L1_ffn_all
    return {'x': x, 'ctx_1024': ctx_1024, 'mask_BxSxS2_ik1': mask_BxSxS2_ik1, 'mask_BxS_ik0': mask_BxS_ik0, 'L0_xattn_Wq': _L0_xattn_in['Wq'], 'L0_xattn_bq': _L0_xattn_in['bq'], 'L0_xattn_Wk': _L0_xattn_in['Wk'], 'L0_xattn_bk': _L0_xattn_in['bk'], 'L0_xattn_Wv': _L0_xattn_in['Wv'], 'L0_xattn_bv': _L0_xattn_in['bv'], 'L0_xattn_Wo': _L0_xattn_in['Wo'], 'L0_xattn_bo': _L0_xattn_in['bo'], 'L0_ffn_gate_w': _L0_ffn_in['gate_w'], 'L0_ffn_gate_b': _L0_ffn_in['gate_b'], 'L0_ffn_dp_w1': _L0_ffn_in['dp_w1'], 'L0_ffn_dp_b1': _L0_ffn_in['dp_b1'], 'L0_ffn_dp_w2': _L0_ffn_in['dp_w2'], 'L0_ffn_dp_b2': _L0_ffn_in['dp_b2'], 'L0_ffn_ew1': _L0_ffn_in['ew1'], 'L0_ffn_eb1': _L0_ffn_in['eb1'], 'L0_ffn_ew2': _L0_ffn_in['ew2'], 'L0_ffn_eb2': _L0_ffn_in['eb2'], 'L1_xattn_Wq': _L1_xattn_in['Wq'], 'L1_xattn_Wkv': _L1_xattn_in['Wkv'], 'L1_xattn_Wout': _L1_xattn_in['Wout'], 'L1_xattn_bout': _L1_xattn_in['bout'], 'L1_ffn_Wr': _L1_ffn_in['Wr'], 'L1_ffn_Wg': _L1_ffn_in['Wg'], 'L1_ffn_Wu': _L1_ffn_in['Wu'], 'L1_ffn_Wd': _L1_ffn_in['Wd'], 'L1_ffn_Sg': _L1_ffn_in['Sg'], 'L1_ffn_Su': _L1_ffn_in['Su'], 'L1_ffn_Sd': _L1_ffn_in['Sd']}

def reference(x, ctx_1024, mask_BxSxS2_ik1, mask_BxS_ik0, L0_xattn_Wq, L0_xattn_bq, L0_xattn_Wk, L0_xattn_bk, L0_xattn_Wv, L0_xattn_bv, L0_xattn_Wo, L0_xattn_bo, L0_ffn_gate_w, L0_ffn_gate_b, L0_ffn_dp_w1, L0_ffn_dp_b1, L0_ffn_dp_w2, L0_ffn_dp_b2, L0_ffn_ew1, L0_ffn_eb1, L0_ffn_ew2, L0_ffn_eb2, L1_xattn_Wq, L1_xattn_Wkv, L1_xattn_Wout, L1_xattn_bout, L1_ffn_Wr, L1_ffn_Wg, L1_ffn_Wu, L1_ffn_Wd, L1_ffn_Sg, L1_ffn_Su, L1_ffn_Sd):
    import jax
    import jax.numpy as jnp

    def _L0_xattn_ref(query, key, value, mask, Wq, bq, Wk, bk, Wv, bv, Wo, bo):
        import jax, jax.numpy as jnp
        import numpy as np
        H = 16
        D_MODEL = 128
        D_K = D_MODEL // H
        B, S = (2, 256)
        SCALE = 1.0 / 8.0
        MASK_FILL = -1000000000.0
        Q = jnp.einsum('bsd,hdk->bhsk', query, Wq) + bq[None, :, None, :]
        K = jnp.einsum('bsd,hdk->bhsk', key, Wk) + bk[None, :, None, :]
        V = jnp.einsum('bsd,hdk->bhsk', value, Wv) + bv[None, :, None, :]
        scores = jnp.einsum('bhqk,bhsk->bhqs', Q, K) * SCALE
        scores = jnp.where(mask[:, None, :, :] == 0, MASK_FILL, scores)
        soft = jax.nn.softmax(scores, axis=2)
        out = jnp.einsum('bhqs,bhsv->bhqv', soft, V)
        concat = out.transpose(0, 2, 1, 3).reshape(query.shape[0], query.shape[1], -1)
        return concat @ Wo.T + bo

    def _L0_ffn_ref(x, gate_w, gate_b, dp_w1, dp_b1, dp_w2, dp_b2, ew1, eb1, ew2, eb2):
        import jax, jax.numpy as jnp
        import numpy as np
        D_MODEL = 128
        E = 4
        MIN_E = 1
        TH_LO = 0.5
        TH_HI = 2.0
        B, N, D = x.shape
        xf = x.reshape(B * N, D)
        T = B * N
        h = jax.nn.relu(xf @ dp_w1 + dp_b1)
        entropy = jax.nn.softplus(h @ dp_w2 + dp_b2)[:, 0]
        norm = jnp.clip((entropy - TH_LO) / (TH_HI - TH_LO), 0.0, 1.0)
        k_tok = jnp.clip(jnp.round(MIN_E + norm * (E - MIN_E)).astype(jnp.int32), MIN_E, E)
        logits = xf @ gate_w + gate_b
        top_logits, top_idx = jax.lax.top_k(logits, E)
        pos = jnp.arange(E)
        sel = pos[None, :] < k_tok[:, None]
        masked = jnp.where(sel, top_logits, -jnp.inf)
        w_top = jax.nn.softmax(masked, axis=-1)
        dense_w = jnp.zeros((T, E), dtype=xf.dtype).at[jnp.arange(T)[:, None], top_idx].set(w_top)
        hid = jax.nn.relu(jnp.einsum('td,edh->teh', xf, ew1) + eb1[None, :, :])
        y = jnp.einsum('teh,ehd->ted', hid, ew2) + eb2[None, :, :]
        out = jnp.einsum('te,ted->td', dense_w, y)
        return out.reshape(B, N, D)

    def _L1_xattn_ref(x, context, mask, Wq, Wkv, Wout, bout):
        import jax, jax.numpy as jnp
        import numpy as np
        HEADS = 16
        DIM_HEAD = 64
        SCALE = DIM_HEAD ** (-0.5)
        MASK_NEG = 1000000.0

        def _split_heads(t):
            b, n, _ = t.shape
            return t.reshape(b, n, HEADS, DIM_HEAD).transpose(0, 2, 1, 3)
        kv = context @ Wkv
        k, v = jnp.split(kv, 2, axis=-1)
        q = x @ Wq
        q, k, v = (_split_heads(q), _split_heads(k), _split_heads(v))
        dots = jnp.einsum('bhnd,bhmd->bhnm', q, k) * SCALE
        dots = dots - (1.0 - mask.astype(jnp.float32))[:, None, :, None] * MASK_NEG
        attn = jax.nn.softmax(dots, axis=-1)
        out = jnp.einsum('bhnm,bhmd->bhnd', attn, v)
        b, h, n, d = out.shape
        out = out.transpose(0, 2, 1, 3).reshape(b, n, h * d)
        return out @ Wout + bout

    def _L1_ffn_ref(x, Wr, Wg, Wu, Wd, Sg, Su, Sd):
        import jax, jax.numpy as jnp
        import numpy as np
        B, S, D = (2, 256, 128)
        E, K, F = (16, 2, 64)
        FS = 128
        b, s, d = x.shape
        T = b * s
        xf = x.reshape(T, d)
        shared = jax.nn.silu(xf @ Sg) * (xf @ Su) @ Sd
        probs = jax.nn.softmax(xf @ Wr, axis=-1)
        topk_p, topk_i = jax.lax.top_k(probs, K)
        n_exp = Wr.shape[1]
        cw = jnp.zeros((T, n_exp), x.dtype).at[jnp.arange(T)[:, None], topk_i].add(topk_p)

        def step(acc, ew):
            wg, wu, wd, c = ew
            y = jax.nn.silu(xf @ wg) * (xf @ wu) @ wd
            return (acc + y * c[:, None], None)
        routed, _ = jax.lax.scan(step, jnp.zeros_like(xf), (Wg, Wu, Wd, cw.T))
        return (routed + shared).reshape(b, s, d)
    x = x + _L0_xattn_ref(_layernorm(x, axis=-1), ctx_1024, ctx_1024, mask_BxSxS2_ik1, L0_xattn_Wq, L0_xattn_bq, L0_xattn_Wk, L0_xattn_bk, L0_xattn_Wv, L0_xattn_bv, L0_xattn_Wo, L0_xattn_bo)
    x = x + _L0_ffn_ref(_layernorm(x, axis=-1), L0_ffn_gate_w, L0_ffn_gate_b, L0_ffn_dp_w1, L0_ffn_dp_b1, L0_ffn_dp_w2, L0_ffn_dp_b2, L0_ffn_ew1, L0_ffn_eb1, L0_ffn_ew2, L0_ffn_eb2)
    x = x + _L1_xattn_ref(_layernorm(x, axis=-1), ctx_1024, mask_BxS_ik0, L1_xattn_Wq, L1_xattn_Wkv, L1_xattn_Wout, L1_xattn_bout)
    x = x + _L1_ffn_ref(_layernorm(x, axis=-1), L1_ffn_Wr, L1_ffn_Wg, L1_ffn_Wu, L1_ffn_Wd, L1_ffn_Sg, L1_ffn_Su, L1_ffn_Sd)
    return x

_drawn_inputs = setup_inputs


def setup_inputs(seed=0):
    import zlib

    import numpy as np

    out = dict(_drawn_inputs(seed))
    spreads = {'L0_ffn_gate_b': (0.0, 0.1),
     'L0_ffn_dp_b1': (0.0, 0.1),
     'L0_ffn_eb1': (0.0, 0.394),
     'L0_ffn_eb2': (0.0, 0.1),
     'L1_xattn_bout': (0.0, 0.1)}
    factors = {'L0_xattn_bq': 8.0, 'L0_xattn_bk': 5.235}
    for name, (base, spread) in spreads.items():
        noise = np.random.default_rng([zlib.crc32(name.encode()), seed]).standard_normal(out[name].shape)
        drawn = base * np.exp(spread * noise) if base else spread * noise
        out[name] = jnp.asarray(drawn.astype(out[name].dtype))
    for name, factor in factors.items():
        out[name] = (out[name] * factor).astype(out[name].dtype)
    return out
```

```python
from contextlib import ExitStack

import numpy as np
import concourse.bass as bass
from concourse import mybir
from concourse.bass import ds

F32 = mybir.dt.float32
F16 = mybir.dt.float16
BF16 = mybir.dt.bfloat16
I32 = mybir.dt.int32
U32 = mybir.dt.uint32
ALU = mybir.AluOpType
ACT = mybir.ActivationFunctionType
AX = mybir.AxisListType
P = 128
BANK = 512

MASK_FILL = -1e30
MASK_NEG = 1e6
LN_EPS = 1e-5


class Steps:

    def __init__(self):
        self.n = 0

    def up(self):
        self.n += 1
        return self.n


class Jobs:

    def __init__(self, first, per, banks):
        self.lists, self.banks = (first, per), banks

    def filled(self, n, it=None):
        return n + 1 if it is None else it * len(self.lists[1]) + (len(self.lists[0]) + n + 1)

    def emptied(self, who, n, it=None):
        first, per = ([w == who for _, w in x] for x in self.lists)
        return sum(first[:n]) if it is None else it * sum(per) + (sum(first) + sum(per[:n]))

    def free(self, n, it=None):
        if n >= self.banks:
            who = self.lists[it is not None][n - self.banks][1]
            return [(who, self.emptied(who, n - self.banks + 1, it))]
        if n > 0 or it is None:
            return []
        return [(who, self.emptied(who, 0, it)) for who in sorted({w for x in self.lists for _, w in x})]


def tiles(n, size=P):
    return [(a, min(size, n - a)) for a in range(0, n, size)]


def layernorm(nc, resid, xnT, ident, TT, tag):
    G = 4
    with ExitStack() as ctx:
        stats = ctx.enter_context(nc.sbuf_tensor(f"{tag}_stats", [P, TT, 6], F32))
        mean = ctx.enter_context(nc.sbuf_tensor(f"{tag}_mean", [P, TT], F32))
        var = ctx.enter_context(nc.sbuf_tensor(f"{tag}_var", [P, TT], F32))
        tmp = ctx.enter_context(nc.sbuf_tensor(f"{tag}_tmp", [P, TT], F32))
        rstd = ctx.enter_context(nc.sbuf_tensor(f"{tag}_rstd", [P, TT], F32))
        xn = [ctx.enter_context(nc.sbuf_tensor(f"{tag}_xn{i}", [P, G, P], F32)) for i in range(2)]
        turned = [ctx.enter_context(nc.psum_tensor(f"{tag}_turned{i}", [P, BANK], F32)) for i in range(2)]
        s_stats = ctx.enter_context(nc.semaphore(f"{tag}_stats_done"))
        s_var = ctx.enter_context(nc.semaphore(f"{tag}_var_done"))
        s_std = ctx.enter_context(nc.semaphore(f"{tag}_std_done"))
        s_xn = ctx.enter_context(nc.semaphore(f"{tag}_xn_ready"))
        s_turned = ctx.enter_context(nc.semaphore(f"{tag}_turned_ready"))
        s_out = ctx.enter_context(nc.semaphore(f"{tag}_xnT_written"))
        block = ctx.enter_context(nc.Block())

        @block.vector
        def _(dve):
            with dve.Fori(0, TT // G) as i:
                for j in range(G):
                    x = resid[:, ds(i * G + j, 1), :].rearrange("p t d -> p (t d)")
                    st = stats[:, ds(i * G + j, 1), :].rearrange("p t d -> p (t d)")
                    nc.vector.bn_stats(st, x).then_inc(s_stats, 1)
            dve.wait_ge(s_stats, TT)
            c = Steps()
            nc.vector.tensor_tensor(mean[:, :], stats[:, :, 1], stats[:, :, 4], ALU.add).then_inc(s_var, 1)
            dve.wait_ge(s_var, c.up())
            nc.vector.tensor_scalar(mean[:, :], mean[:, :], 0.5, None, ALU.mult).then_inc(s_var, 1)
            dve.wait_ge(s_var, c.up())
            nc.vector.tensor_tensor(tmp[:, :], stats[:, :, 1], mean[:, :], ALU.subtract).then_inc(s_var, 1)
            dve.wait_ge(s_var, c.up())
            nc.vector.tensor_tensor(tmp[:, :], tmp[:, :], tmp[:, :], ALU.mult).then_inc(s_var, 1)
            dve.wait_ge(s_var, c.up())
            nc.vector.tensor_tensor(var[:, :], stats[:, :, 2], stats[:, :, 5], ALU.add).then_inc(s_var, 1)
            dve.wait_ge(s_var, c.up())
            nc.vector.tensor_scalar(var[:, :], var[:, :], 1.0 / P, LN_EPS, ALU.mult, ALU.add).then_inc(s_var, 1)
            dve.wait_ge(s_var, c.up())
            nc.vector.tensor_tensor(var[:, :], var[:, :], tmp[:, :], ALU.add).then_inc(s_var, 1)
            dve.wait_ge(s_var, c.up())
            dve.wait_ge(s_std, 1)
            nc.vector.reciprocal(rstd[:, :], tmp[:, :]).then_inc(s_var, 1)
            dve.wait_ge(s_var, c.up())
            with dve.Fori(0, TT // G // 2) as i:
                for k in range(2):
                    dve.wait_ge(s_turned, i * 2 + k - 1) if k else dve.wait_ge(s_turned, i * 2)
                    for j in range(G):
                        t = i * 2 * G + k * G + j
                        x = resid[:, ds(t, 1), :].rearrange("p t d -> p (t d)")
                        nc.vector.tensor_scalar(xn[k][:, j, :], x, mean[:, ds(t, 1)], rstd[:, ds(t, 1)],
                                                ALU.subtract, ALU.mult).then_inc(s_xn, 1)

        @block.tensor
        def _(pe):
            with pe.Fori(0, TT // G // 2) as i:
                for k in range(2):
                    pe.wait_ge(s_xn, i * 2 * G + (k + 1) * G)
                    pe.wait_ge(s_out, i * 2) if k == 0 else pe.wait_ge(s_out, i * 2)
                    for j in range(G):
                        mm = nc.tensor.transpose(turned[k][:, j * P:(j + 1) * P], xn[k][:, j, :], ident[:, :])
                    mm.then_inc(s_turned, 1)

        @block.scalar
        def _(act):
            act.wait_ge(s_var, 7)
            nc.scalar.activation(tmp[:, :], var[:, :], ACT.Sqrt).then_inc(s_std, 1)
            with act.Fori(0, TT // G // 2) as i:
                for k in range(2):
                    act.wait_ge(s_turned, i * 2 + k + 1)
                    nc.scalar.activation(xnT[:, ds((i * 2 + k) * BANK, BANK)], turned[k][:, :],
                                         ACT.Copy).then_inc(s_out, 1)


def cross_attention_0(nc, resid, xnT, ident, ctx_in, mask_in, Wq, bq, Wk, bk, Wv, bv, Wo, bo, B, SQ):
    SK = ctx_in.shape[1]
    H, D, DK = Wq.shape
    G, HG, CP = 4, 4, 4
    KT = tiles(SK)
    NT = len(KT)
    CH = tiles(SK, BANK)
    U = G * NT
    QT = SQ // P
    ROW = HG * CP * DK
    assert ROW == P and H == G * HG and H * DK == P

    at = {u: [] for u in range(U)}
    at[1].append(("mask", 1))
    at[2].append(("v", 1))
    at[5].append(("mask", 2))
    at[6].append(("v", 2))
    at[9].append(("mask", 3))
    at[10].append(("v", 3))
    for n, u in enumerate((3, 4, 7, 8, 11)):
        at[u].append(("k", 3, n - 1) if n else ("q", 3))
    for c in range(4):
        at[NT + c].append(("ctxT", c))
    for g in range(3):
        at[NT * (g + 1) + 4].append(("q", g))
        for c in range(4):
            at[NT * (g + 1) + 5 + c].append(("k", g, c))
    at[U - 4].append(("mask", 0))
    at[U - 3].append(("v", 0))
    per = [(j, "dve") for u in range(U) for j in at[u]] + [(("y",), "dve")]
    first = [(("ctxT", c), "dve") for c in range(4)]
    for g in range(3):
        first += [(("q", g), "dve")] + [(("k", g, c), "dve") for c in range(4)]
    first += [(("mask", 0), "dve"), (("v", 0), "dve")]
    jobs = Jobs(first, per, 2)
    is_next = {j: u >= NT for u in range(U) for j in at[u]}

    with ExitStack() as ctx:
        def sb(name, shape, dt=F32):
            return ctx.enter_context(nc.sbuf_tensor("a0_" + name, shape, dt))

        def ps(name, shape, dt=F32):
            return ctx.enter_context(nc.psum_tensor("a0_" + name, shape, dt))

        def sem(name):
            return ctx.enter_context(nc.semaphore("a0_" + name))

        w_in = sb("w_in", [D, 3, H, DK])
        wq_rows = sb("wq_rows", [D, G, HG, CP, DK])
        wk_rows = sb("wk_rows", [D, G, HG, CP, DK])
        wo_in = sb("wo_in", [P, P])
        wo_wide = sb("wo_wide", [P, G, HG, 32])
        wo_T = sb("wo_T", [P, G, P])
        b_row = sb("b_row", [1, 2, P])
        HEAD = 2 * G + 2
        rows = sb("rows", [1, HEAD + HG, HG, CP, DK])
        cols = sb("cols", [P, HEAD + HG])
        lo_bias = sb("lo_bias", [P, 2 * G])
        bv_all = sb("bv_all", [P, P])
        bo_all = sb("bo_all", [P, P])
        ident16 = sb("ident16", [P, P], BF16)
        ctx_rows = sb("ctx_rows", [P, NT, D])
        ctxT = sb("ctxT", [D, SK])
        mask_i = sb("mask_i", [P, QT, SK], I32)
        fill = sb("fill", [P, QT, SK], BF16)
        fillT = sb("fillT", [P, NT, SQ], BF16)
        hi = [sb(f"hi{i}", [P, BANK], F16) for i in range(2)]
        q_mix = sb("q_mix", [P, SQ], F16)
        k_op = [sb(f"k_op{g}", [P, SK], F16) for g in range(G)]
        q_op = [sb(f"q_op{g}", [P, HG, SQ], F16) for g in range(G)]
        v = sb("v", [P, NT, P])
        SLOTS, SCORES, LAG, PV_LAG = 4, 5, 2, 3
        neg_max = [sb(f"neg_max{i}", [P, HG]) for i in range(SLOTS)]
        total = [sb(f"total{i}", [P, HG]) for i in range(SLOTS)]
        recip = [sb(f"recip{i}", [P, HG]) for i in range(SLOTS)]
        e = [sb(f"e{i}", [P, HG, SQ]) for i in range(SLOTS)]
        vn = [sb(f"vn{i}", [P, HG, 32]) for i in range(SLOTS)]
        attn = sb("attn", [P, G, SQ])
        yb = sb("yb", [P, QT, P])

        score = [ps(f"score{i}", [P, HG // 2, SQ]) for i in range(SCORES)]
        attn_acc = ps("attn_acc", [P, 2, SQ])
        bank = [ps(f"bank{i}", [P, BANK]) for i in range(2)]

        s_w = sem("weights_in")
        s_zero = sem("zeros_set")
        s_pool = sem("pool_steps_begun")
        s_id = sem("ident16_set")
        s_const = sem("const_steps")
        s_cpe = sem("const_products")
        s_rec0 = sem("const_parts")
        s_ctx = sem("ctx_in")
        s_mask = sem("mask_in")
        s_fill = sem("fill_ready")
        s_filled = sem("bank_filled")
        s_emptied = sem("bank_emptied")
        s_hi = sem("hi_part_ready")
        s_mix = sem("q_mix_ready")
        s_qop = sem("q_op_rows_written")
        s_score = sem("scores_ready")
        s_max = sem("neg_max_ready")
        s_exp = sem("exp_done")
        s_rec = sem("recip_ready")
        s_vn = sem("vn_ready")
        s_pv = sem("pv_done")
        s_att = sem("attn_copied")
        s_y = sem("resid_steps")
        block = ctx.enter_context(nc.Block())

        N1, NP = len(first), len(per)
        names = [[n for n, _ in x] for x in (first, per)]
        CTX_DMAS = 2 if SK % P else 1

        def after_job(job, it):
            return jobs.emptied("dve", names[1].index(job) + 1, it)

        def group_free(job, it):
            return it * (2 * U) + (2 * NT * (job[1] + 1) if job[1] < G - 1 else 0)

        @block.sync
        def _(sp):
            for i, w in enumerate((Wq, Wk, Wv)):
                sp.dma_start(w_in[:, i, :, :], w.rearrange("h d k -> d h k")).then_inc(s_w, 16)
            for i, b in enumerate((bk, bq)):
                sp.dma_start(b_row[:, i, :], b.rearrange("(o h) k -> o (h k)", o=1)).then_inc(s_w, 16)
            sp.dma_start(wo_in[:, :], Wo).then_inc(s_w, 16)
            sp.dma_start(bv_all[:, :], bv.rearrange("(o h) k -> o (h k)", o=1).to_broadcast([P, P])).then_inc(s_w, 16)
            sp.dma_start(bo_all[:, :], bo.rearrange("(o d) -> o d", o=1).to_broadcast([P, P])).then_inc(s_w, 16)

            def load_ctx(b):
                c = ctx_in[ds(b, 1), :, :]
                whole = SK // P
                sp.dma_start(ctx_rows[:, 0:whole, :],
                             c[:, 0:whole * P, :].rearrange("o (t p) d -> p (o t) d", p=P)).then_inc(s_ctx, 16)
                if SK % P:
                    sp.dma_start(ctx_rows[0:SK % P, whole, :],
                                 c[:, whole * P:SK, :].rearrange("o p d -> (o p) d")).then_inc(s_ctx, 16)

            def load_mask(b):
                m = mask_in[ds(b, 1), :, :]
                sp.dma_start(mask_i[:, :, :], m.rearrange("o (t p) s -> p (o t) s", p=P)).then_inc(s_mask, 16)

            load_ctx(0)
            load_mask(0)
            with sp.Fori(0, B) as it:
                sp.wait_ge(s_filled, it * NP + N1)
                load_ctx((it + 1) % B)
                sp.wait_ge(s_fill, (it + 1) * QT)
                load_mask((it + 1) % B)
            sp.wait_ge(s_ctx, 16 * CTX_DMAS * (B + 1))
            sp.wait_ge(s_mask, 16 * (B + 1))

        @block.gpsimd
        def _(pool):
            nc.gpsimd.memset(wo_wide[:, :, :, :], 0.0).then_inc(s_zero, 1)
            for x in vn:
                nc.gpsimd.memset(x[:, :, :], 0.0).then_inc(s_zero, 1)
            nc.gpsimd.tensor_scalar(ident16[:, :], ident[:, :], 1.0, 1.0, ALU.mult, ALU.mult).then_inc(s_id, 1)

            def make_fill(before):
                pool.wait_ge(s_mask, 16 * before + 16)
                pool.sem_inc(s_pool, 1)
                pool.wait_ge(s_zero, 1 + SLOTS)
                for q in range(QT):
                    nc.gpsimd.tensor_scalar(fill[:, q, :], mask_i[:, q, :], 0.0, MASK_FILL,
                                            ALU.is_equal, ALU.mult).then_inc(s_fill, 1)

            def place_q(g, before, it=None):
                pool.wait_ge(s_mix, before + 1)
                if it is not None:
                    pool.wait_ge(s_score, group_free(("q", g), it))
                    pool.sem_inc(s_pool, 1)
                for i in range(HG):
                    nc.gpsimd.tensor_scalar(q_op[g][:, i, :], q_mix[:, :], cols[:, HEAD + i:HEAD + i + 1], 1.0,
                                            ALU.mult, ALU.mult).then_inc(s_qop, 1)

            make_fill(0)
            pool.wait_ge(s_const, 4)
            for g in range(G - 1):
                place_q(g, g)
            with pool.Fori(0, B) as it:
                place_q(G - 1, it * G + (G - 1), it)
                pool.wait_ge(s_filled, jobs.filled(names[1].index(("mask", 3)), it))
                make_fill(it + 1)
                for g in range(G - 1):
                    place_q(g, it * G + (G + g), it)

        @block.tensor
        def _(pe):
            pe.wait_ge(s_const, 1)
            for j in range(HEAD + HG):
                mm = nc.tensor.matmul(bank[0][:, j:j + 1], rows[0:1, j, :, :, :].rearrange("o h c k -> o (h c k)"),
                                      ident[0:1, 0:1], start=True, stop=True)
            mm.then_inc(s_cpe, 1)
            pe.wait_ge(s_const, 3)
            for g in range(G):
                mm = nc.tensor.transpose(bank[0][:, g * P:(g + 1) * P],
                                         wo_wide[:, g, :, :].rearrange("p h k -> p (h k)"), ident[:, :])
            mm.then_inc(s_cpe, 1)
            pe.wait_ge(s_const, 4)
            pe.wait_ge(s_id, 1)

            def job(n, j, it=None):
                for _, count in jobs.free(n, it):
                    pe.wait_ge(s_emptied, count)
                bk_ = bank[n % 2]
                if j[0] == "ctxT":
                    if it is None:
                        pe.wait_ge(s_ctx, 16 * CTX_DMAS)
                    else:
                        pe.wait_ge(s_ctx, it * (16 * CTX_DMAS) + 32 * CTX_DMAS)
                    for t in range(4 * j[1], min(4 * j[1] + 4, NT)):
                        r = KT[t][1]
                        mm = nc.tensor.transpose(bk_[:, (t % 4) * P:(t % 4) * P + r], ctx_rows[0:r, t, :],
                                                 ident[0:r, 0:r])
                elif j[0] == "mask":
                    turned = bk_[:, :].bitcast(BF16)
                    if it is None or is_next[j]:
                        pe.wait_ge(s_fill, QT if it is None else it * QT + 2 * QT)
                    for t in range(4 * j[1], min(4 * j[1] + 4, NT)):
                        s0, r = KT[t]
                        for q in range(QT):
                            at_ = (t % 4) * SQ + q * P
                            mm = nc.tensor.transpose(turned[0:r, at_:at_ + P], fill[:, q, s0:s0 + r], ident16[:, :])
                elif j[0] == "q":
                    b = 0 if it is None else (it + 1) % B if is_next[j] else it
                    mm = nc.tensor.matmul(bk_[:, 0:SQ], wq_rows[:, j[1], :, :, :].rearrange("p h c k -> p (h c k)"),
                                          xnT[:, ds(b * SQ, SQ)], start=True, stop=True)
                elif j[0] == "k":
                    s0, r = CH[j[2]]
                    pe.wait_ge(s_emptied, jobs.emptied("dve", 4) if it is None else
                               after_job(("ctxT", 3), it) if is_next[j] else it * NP + N1)
                    mm = nc.tensor.matmul(bk_[:, 0:r], wk_rows[:, j[1], :, :, :].rearrange("p h c k -> p (h c k)"),
                                          ctxT[:, s0:s0 + r], start=True, stop=True)
                elif j[0] == "v":
                    pe.wait_ge(s_emptied, jobs.emptied("dve", 4) if it is None else
                               after_job(("ctxT", 3), it) if is_next[j] else it * NP + N1)
                    for t in range(4 * j[1], min(4 * j[1] + 4, NT)):
                        s0, r = KT[t]
                        mm = nc.tensor.matmul(bk_[0:r, (t % 4) * P:(t % 4 + 1) * P], ctxT[:, s0:s0 + r],
                                              w_in[:, 2, :, :].rearrange("p h k -> p (h k)"), start=True, stop=True)
                elif j[0] == "y":
                    pe.wait_ge(s_att, it * G + G)
                    for q in range(QT):
                        for g in range(G):
                            mm = nc.tensor.matmul(bk_[:, q * P:(q + 1) * P], attn[:, g, q * P:(q + 1) * P],
                                                  wo_T[:, g, :], start=(q == 0 and g == 0), stop=(g == G - 1),
                                                  skip_group_check=True)
                mm.then_inc(s_filled, 1)

            def scores(u, it):
                g, t = divmod(u, NT)
                s0, r = KT[t]
                if t == 0:
                    pe.wait_ge(s_qop, it * (HG * G) + HG * (g + 1))
                if u == 0:
                    pe.wait_ge(s_emptied, it * NP + N1)
                elif g == 0 and t % 4 == 0:
                    pe.wait_ge(s_emptied, after_job(("mask", t // 4), it))
                elif u == NT * (G - 1):
                    pe.wait_ge(s_emptied, after_job(("k", G - 1, 3), it))
                for half in range(2):
                    w = 2 * u + half
                    pe.wait_ge(s_exp, it * (2 * U) + max(w - SCORES + 1, 0))
                    o = score[w % SCORES][0:r, :, :]
                    nc.tensor.matmul(o, k_op[g][:, s0:s0 + r], q_op[g][:, 2 * half:2 * half + 2, :],
                                     start=True, stop=False)
                    mm = nc.tensor.matmul(o, ident16[0:r, 0:r],
                                          fillT[0:r, t, :].unsqueeze(1).to_broadcast([r, 2, SQ]),
                                          start=False, stop=True)
                    mm.then_inc(s_score, 1)

            def pv(u, it):
                g, t = divmod(u, NT)
                r = KT[t][1]
                pe.wait_ge(s_vn, it * U + u + 1)
                if t == 0:
                    pe.wait_ge(s_att, it * G + g)
                for i in range(HG):
                    mm = nc.tensor.matmul(attn_acc[32 * i:32 * i + 32, g % 2, :], vn[u % SLOTS][0:r, i, :],
                                          e[u % SLOTS][0:r, i, :], start=(t == 0),
                                          stop=(t == NT - 1))
                mm.then_inc(s_pv, 1)

            for n, (j, _) in enumerate(first):
                job(n, j)
            with pe.Fori(0, B) as it:
                n = 0
                for u in range(U):
                    scores(u, it)
                    for j in at[u]:
                        job(n, j, it)
                        n += 1
                    if u >= PV_LAG:
                        pv(u - PV_LAG, it)
                for u in range(U - PV_LAG, U):
                    pv(u, it)
                job(n, ("y",), it)

        @block.scalar
        def _(act):
            def hi_part(n, j, k, it=None):
                N = SQ if j[0] == "q" else CH[j[2]][1]
                act.wait_ge(s_filled, jobs.filled(n, it))
                if k >= 2:
                    act.wait_ge(s_emptied, jobs.emptied("dve", hi_at[it is not None][k - 2] + 1, it))
                elif it is not None:
                    act.wait_ge(s_emptied, it * NP + N1)
                c = j[1] + (G if j[0] == "q" else 0)
                m = 2 * G + (1 if j[0] == "q" else 0)
                nc.scalar.activation(hi[k % 2][:, 0:N], bank[n % 2][:, 0:N], ACT.Identity,
                                     bias=lo_bias[:, c:c + 1], scale=cols[:, m:m + 1]).then_inc(s_hi, 1)

            hi_at = [[n for n, j in enumerate(x) if j[0] in "qk"] for x in names]
            act.wait_ge(s_const, 4)
            for k, n in enumerate(hi_at[0]):
                hi_part(n, names[0][n], k)
            with act.Fori(0, B) as it:
                n = 0
                for u in range(U):
                    for j in at[u - 1] if u else []:
                        if n in hi_at[1]:
                            hi_part(n, j, hi_at[1].index(n), it)
                        n += 1
                    r = KT[u % NT][1]
                    act.wait_ge(s_pv, it * U + max(u - SLOTS + 1, 0))
                    for i in range(HG):
                        w = 2 * u + i // 2
                        if i % 2 == 0:
                            act.wait_ge(s_max, it * (2 * U) + w + 1)
                        ex = nc.scalar.activation(e[u % SLOTS][0:r, i, :], score[w % SCORES][0:r, i % 2, :], ACT.Exp,
                                                  bias=neg_max[u % SLOTS][0:r, i:i + 1],
                                                  accum_out=total[u % SLOTS][0:r, i:i + 1])
                        if i % 2 == 1:
                            ex.then_inc(s_exp, 1)

        @block.vector
        def _(dve):
            dve.wait_ge(s_w, 8 * 16)
            nc.vector.memset(rows[:, 2 * G:, :, :, :], 0.0).then_inc(s_rec0, 1)
            dve.wait_ge(s_rec0, 1)
            nc.vector.memset(rows[:, 2 * G, :, 2:4, :], 1.0)
            for i in range(HG):
                nc.vector.memset(rows[:, HEAD + i, i, :, :], 1.0)
            for c in (1, 3):
                nc.vector.memset(rows[:, 2 * G + 1, :, c, :], 1.0)
            for i, scale in ((0, 1.0), (1, 0.125)):
                for g in range(G):
                    src = b_row[0:1, i, g * HG * DK:(g + 1) * HG * DK].rearrange("o (h k) -> o h k", h=HG)
                    last = nc.vector.tensor_scalar(rows[:, i * G + g, :, :, :],
                                                   src.unsqueeze(2).to_broadcast([1, HG, CP, DK]),
                                                   scale, None, ALU.mult)
            last.then_inc(s_const, 1)
            dve.wait_ge(s_zero, 1 + SLOTS)
            for g in range(G):
                last = nc.vector.tensor_copy(wo_wide[:, g, :, 0:DK],
                                             wo_in[:, g * HG * DK:(g + 1) * HG * DK].rearrange("p (h k) -> p h k", h=HG))
            last.then_inc(s_const, 1)
            for i, (dst, scale) in enumerate(((wq_rows, 0.125), (wk_rows, 1.0))):
                for g in range(G):
                    nc.vector.tensor_scalar(dst[:, g, :, :, :],
                                            w_in[:, i, g * HG:(g + 1) * HG, :].unsqueeze(2).to_broadcast([D, HG, CP, DK]),
                                            scale, None, ALU.mult)
            dve.wait_ge(s_cpe, 1)
            nc.vector.tensor_copy(cols[:, :], bank[0][:, 0:HEAD + HG]).then_inc(s_rec0, 1)
            dve.wait_ge(s_rec0, 2)
            for i in range(2):
                last = nc.vector.tensor_scalar(lo_bias[:, i * G:(i + 1) * G], cols[:, i * G:(i + 1) * G],
                                               cols[:, 2 * G + i:2 * G + i + 1], None, ALU.mult)
            last.then_inc(s_const, 1)
            dve.wait_ge(s_cpe, 2)
            nc.vector.tensor_copy(wo_T[:, :, :], bank[0][:, :].rearrange("p (g d) -> p g d", g=G)).then_inc(s_const, 1)

            def empty(n, j, it=None):
                bk_ = bank[n % 2]
                dve.wait_ge(s_filled, jobs.filled(n, it))
                if j[0] == "ctxT":
                    s0, r = CH[j[1]]
                    if it is not None and j[1] == 0:
                        dve.wait_ge(s_filled, it * NP + N1 + n)
                    ins = nc.vector.tensor_copy(ctxT[:, s0:s0 + r], bk_[:, 0:r])
                elif j[0] == "mask":
                    turned = bk_[:, :].bitcast(BF16)
                    if it is not None:
                        dve.wait_ge(s_score, it * (2 * U) + (2 * (NT * (G - 1) + 4) if is_next[j] else 0))
                    lo, hi_ = 4 * j[1], min(4 * j[1] + 4, NT)
                    r = KT[hi_ - 1][1]
                    ins = nc.vector.tensor_copy(fillT[0:r, lo:hi_, :],
                                                turned[0:r, 0:(hi_ - lo) * SQ].rearrange("p (t q) -> p t q", q=SQ))
                elif j[0] == "v":
                    lo, hi_ = 4 * j[1], min(4 * j[1] + 4, NT)
                    r = KT[hi_ - 1][1]
                    ins = nc.vector.tensor_tensor(v[0:r, lo:hi_, :], bk_[0:r, 0:(hi_ - lo) * P].rearrange("p (t d) -> p t d", d=P),
                                                  bv_all[0:r, :].unsqueeze(1).to_broadcast([r, hi_ - lo, P]), ALU.add)
                elif j[0] in "qk":
                    k = hi_at[it is not None].index(n)
                    before = len(hi_at[0]) if it is not None else 0
                    dve.wait_ge(s_hi, k + 1 if it is None else it * len(hi_at[1]) + (before + k + 1))
                    q_jobs = sum(x[0] == "q" for x in names[it is not None][:n])
                    if j[0] == "q":
                        N, c, dst = SQ, G + j[1], q_mix[:, :]
                        dve.wait_ge(s_qop, HG * q_jobs if it is None else it * (HG * G) + HG * (G - 1 + q_jobs))
                    else:
                        s0, N = CH[j[2]]
                        c, dst = j[1], k_op[j[1]][:, s0:s0 + N]
                        if it is not None and j[2] == 0:
                            dve.wait_ge(s_score, group_free(j, it))
                    ins = nc.vector.scalar_tensor_tensor(out=dst, in0=bk_[:, 0:N], scalar=cols[:, c:c + 1],
                                                         in1=hi[k % 2][:, 0:N], op0=ALU.add, op1=ALU.subtract)
                ins.then_inc(s_emptied, 1)
                if j[0] == "q":
                    dve.wait_ge(s_emptied, jobs.emptied("dve", n + 1, it))
                    dve.sem_inc(s_mix, 1)

            def maximum(u, it):
                r = KT[u % NT][1]
                for w in (2 * u, 2 * u + 1):
                    dve.wait_ge(s_score, it * (2 * U) + w + 1)
                    nc.vector.tensor_reduce(neg_max[u % SLOTS][0:r, w % 2 * 2:w % 2 * 2 + 2],
                                            score[w % SCORES][0:r, :, :], AX.X, ALU.max,
                                            negate=True).then_inc(s_max, 1)

            def scaled_v(u, it):
                g, t = divmod(u, NT)
                r, slot = KT[t][1], u % SLOTS
                dve.wait_ge(s_exp, it * (2 * U) + 2 * u + 2)
                nc.vector.reciprocal(recip[slot][0:r, :], total[slot][0:r, :]).then_inc(s_rec, 1)
                dve.wait_ge(s_rec, it * U + u + 1)
                if u == 0:
                    dve.wait_ge(s_emptied, it * NP + N1)
                elif g == 0 and t % 4 == 0:
                    dve.wait_ge(s_emptied, after_job(("v", t // 4), it))
                dve.wait_ge(s_pv, it * U + max(u - SLOTS + 1, 0))
                w = HG * DK
                nc.vector.tensor_tensor(vn[slot][0:r, :, 0:DK],
                                        v[0:r, t, g * w:(g + 1) * w].rearrange("p (h k) -> p h k", h=HG),
                                        recip[slot][0:r, :].unsqueeze(2).to_broadcast([r, HG, DK]),
                                        ALU.mult).then_inc(s_vn, 1)

            def copy_attn(g, it):
                dve.wait_ge(s_pv, it * U + (g + 1) * NT)
                dve.wait_ge(s_filled, it * NP + N1)
                nc.vector.tensor_copy(attn[:, g, :], attn_acc[:, g % 2, :]).then_inc(s_att, 1)

            hi_at = [[n for n, j in enumerate(x) if j[0] in "qk"] for x in names]
            for n, (j, _) in enumerate(first):
                empty(n, j)
            with dve.Fori(0, B) as it:
                n = 0
                for u in range(U):
                    if u > NT and u % NT == PV_LAG:
                        copy_attn(u // NT - 1, it)
                    maximum(u, it)
                    for j in at[u - 1] if u else []:
                        empty(n, j, it)
                        n += 1
                    if u >= LAG:
                        scaled_v(u - LAG, it)
                for u in range(U - LAG, U):
                    scaled_v(u, it)
                copy_attn(G - 1, it)
                dve.wait_ge(s_filled, jobs.filled(n, it))
                nc.vector.tensor_tensor(yb[:, :, :], bank[n % 2][:, 0:QT * P].rearrange("p (q d) -> p q d", q=QT),
                                        bo_all[:, :].unsqueeze(1).to_broadcast([P, QT, P]), ALU.add).then_inc(s_emptied, 1)
                dve.wait_ge(s_emptied, jobs.emptied("dve", n + 1, it))
                x = resid[:, ds(it * QT, QT), :]
                nc.vector.tensor_tensor(x, x, yb[:, :, :], ALU.add).then_inc(s_y, 1)


def moe_ffn_0(nc, resid, xnT, ident, gate_w, gate_b, dp_w1, dp_b1, dp_w2, dp_b2, ew1, eb1, ew2, eb2, TT):
    D, E = gate_w.shape
    DH = dp_w1.shape[1]
    HE = ew1.shape[2]
    HC = HE // P
    TG = BANK // P
    PASSES = TT // TG
    LROW = 96
    assert HC == 2 and E == 4
    Z_STEPS = 2
    L_STEPS = Z_STEPS + 1 + E + E - 1 + E
    with ExitStack() as ctx:
        def sb(name, shape, dt=F32):
            return ctx.enter_context(nc.sbuf_tensor("f0_" + name, shape, dt))

        def sem(name):
            return ctx.enter_context(nc.semaphore("f0_" + name))

        w_dp1 = sb("w_dp1", [D, P])
        w_dp2 = sb("w_dp2", [P, P])
        b_dp1 = sb("b_dp1", [P, 1])
        b_dp2 = sb("b_dp2", [P, 1])
        b_gate = sb("b_gate", [P, E])
        w_e1 = sb("w_e1", [D, E, HE])
        w_e2 = sb("w_e2", [P, E, HC, D])
        b_e1 = sb("b_e1", [P, E * HC])
        b_e2 = sb("b_e2", [P, E, D])
        dp_h = sb("dp_h", [P, BANK])
        lz_rows = sb("lz_rows", [P, BANK])
        logit = sb("logit", [P, TT, E + 1])
        lg = [sb(f"lg{i}", [P, TT]) for i in range(E)]
        weight = sb("weight", [P, E, TT])
        pos = [sb(f"pos{i}", [P, TT]) for i in range(E)]
        top = sb("top", [P, TT])
        z = sb("z", [P, TT])
        ez = sb("ez", [P, TT])
        k_tok = sb("k_tok", [P, TT])
        t0 = sb("t0", [P, TT])
        t1 = sb("t1", [P, TT])
        hid = [sb(f"hid{i}", [P, BANK]) for i in range(E * HC)]
        y_b = [sb(f"y_b{i}", [P, E, D]) for i in range(TG)]
        hbank = [ctx.enter_context(nc.psum_tensor(f"f0_hbank{i}", [P, BANK], F32)) for i in range(4)]
        ybank = [ctx.enter_context(nc.psum_tensor(f"f0_ybank{i}", [P, E, D], F32)) for i in range(TG)]
        s_w = sem("weights_in")
        s_zero = sem("lz_rows_zeroed")
        s_dp = sem("difficulty_hidden")
        s_dph = sem("dp_h_ready")
        s_lz = sem("logits_and_z")
        s_lzr = sem("lz_rows_ready")
        s_turn = sem("logits_turned")
        s_log = sem("logit_written")
        s_g = sem("gate_steps")
        s_ea = sem("exp_abs_z")
        s_ln = sem("softplus_log")
        s_el = sem("exp_logits")
        s_h = sem("hidden_filled")
        s_ha = sem("hidden_relu_act")
        s_hv = sem("hidden_relu_dve")
        s_y = sem("y_filled")
        s_yb = sem("y_biased")
        s_r = sem("resid_steps")
        block = ctx.enter_context(nc.Block())

        @block.sync
        def _(sp):
            sp.wait_ge(s_zero, 4)
            with nc.allow_non_contiguous_dma(reason="narrow weights"):
                sp.dma_start(w_dp1[:, LROW:LROW + E], gate_w).then_inc(s_w, 16)
                sp.dma_start(w_dp1[:, 0:DH], dp_w1).then_inc(s_w, 16)
                sp.dma_start(w_dp2[0:DH, LROW + E:LROW + E + 1], dp_w2).then_inc(s_w, 16)
                sp.dma_start(b_dp1[0:DH, :], dp_b1.rearrange("(p o) -> p o", o=1)).then_inc(s_w, 16)
            sp.dma_start(b_dp2[:, :], dp_b2.rearrange("(o p) -> o p", o=1).to_broadcast([P, 1])).then_inc(s_w, 16)
            sp.dma_start(b_gate[:, :], gate_b.rearrange("(o e) -> o e", o=1).to_broadcast([P, E])).then_inc(s_w, 16)
            sp.dma_start(w_e1[:, :, :], ew1.rearrange("e d h -> d e h")).then_inc(s_w, 16)
            sp.dma_start(w_e2[:, :, :, :], ew2.rearrange("e (c p) d -> p e c d", p=P)).then_inc(s_w, 16)
            for e in range(E):
                with nc.allow_non_contiguous_dma(reason="a bias to a partition"):
                    sp.dma_start(b_e1[:, e * HC:(e + 1) * HC],
                                 eb1[e, :].rearrange("(c p) -> p c", p=P)).then_inc(s_w, 16)
            sp.dma_start(b_e2[:, :, :], eb2.rearrange("(o e) d -> o e d", o=1).to_broadcast([P, E, D])).then_inc(s_w, 16)
            sp.wait_ge(s_w, 16 * (9 + E))

        @block.tensor
        def _(pe):
            pe.wait_ge(s_w, 16 * (9 + E))
            with pe.Fori(0, PASSES) as it:
                x = xnT[:, ds(it * BANK, BANK)]
                pe.wait_ge(s_lzr, 2 * it)
                nc.tensor.matmul(hbank[0][:, :], w_dp1[:, :], x, start=True, stop=True).then_inc(s_dp, 1)
                pe.wait_ge(s_dph, it + 1)
                nc.tensor.matmul(hbank[1][:, :], w_dp2[:, :], dp_h[:, :], start=True, stop=True).then_inc(s_lz, 1)
                pe.wait_ge(s_lzr, 2 * it + 2)
                pe.wait_ge(s_log, it)
                for j in range(TG):
                    mm = nc.tensor.transpose(hbank[2][:, j * P:(j + 1) * P], lz_rows[:, j * P:(j + 1) * P],
                                             ident[:, :])
                mm.then_inc(s_turn, 1)
            pe.wait_ge(s_log, PASSES)
            with pe.Fori(0, PASSES) as it:
                x = xnT[:, ds(it * BANK, BANK)]
                for n in range(E * HC):
                    e, c = divmod(n, HC)
                    pe.wait_ge(s_hv if n % 2 else s_ha, it * (E * HC // 2) + max(n // 2 - 1, 0))
                    nc.tensor.matmul(hbank[n % 4][:, :], w_e1[:, e, c * P:(c + 1) * P], x,
                                     start=True, stop=True).then_inc(s_h, 1)
                for j in range(TG):
                    pe.wait_ge(s_yb, it * TG + j)
                    for n in range(E * HC):
                        if j == 0:
                            pe.wait_ge(s_hv if n % 2 else s_ha, it * (E * HC // 2) + (n // 2 + 1))
                        e, c = divmod(n, HC)
                        mm = nc.tensor.matmul(ybank[j][:, e, :], hid[n][:, j * P:(j + 1) * P], w_e2[:, e, c, :],
                                              start=(n == 0), stop=(c == HC - 1), skip_group_check=True)
                    mm.then_inc(s_y, 1)

        @block.scalar
        def _(act):
            with act.Fori(0, PASSES) as it:
                act.wait_ge(s_dp, it + 1)
                act.wait_ge(s_lz, it)
                nc.scalar.activation(dp_h[:, :], hbank[0][:, :], ACT.Relu, bias=b_dp1[:, 0:1]).then_inc(s_dph, 1)
            act.wait_ge(s_g, Z_STEPS)
            nc.scalar.activation(ez[:, :], t0[:, :], ACT.Exp, scale=-1.0).then_inc(s_ea, 1)
            act.wait_ge(s_g, Z_STEPS + 1)
            nc.scalar.activation(t0[:, :], ez[:, :], ACT.Ln).then_inc(s_ln, 1)
            act.wait_ge(s_g, L_STEPS)
            nc.scalar.activation(weight[:, :, :], weight[:, :, :], ACT.Exp).then_inc(s_el, 1)
            with act.Fori(0, PASSES) as it:
                for n in range(0, E * HC, 2):
                    act.wait_ge(s_h, it * (E * HC) + n + 1)
                    act.wait_ge(s_y, it * TG)
                    nc.scalar.activation(hid[n][:, :], hbank[n % 4][:, :], ACT.Relu,
                                         bias=b_e1[:, n:n + 1]).then_inc(s_ha, 1)

        @block.vector
        def _(dve):
            for x in (lz_rows, w_dp1, w_dp2, b_dp1):
                nc.vector.memset(x[:, :], 0.0).then_inc(s_zero, 1)
            dve.wait_ge(s_zero, 4)
            dve.wait_ge(s_w, 16 * (9 + E))
            with dve.Fori(0, PASSES) as it:
                rows = slice(LROW, P)
                dve.wait_ge(s_turn, it)
                dve.wait_ge(s_dph, it + 1)
                nc.vector.tensor_copy(lz_rows[rows, :], hbank[0][rows, :]).then_inc(s_lzr, 1)
                dve.wait_ge(s_lzr, 2 * it + 1)
                dve.wait_ge(s_lz, it + 1)
                nc.vector.tensor_tensor(lz_rows[rows, :], hbank[1][rows, :], lz_rows[rows, :], ALU.add).then_inc(s_lzr, 1)
                dve.wait_ge(s_turn, it + 1)
                nc.vector.tensor_copy(logit[:, ds(it * TG, TG), :],
                                      hbank[2][:, :].rearrange("p (t r) -> p t r", t=TG)[:, :, LROW:LROW + E + 1]).then_inc(s_log, 1)
            dve.wait_ge(s_log, PASSES)
            c = Steps()
            tt, ts = nc.vector.tensor_tensor, nc.vector.tensor_scalar
            ts(z[:, :], logit[:, :, E], b_dp2[:, 0:1], None, ALU.add).then_inc(s_g, 1)
            dve.wait_ge(s_g, c.up())
            nc.vector.scalar_tensor_tensor(out=t0[:, :], in0=z[:, :], scalar=-1.0, in1=z[:, :],
                                           op0=ALU.mult, op1=ALU.max).then_inc(s_g, 1)
            dve.wait_ge(s_g, c.up())
            assert c.n == Z_STEPS
            dve.wait_ge(s_ea, 1)
            ts(ez[:, :], ez[:, :], 1.0, None, ALU.add).then_inc(s_g, 1)
            dve.wait_ge(s_g, c.up())
            for i in range(E):
                ts(lg[i][:, :], logit[:, :, i], b_gate[:, i:i + 1], None, ALU.add).then_inc(s_g, 1)
                dve.wait_ge(s_g, c.up())
            tt(top[:, :], lg[0][:, :], lg[1][:, :], ALU.max).then_inc(s_g, 1)
            dve.wait_ge(s_g, c.up())
            for i in range(2, E):
                tt(top[:, :], top[:, :], lg[i][:, :], ALU.max).then_inc(s_g, 1)
                dve.wait_ge(s_g, c.up())
            for i in range(E):
                tt(weight[:, i, :], lg[i][:, :], top[:, :], ALU.subtract).then_inc(s_g, 1)
                c.up()
            dve.wait_ge(s_g, c.n)
            assert c.n == L_STEPS
            for i in range(E):
                nc.vector.memset(pos[i][:, :], float(E - 1 - i)).then_inc(s_g, 1)
                dve.wait_ge(s_g, c.up())
            for i in range(E):
                for j in range(i + 1, E):
                    tt(t1[:, :], lg[i][:, :], lg[j][:, :], ALU.is_ge).then_inc(s_g, 1)
                    dve.wait_ge(s_g, c.up())
                    tt(pos[j][:, :], pos[j][:, :], t1[:, :], ALU.add).then_inc(s_g, 1)
                    dve.wait_ge(s_g, c.up())
                    tt(pos[i][:, :], pos[i][:, :], t1[:, :], ALU.subtract).then_inc(s_g, 1)
                    dve.wait_ge(s_g, c.up())
            dve.wait_ge(s_ln, 1)
            nc.vector.scalar_tensor_tensor(out=z[:, :], in0=z[:, :], scalar=0.0, in1=t0[:, :],
                                           op0=ALU.max, op1=ALU.add).then_inc(s_g, 1)
            dve.wait_ge(s_g, c.up())
            ts(z[:, :], z[:, :], -0.5, 1.0 / 1.5, ALU.add, ALU.mult).then_inc(s_g, 1)
            dve.wait_ge(s_g, c.up())
            ts(z[:, :], z[:, :], 0.0, 1.0, ALU.max, ALU.min).then_inc(s_g, 1)
            dve.wait_ge(s_g, c.up())
            ts(z[:, :], z[:, :], float(E - 1), 1.0, ALU.mult, ALU.add).then_inc(s_g, 1)
            dve.wait_ge(s_g, c.up())
            ts(k_tok[:, :], z[:, :], 1.5, 1.0, ALU.is_ge, ALU.add).then_inc(s_g, 1)
            dve.wait_ge(s_g, c.up())
            for edge, compare in ((2.5, ALU.is_gt), (3.5, ALU.is_ge)):
                ts(t1[:, :], z[:, :], edge, None, compare).then_inc(s_g, 1)
                dve.wait_ge(s_g, c.up())
                tt(k_tok[:, :], k_tok[:, :], t1[:, :], ALU.add).then_inc(s_g, 1)
                dve.wait_ge(s_g, c.up())
            dve.wait_ge(s_el, 1)
            for i in range(E):
                tt(t1[:, :], pos[i][:, :], k_tok[:, :], ALU.is_lt).then_inc(s_g, 1)
                dve.wait_ge(s_g, c.up())
                tt(weight[:, i, :], weight[:, i, :], t1[:, :], ALU.mult).then_inc(s_g, 1)
                dve.wait_ge(s_g, c.up())
            nc.vector.tensor_reduce(t0[:, :], weight[:, :, :].rearrange("p e t -> p t e"), AX.X, ALU.add).then_inc(s_g, 1)
            dve.wait_ge(s_g, c.up())
            nc.vector.reciprocal(t1[:, :], t0[:, :]).then_inc(s_g, 1)
            dve.wait_ge(s_g, c.up())
            for i in range(E):
                tt(weight[:, i, :], weight[:, i, :], t1[:, :], ALU.mult).then_inc(s_g, 1)
                dve.wait_ge(s_g, c.up())
            with dve.Fori(0, PASSES) as it:
                for n in range(1, E * HC, 2):
                    dve.wait_ge(s_h, it * (E * HC) + n + 1)
                    dve.wait_ge(s_y, it * TG)
                    ts(hid[n][:, :], hbank[n % 4][:, :], b_e1[:, n:n + 1], 0.0, ALU.add, ALU.max).then_inc(s_hv, 1)
                for j in range(TG):
                    dve.wait_ge(s_y, it * TG + j + 1)
                    dve.wait_ge(s_r, it * (E * TG))
                    tt(y_b[j][:, :, :], ybank[j][:, :, :], b_e2[:, :, :], ALU.add).then_inc(s_yb, 1)
                dve.wait_ge(s_yb, it * TG + TG)
                for i in range(E):
                    dve.wait_ge(s_r, it * (E * TG) + i * TG)
                    for j in range(TG):
                        x = resid[:, ds(it * TG + j, 1), :].rearrange("p t d -> p (t d)")
                        w = weight[:, i, ds(it * TG + j, 1)]
                        nc.vector.scalar_tensor_tensor(out=x, in0=y_b[j][:, i, :], scalar=w, in1=x,
                                                       op0=ALU.mult, op1=ALU.add).then_inc(s_r, 1)


def cross_attention_1(nc, resid, xnT, ident, ctx_in, mask_in, Wq, Wkv, Wout, bout, B, SQ):
    SK, D = ctx_in.shape[1:]
    INNER = Wq.shape[1]
    DH = 64
    H = INNER // DH
    HP = H // 2
    KT = tiles(SK)
    NT = len(KT)
    CH = tiles(SK, BANK)
    NC = len(CH)
    QT = SQ // P
    TT = B * QT
    U = HP * 2 * QT
    PU = 2 * QT
    VH = INNER // BANK
    LAG = 2
    T_BY = ("act", "act", "act", "dve")

    at = {s: [] for s in range(U + LAG)}
    v_steps = [[s for s in (0, 1, 2)], [U // 2 + 2, U // 2 + 3, U // 2 + 4]]
    for half, steps in enumerate(v_steps):
        for t in range(NT):
            at[steps[t * len(steps) // NT]].append((("v", half, t), ("act", "dve")[t % 2]))
    at[U] += [(("ctxT", c), "dve") for c in range(NC)]
    at[U] += [(("q", p), "dve") for p in range(HP // 2)]
    at[U + 1] += [(("q", p), "dve") for p in range(HP // 2, HP)]
    per = []
    for s in range(U + LAG):
        per += at[s]
        if s >= LAG:
            per += [(("t", s - LAG, c), T_BY[c]) for c in range(NC)]
    per += [(("y",), "dve")]
    first = [(("ctxT", c), "dve") for c in range(NC)] + [(("q", p), "dve") for p in range(HP)]
    jobs = Jobs(first, per, 3)
    names = [[n for n, _ in x] for x in (first, per)]
    owner = dict(per)
    N1, NP = len(first), len(per)
    CTX_DMAS = 2 if SK % P else 1

    with ExitStack() as ctx:
        def sb(name, shape, dt=F32, stack=ctx):
            return stack.enter_context(nc.sbuf_tensor("a1_" + name, shape, dt))

        def ps(name, shape, dt=F32, stack=ctx):
            return stack.enter_context(nc.psum_tensor("a1_" + name, shape, dt))

        def sem(name, stack=ctx):
            return stack.enter_context(nc.semaphore("a1_" + name))

        A = sb("A", [D, H, D])
        wv = [sb(f"wv{i}", [D, INNER], F16) for i in range(2)]
        w_out = sb("w_out", [P, HP, D])
        b_out = sb("b_out", [P, D])
        mask_fill = sb("mask_fill", [P, TT])

        with ExitStack() as tmp:
            wq_in = sb("wq_in", [D, INNER], stack=tmp)
            wkv_in = sb("wkv_in", [D, 2 * INNER], stack=tmp)
            wq_T = sb("wq_T", [P, HP, D], stack=tmp)
            wk_T = sb("wk_T", [P, HP, D], stack=tmp)
            mask_i = sb("mask_i", [TT, P], I32, stack=tmp)
            mask_f = sb("mask_f", [TT, P], stack=tmp)
            sbank = [ps(f"sbank{i}", [P, BANK], stack=tmp) for i in range(8)]
            s_w = sem("weights_in", tmp)
            s_t = sem("weights_turned", tmp)
            s_c = sem("turned_copied", tmp)
            s_a = sem("A_filled", tmp)
            s_v = sem("wv_parts", tmp)
            s_m = sem("mask_steps", tmp)
            s_e = sem("A_copied", tmp)
            TB = BANK // P
            block = tmp.enter_context(nc.Block())

            @block.sync
            def _(sp):
                sp.dma_start(wq_in[:, :], Wq).then_inc(s_w, 16)
                sp.dma_start(mask_i[:, :], mask_in.rearrange("b (q p) -> (b q) p", p=P)).then_inc(s_w, 16)
                sp.dma_start(wkv_in[:, :], Wkv).then_inc(s_w, 16)
                sp.dma_start(w_out[:, :, :], Wout.rearrange("(h p) d -> p h d", p=P)).then_inc(s_w, 16)
                sp.dma_start(b_out[:, :], bout.rearrange("(o d) -> o d", o=1).to_broadcast([P, D])).then_inc(s_w, 16)

            @block.tensor
            def _(pe):
                pe.wait_ge(s_w, 5 * 16)
                for w, x in enumerate((wq_in, wkv_in)):
                    for p in range(HP):
                        mm = nc.tensor.transpose(sbank[2 * w + p // TB][:, p % TB * P:(p % TB + 1) * P],
                                                 x[:, p * P:(p + 1) * P], ident[:, :])
                        if p % TB == TB - 1:
                            mm.then_inc(s_t, 1)
                pe.wait_ge(s_c, 4)
                for i in range(2):
                    half = slice(DH * i, DH * i + DH)
                    for p in range(HP):
                        mm = nc.tensor.matmul(sbank[4 + i * HP // TB + p // TB][:, p % TB * P:(p % TB + 1) * P],
                                              wq_T[half, p, :], wk_T[half, p, :], start=True, stop=True)
                        if p % TB == TB - 1:
                            mm.then_inc(s_a, 1)
                pe.wait_ge(s_m, 2)
                nc.tensor.transpose(sbank[0][:, 0:TT], mask_f[:, :], ident[0:TT, 0:TT]).then_inc(s_t, 1)

            @block.scalar
            def _(act):
                for n in range(4):
                    act.wait_ge(s_t, n + 1)
                    dst = (wq_T, wk_T)[n // 2][:, n % 2 * TB:(n % 2 + 1) * TB, :]
                    nc.scalar.activation(dst, sbank[n][:, :].rearrange("p (h d) -> p h d", h=TB), ACT.Copy,
                                         scale=(-0.125, 1.0)[n // 2]).then_inc(s_c, 1)
                for n in range(H // TB):
                    act.wait_ge(s_a, n + 1)
                    i, k = divmod(n, HP // TB)
                    nc.scalar.activation(A[:, :, :].rearrange("p (h i) d -> p i h d", i=2)[:, i, k * TB:(k + 1) * TB, :],
                                         sbank[4 + n][:, :].rearrange("p (h d) -> p h d", h=TB), ACT.Copy).then_inc(s_e, 1)

            @block.vector
            def _(dve):
                dve.wait_ge(s_w, 5 * 16)
                nc.vector.tensor_scalar(mask_f[:, :], mask_i[:, :], -1.0, 1.0, ALU.mult, ALU.add).then_inc(s_m, 1)
                dve.wait_ge(s_m, 1)
                nc.vector.tensor_scalar(mask_f[:, :], mask_f[:, :], MASK_NEG, None, ALU.mult).then_inc(s_m, 1)
                nc.vector.tensor_copy(wv[0][:, :], wkv_in[:, INNER:]).then_inc(s_v, 1)
                dve.wait_ge(s_v, 1)
                nc.vector.tensor_tensor(wv[1][:, :], wkv_in[:, INNER:], wv[0][:, :], ALU.subtract).then_inc(s_v, 1)
                dve.wait_ge(s_t, 5)
                nc.vector.tensor_copy(mask_fill[:, :], sbank[0][:, 0:TT]).then_inc(s_v, 1)
        nc.all_engine_barrier()

        ctx_rows = sb("ctx_rows", [P, NT, D])
        ctxT = [sb(f"ctxT{i}", [D, SK], F16) for i in range(2)]
        qA = [sb(f"qA{i}", [D, H, SQ], F16) for i in range(2)]
        v = sb("v", [P, NT, BANK])
        SLOTS = 4
        e = [sb(f"e{i}", [P, SK]) for i in range(SLOTS)]
        least = [sb(f"least{i}", [P, 1]) for i in range(SLOTS)]
        total = [sb(f"total{i}", [P, 1]) for i in range(SLOTS)]
        recip = [sb(f"recip{i}", [P, 1]) for i in range(SLOTS)]
        eT = [sb(f"eT{i}", [P, NT, SQ]) for i in range(2)]
        outT = sb("outT", [P, HP, SQ])
        yb = sb("yb", [P, QT, D])
        score = ps("score", [P, NC * BANK])
        bank = [ps(f"bank{i}", [P, BANK]) for i in range(3)]
        out_acc = ps("out_acc", [P, BANK])

        s_ctx = sem("ctx_in")
        s_pool = sem("pool_steps_begun")
        s_filled = sem("bank_filled")
        s_emptied = {"act": sem("bank_emptied_act"), "dve": sem("bank_emptied_dve")}
        s_hi = sem("hi_part_ready")
        s_score = sem("scores_ready")
        s_sub = sem("scores_taken")
        s_exp = sem("exp_done")
        s_rec = sem("recip_ready")
        s_norm = sem("weights_normalised")
        s_pv = sem("pv_done")
        s_out = sem("outT_copied")
        s_y = sem("resid_steps")
        block = ctx.enter_context(nc.Block())

        def after_jobs(eng, last, it):
            n = names[1].index(last) + 1
            for who in ("act", "dve"):
                eng.wait_ge(s_emptied[who], jobs.emptied(who, n, it))

        def unit(u):
            p, r = divmod(u, PU)
            return p, r // 2, r % 2

        @block.sync
        def _(sp):
            def load(b):
                c = ctx_in[ds(b, 1), :, :]
                whole = SK // P
                sp.dma_start(ctx_rows[:, 0:whole, :],
                             c[:, 0:whole * P, :].rearrange("o (t p) d -> p (o t) d", p=P)).then_inc(s_ctx, 16)
                if SK % P:
                    sp.dma_start(ctx_rows[0:SK % P, whole, :],
                                 c[:, whole * P:SK, :].rearrange("o p d -> (o p) d")).then_inc(s_ctx, 16)

            load(0)
            with sp.Fori(0, B) as it:
                sp.wait_ge(s_filled, it * NP + N1)
                load((it + 1) % B)
            sp.wait_ge(s_ctx, 16 * CTX_DMAS * (B + 1))

        @block.tensor
        def _(pe):
            def job(n, j, it=None):
                for who, count in jobs.free(n, it):
                    pe.wait_ge(s_emptied[who], count)
                bk_ = bank[n % 3]
                if j[0] == "ctxT":
                    if it is None:
                        pe.wait_ge(s_ctx, 16 * CTX_DMAS)
                    else:
                        pe.wait_ge(s_ctx, it * (16 * CTX_DMAS) + 32 * CTX_DMAS)
                    for t in range(4 * j[1], min(4 * j[1] + 4, NT)):
                        r = KT[t][1]
                        mm = nc.tensor.transpose(bk_[:, (t % 4) * P:(t % 4) * P + r], ctx_rows[0:r, t, :],
                                                 ident[0:r, 0:r])
                elif j[0] == "q":
                    b = 0 if it is None else (it + 1) % B
                    for i in range(2):
                        mm = nc.tensor.matmul(bk_[:, i * SQ:(i + 1) * SQ], A[:, 2 * j[1] + i, :],
                                              xnT[:, ds(b * SQ, SQ)], start=True, stop=True)
                elif j[0] == "v":
                    s0, r = KT[j[2]]
                    w = slice(j[1] * BANK, (j[1] + 1) * BANK)
                    for i, (a_, b_) in enumerate(((0, 0), (0, 1), (1, 0))):
                        mm = nc.tensor.matmul(bk_[0:r, :], ctxT[a_][:, s0:s0 + r], wv[b_][:, w],
                                              start=(i == 0), stop=(i == 2))
                elif j[0] == "t":
                    u = j[1]
                    if j[2] == 0:
                        pe.wait_ge(s_norm, it * U + u + 1)
                    for t in range(4 * j[2], min(4 * j[2] + 4, NT)):
                        s0, r = KT[t]
                        mm = nc.tensor.transpose(bk_[0:r, (t % 4) * P:(t % 4 + 1) * P], e[u % SLOTS][:, s0:s0 + r],
                                                 ident[:, :])
                elif j[0] == "y":
                    pe.wait_ge(s_out, it * HP + HP)
                    for q in range(QT):
                        for p in range(HP):
                            mm = nc.tensor.matmul(bk_[:, q * P:(q + 1) * P], outT[:, p, q * P:(q + 1) * P],
                                                  w_out[:, p, :], start=(q == 0 and p == 0), stop=(p == HP - 1),
                                                  skip_group_check=True)
                mm.then_inc(s_filled, 1)

            def scores(u, it):
                p, q, i = unit(u)
                h = 2 * p + i
                pe.wait_ge(s_sub, it * U + u)
                if u == 0:
                    pe.wait_ge(s_emptied["dve"], jobs.emptied("dve", 0, it))
                qs = slice(q * P, (q + 1) * P)
                for s0, r in CH:
                    for n, (a_, b_) in enumerate(((0, 0), (0, 1), (1, 0))):
                        mm = nc.tensor.matmul(score[:, s0:s0 + r], qA[a_][:, h, qs], ctxT[b_][:, s0:s0 + r],
                                              start=(n == 0), stop=(n == 2))
                mm.then_inc(s_score, 1)

            def pv(p, it):
                pe.wait_ge(s_out, it * HP + p)
                after_jobs(pe, ("t", PU * p + PU - 1, NC - 1), it)
                for t, (_, r) in enumerate(KT):
                    for i in range(2):
                        w = (2 * p + i) % (BANK // DH) * DH
                        mm = nc.tensor.matmul(out_acc[DH * i:DH * i + DH, 0:SQ], v[0:r, t, w:w + DH],
                                              eT[i][0:r, t, :], start=(t == 0), stop=(t == NT - 1))
                mm.then_inc(s_pv, 1)

            for n, j in enumerate(names[0]):
                job(n, j)
            with pe.Fori(0, B) as it:
                n = 0
                for s in range(U + LAG):
                    if s < U:
                        scores(s, it)
                    for j, _ in at[s]:
                        job(n, j, it)
                        n += 1
                    if s >= LAG:
                        for c in range(NC):
                            job(n, ("t", s - LAG, c), it)
                            n += 1
                        if (s - LAG) % PU == PU - 1:
                            pv((s - LAG) // PU, it)
                job(n, ("y",), it)

        def eT_free(eng, u, it):
            eng.wait_ge(s_pv, it * HP + u // PU)

        def turned(n, j):
            _, q, i = unit(j[1])
            lo, hi_ = 4 * j[2], min(4 * j[2] + 4, NT)
            r = KT[hi_ - 1][1]
            return (eT[i][0:r, lo:hi_, q * P:(q + 1) * P],
                    bank[n % 3][0:r, 0:(hi_ - lo) * P].rearrange("p (t q) -> p t q", q=P))

        hi_jobs = [[n for n, j in enumerate(x) if j[0] in ("ctxT", "q")] for x in names]

        @block.scalar
        def _(act):
            def part(n, j, it=None):
                bk_ = bank[n % 3]
                if j[0] in ("ctxT", "q"):
                    act.wait_ge(s_filled, jobs.filled(n, it))
                    if it is not None:
                        act.wait_ge(s_score, it * U + U)
                    if j[0] == "ctxT":
                        s0, r = CH[j[1]]
                        nc.scalar.activation(ctxT[0][:, s0:s0 + r], bk_[:, 0:r], ACT.Copy).then_inc(s_hi, 1)
                    else:
                        nc.scalar.activation(qA[0][:, 2 * j[1]:2 * j[1] + 2, :],
                                             bk_[:, :].rearrange("p (h q) -> p h q", h=2), ACT.Copy).then_inc(s_hi, 1)
                elif j[0] == "v" and owner[j] == "act":
                    act.wait_ge(s_filled, jobs.filled(n, it))
                    r = KT[j[2]][1]
                    nc.scalar.activation(v[0:r, j[2], :], bk_[0:r, :], ACT.Copy).then_inc(s_emptied["act"], 1)
                elif j[0] == "t" and owner[j] == "act":
                    act.wait_ge(s_filled, jobs.filled(n, it))
                    eT_free(act, j[1], it)
                    dst, src = turned(n, j)
                    nc.scalar.activation(dst, src, ACT.Copy).then_inc(s_emptied["act"], 1)

            for n, j in enumerate(names[0]):
                part(n, j)
            with act.Fori(0, B) as it:
                n = 0
                for s in range(U + LAG):
                    for j in names[1][n:n + len(at[s]) + (NC if s >= LAG else 0)]:
                        part(n, j, it)
                        n += 1
                    if s < U:
                        act.wait_ge(s_sub, it * U + s + 1)
                        nc.scalar.activation(e[s % SLOTS][:, :], e[s % SLOTS][:, :], ACT.Exp, bias=least[s % SLOTS][:, 0:1],
                                             scale=-1.0, accum_out=total[s % SLOTS][:, 0:1]).then_inc(s_exp, 1)

        @block.gpsimd
        def _(pool):
            with pool.Fori(0, B) as it:
                for u in range(U):
                    pool.wait_ge(s_rec, it * U + u + 1)
                    pool.sem_inc(s_pool, 1)
                    x = e[u % SLOTS][:, :]
                    nc.gpsimd.tensor_scalar(x, x, recip[u % SLOTS][:, 0:1], 1.0, ALU.mult, ALU.mult).then_inc(s_norm, 1)

        @block.vector
        def _(dve):
            def part(n, j, it=None):
                bk_ = bank[n % 3]
                if j[0] in ("ctxT", "q"):
                    k = hi_jobs[it is not None].index(n)
                    dve.wait_ge(s_hi, k + 1 if it is None else it * len(hi_jobs[1]) + (len(hi_jobs[0]) + k + 1))
                    if j[0] == "ctxT":
                        s0, r = CH[j[1]]
                        dst, src, hi_ = ctxT[1][:, s0:s0 + r], bk_[:, 0:r], ctxT[0][:, s0:s0 + r]
                    else:
                        hs = slice(2 * j[1], 2 * j[1] + 2)
                        dst, src, hi_ = qA[1][:, hs, :], bk_[:, :].rearrange("p (h q) -> p h q", h=2), qA[0][:, hs, :]
                    nc.vector.tensor_tensor(dst, src, hi_, ALU.subtract).then_inc(s_emptied["dve"], 1)
                elif j[0] == "v" and owner[j] == "dve":
                    dve.wait_ge(s_filled, jobs.filled(n, it))
                    r = KT[j[2]][1]
                    nc.vector.tensor_copy(v[0:r, j[2], :], bk_[0:r, :]).then_inc(s_emptied["dve"], 1)
                elif j[0] == "t" and owner[j] == "dve":
                    dve.wait_ge(s_filled, jobs.filled(n, it))
                    eT_free(dve, j[1], it)
                    dst, src = turned(n, j)
                    nc.vector.tensor_copy(dst, src).then_inc(s_emptied["dve"], 1)

            def reciprocal(u, it):
                dve.wait_ge(s_exp, it * U + u + 1)
                nc.vector.reciprocal(recip[u % SLOTS][:, :], total[u % SLOTS][:, :]).then_inc(s_rec, 1)

            def take(u, it):
                _, q, _ = unit(u)
                dve.wait_ge(s_score, it * U + u + 1)
                done = jobs.filled(names[1].index(("t", u - SLOTS, NC - 1)), it) if u >= SLOTS else it * NP + N1
                dve.wait_ge(s_filled, done)
                nc.vector.tensor_scalar(e[u % SLOTS][:, :], score[:, 0:SK], mask_fill[:, ds(it * QT + q, 1)], None,
                                        ALU.add, ALU.min, accum_out=least[u % SLOTS][:, 0:1]).then_inc(s_sub, 1)

            for n, j in enumerate(names[0]):
                part(n, j)
            with dve.Fori(0, B) as it:
                n = 0
                for s in range(U + LAG):
                    if 0 < s <= U:
                        reciprocal(s - 1, it)
                    if s < U:
                        take(s, it)
                    for j in names[1][n:n + len(at[s]) + (NC if s >= LAG else 0)]:
                        part(n, j, it)
                        n += 1
                    if s >= LAG and (s - LAG) % PU == PU - 1:
                        p = (s - LAG) // PU
                        dve.wait_ge(s_pv, it * HP + p + 1)
                        dve.wait_ge(s_filled, it * NP + N1)
                        nc.vector.tensor_copy(outT[:, p, :], out_acc[:, 0:SQ]).then_inc(s_out, 1)
                dve.wait_ge(s_filled, jobs.filled(n, it))
                nc.vector.tensor_tensor(yb[:, :, :], bank[n % 3][:, 0:QT * D].rearrange("p (q d) -> p q d", q=QT),
                                        b_out[:, :].unsqueeze(1).to_broadcast([P, QT, D]), ALU.add).then_inc(s_emptied["dve"], 1)
                dve.wait_ge(s_emptied["dve"], jobs.emptied("dve", n + 1, it))
                x = resid[:, ds(it * QT, QT), :]
                nc.vector.tensor_tensor(x, x, yb[:, :, :], ALU.add).then_inc(s_y, 1)


def moe_ffn_1(nc, resid, xnT, ident, Wr, Wg, Wu, Wd, Sg, Su, Sd, TT):
    D, E = Wr.shape
    F = Wg.shape[2]
    NPAIR = E * F // P
    N = NPAIR + 1
    TG = BANK // P
    PASSES = TT // TG
    TOP = 2
    assert 2 * F == P and Sg.shape[1] == P and TG * 2 * E == P and TT * E <= BANK
    with ExitStack() as ctx:
        def sb(name, shape, dt=F32):
            return ctx.enter_context(nc.sbuf_tensor("f1_" + name, shape, dt))

        def ps(name):
            return ctx.enter_context(nc.psum_tensor("f1_" + name, [P, BANK], F32))

        def sem(name):
            return ctx.enter_context(nc.semaphore("f1_" + name))

        w_in = sb("w_in", [D, 2, N, P])
        w_gu = [sb(f"w_gu{i}", [D, 2, N, P], F16) for i in range(2)]
        wr_in = sb("wr_in", [D, E])
        w_r = [sb(f"w_r{i}", [D, E], F16) for i in range(2)]
        w_d = sb("w_d", [P, N, D])
        x16 = [sb(f"x16_{i}", [D, TT * P], F16) for i in range(2)]
        ident16 = sb("ident16", [P, P], F16)
        select = sb("select", [P, TG, E, F], F16)
        order = sb("order", [P, E])
        prob = sb("prob", [P, TT, E])
        left = sb("left", [P, TT, E])
        mark = sb("mark", [P, TT, E])
        pick = sb("pick", [P, TT, E])
        cw = sb("cw", [P, TT, E])
        best = sb("best", [P, TT])
        cw16 = sb("cw16", [P, TT, 2, E], F16)
        cwT = sb("cwT", [P, PASSES, P], F16)
        silu = [sb(f"silu{i}", [P, BANK]) for i in range(2)]
        hid = [sb(f"hid{i}", [P, BANK]) for i in range(2)]
        yT = sb("yT", [D, BANK])
        gbank = [ps(f"gbank{i}") for i in range(2)]
        ubank = [ps(f"ubank{i}") for i in range(2)]
        cbank = [ps(f"cbank{i}") for i in range(2)]
        ybank = ps("ybank")
        tbank = ps("tbank")
        s_w = sem("weights_in")
        s_split = sem("weight_parts")
        s_id = sem("constants_set")
        s_xh = sem("x_hi_ready")
        s_xl = sem("x_lo_ready")
        s_logit = sem("logits_filled")
        s_route = sem("routing_steps")
        s_exp = sem("exp_done")
        s_cwt = sem("cw_turned")
        s_cwc = sem("cwT_written")
        s_fill = sem("pair_filled")
        s_silu = sem("silu_ready")
        s_gate = sem("gated")
        s_hid = sem("hidden_ready")
        s_down = sem("down_added")
        s_yt = sem("yT_copied")
        s_turn = sem("y_turned")
        s_r = sem("resid_added")
        block = ctx.enter_context(nc.Block())
        LOADS = 7

        @block.sync
        def _(sp):
            sp.dma_start(wr_in[:, :], Wr).then_inc(s_w, 16)
            for i, (w, s) in enumerate(((Wg, Sg), (Wu, Su))):
                sp.dma_start(w_in[:, i, 0:NPAIR, :].rearrange("d n (i f) -> d (n i) f", f=F),
                             w.rearrange("e d f -> d e f")).then_inc(s_w, 16)
                sp.dma_start(w_in[:, i, NPAIR, :], s).then_inc(s_w, 16)
            sp.dma_start(w_d[:, 0:NPAIR, :], Wd.rearrange("(n i) f d -> (i f) n d", i=2)).then_inc(s_w, 16)
            sp.dma_start(w_d[:, NPAIR, :], Sd).then_inc(s_w, 16)
            sp.wait_ge(s_w, 16 * LOADS)

        @block.gpsimd
        def _(pool):
            for e in range(E):
                nc.gpsimd.memset(order[:, e:e + 1], float(E - e)).then_inc(s_id, 1)
            nc.gpsimd.tensor_scalar(ident16[:, :], ident[:, :], 1.0, 1.0, ALU.mult, ALU.mult).then_inc(s_id, 1)
            rows = ident[:, :].rearrange("p (j s e) -> p j s e", j=TG, s=2)
            for j in range(TG):
                hi_, lo = (rows[:, j, s, :].unsqueeze(2).to_broadcast([P, E, F]) for s in range(2))
                nc.gpsimd.tensor_tensor(select[:, j, :, :], hi_, lo, ALU.add).then_inc(s_id, 1)

        def fill_free(eng, n, it):
            eng.wait_ge(s_hid, it * N + max(n - 1, 0))

        @block.tensor
        def _(pe):
            pe.wait_ge(s_split, 2)
            with pe.Fori(0, PASSES) as it:
                pe.wait_ge(s_xl, it + 1)
                for j in range(TG):
                    t = it * TG + j
                    for i, (a_, b_) in enumerate(((0, 0), (0, 1), (1, 0))):
                        mm = nc.tensor.matmul(gbank[0][:, ds(t * E, E)], x16[a_][:, ds(t * P, P)], w_r[b_][:, :],
                                              start=(i == 0), stop=(i == 2))
                mm.then_inc(s_logit, 1)
            pe.wait_ge(s_id, E + 1 + TG)
            pe.wait_ge(s_split, 6)
            turned = cbank[0][:, :].bitcast(F16)
            for i in range(PASSES):
                mm = nc.tensor.transpose(turned[:, i * P:(i + 1) * P],
                                         cw16[:, i * TG:(i + 1) * TG, :, :].rearrange("p t s e -> p (t s e)"),
                                         ident16[:, :])
            mm.then_inc(s_cwt, 1)
            pe.wait_ge(s_w, 16 * LOADS)
            pe.wait_ge(s_cwc, 1)

            def down(n, it):
                pe.wait_ge(s_hid, it * N + n + 1)
                if n == 0:
                    pe.wait_ge(s_yt, it)
                nc.tensor.matmul(ybank[:, :], w_d[:, n, :], hid[n % 2][:, :], start=(n == 0),
                                 stop=(n == N - 1)).then_inc(s_down, 1)

            with pe.Fori(0, PASSES) as it:
                for n in range(N):
                    fill_free(pe, n, it)
                    for k, dst in enumerate((gbank[n % 2], ubank[n % 2])):
                        for i, (a_, b_) in enumerate(((0, 0), (0, 1), (1, 0))):
                            mm = nc.tensor.matmul(dst[:, :], w_gu[a_][:, k, n, :], x16[b_][:, ds(it * BANK, BANK)],
                                                  start=(i == 0), stop=(i == 2))
                    if n < NPAIR:
                        for j in range(TG):
                            mm = nc.tensor.matmul(cbank[n % 2][:, j * P:(j + 1) * P],
                                                  select[:, j, 2 * n:2 * n + 2, :].rearrange("p e f -> p (e f)"),
                                                  cwT[:, ds(it, 1), :].rearrange("p t d -> p (t d)"), start=True, stop=True)
                    mm.then_inc(s_fill, 1)
                    if n:
                        down(n - 1, it)
                down(N - 1, it)
                pe.wait_ge(s_yt, it + 1)
                pe.wait_ge(s_r, it)
                for j in range(TG):
                    mm = nc.tensor.transpose(tbank[:, j * P:(j + 1) * P], yT[:, j * P:(j + 1) * P], ident[:, :])
                mm.then_inc(s_turn, 1)

        @block.scalar
        def _(act):
            with act.Fori(0, PASSES) as it:
                w = ds(it * BANK, BANK)
                nc.scalar.activation(x16[0][:, w], xnT[:, w], ACT.Copy).then_inc(s_xh, 1)
            act.wait_ge(s_route, 2)
            nc.scalar.activation(prob[:, :, :], prob[:, :, :], ACT.Exp).then_inc(s_exp, 1)
            with act.Fori(0, PASSES) as it:
                for n in range(N):
                    act.wait_ge(s_fill, it * N + n + 1)
                    fill_free(act, n, it)
                    nc.scalar.activation(silu[n % 2][:, :], gbank[n % 2][:, :], ACT.Silu).then_inc(s_silu, 1)
                act.wait_ge(s_down, it * N + N)
                act.wait_ge(s_turn, it)
                nc.scalar.activation(yT[:, :], ybank[:, :], ACT.Copy).then_inc(s_yt, 1)

        @block.vector
        def _(dve):
            tt = nc.vector.tensor_tensor
            dve.wait_ge(s_w, 16 * LOADS)
            nc.vector.tensor_copy(w_r[0][:, :], wr_in[:, :]).then_inc(s_split, 1)
            dve.wait_ge(s_split, 1)
            tt(w_r[1][:, :], wr_in[:, :], w_r[0][:, :], ALU.subtract).then_inc(s_split, 1)
            with dve.Fori(0, PASSES) as it:
                w = ds(it * BANK, BANK)
                dve.wait_ge(s_xh, it + 1)
                tt(x16[1][:, w], xnT[:, w], x16[0][:, w], ALU.subtract).then_inc(s_xl, 1)
            nc.vector.tensor_copy(w_gu[0][:, :, :, :], w_in[:, :, :, :]).then_inc(s_split, 1)
            dve.wait_ge(s_split, 3)
            tt(w_gu[1][:, :, :, :], w_in[:, :, :, :], w_gu[0][:, :, :, :], ALU.subtract).then_inc(s_split, 1)

            def each(x):
                return x[:, :].unsqueeze(2).to_broadcast([P, TT, E])

            def reduce(dst, src, op):
                return nc.vector.tensor_reduce(dst[:, :], src[:, :, :], AX.X, op)

            c = Steps()
            dve.wait_ge(s_logit, PASSES)
            logits = gbank[0][:, 0:TT * E].rearrange("p (t e) -> p t e", e=E)
            nc.vector.tensor_reduce(best[:, :], logits, AX.X, ALU.max).then_inc(s_route, 1)
            dve.wait_ge(s_route, c.up())
            tt(prob[:, :, :], logits, each(best), ALU.subtract).then_inc(s_route, 1)
            dve.wait_ge(s_route, c.up())
            dve.wait_ge(s_exp, 1)
            reduce(best, prob, ALU.add).then_inc(s_route, 1)
            dve.wait_ge(s_route, c.up())
            nc.vector.reciprocal(best[:, :], best[:, :]).then_inc(s_route, 1)
            dve.wait_ge(s_route, c.up())
            tt(prob[:, :, :], prob[:, :, :], each(best), ALU.mult).then_inc(s_route, 1)
            dve.wait_ge(s_route, c.up())
            dve.wait_ge(s_id, E)
            lower_first = order[:, :].unsqueeze(1).to_broadcast([P, TT, E])
            for k in range(TOP):
                src = left if k else prob
                reduce(best, src, ALU.max).then_inc(s_route, 1)
                dve.wait_ge(s_route, c.up())
                tt(mark[:, :, :], src[:, :, :], each(best), ALU.is_equal).then_inc(s_route, 1)
                dve.wait_ge(s_route, c.up())
                tt(mark[:, :, :], mark[:, :, :], lower_first, ALU.mult).then_inc(s_route, 1)
                dve.wait_ge(s_route, c.up())
                reduce(best, mark, ALU.max).then_inc(s_route, 1)
                dve.wait_ge(s_route, c.up())
                tt(pick[:, :, :], lower_first, each(best), ALU.is_equal).then_inc(s_route, 1)
                dve.wait_ge(s_route, c.up())
                if k == 0:
                    tt(cw[:, :, :], prob[:, :, :], pick[:, :, :], ALU.mult).then_inc(s_route, 1)
                    dve.wait_ge(s_route, c.up())
                    nc.vector.scalar_tensor_tensor(out=left[:, :, :], in0=pick[:, :, :], scalar=-2.0,
                                                   in1=prob[:, :, :], op0=ALU.mult, op1=ALU.add).then_inc(s_route, 1)
                    dve.wait_ge(s_route, c.up())
                else:
                    tt(mark[:, :, :], prob[:, :, :], pick[:, :, :], ALU.mult).then_inc(s_route, 1)
                    dve.wait_ge(s_route, c.up())
                    tt(cw[:, :, :], cw[:, :, :], mark[:, :, :], ALU.add).then_inc(s_route, 1)
                    dve.wait_ge(s_route, c.up())
            nc.vector.tensor_copy(cw16[:, :, 0, :], cw[:, :, :]).then_inc(s_split, 1)
            dve.wait_ge(s_split, 5)
            tt(cw16[:, :, 1, :], cw[:, :, :], cw16[:, :, 0, :], ALU.subtract).then_inc(s_split, 1)
            dve.wait_ge(s_cwt, 1)
            nc.vector.tensor_copy(cwT[:, :, :], cbank[0][:, :].bitcast(F16)[:, 0:PASSES * P].rearrange("p (i d) -> p i d", d=P)).then_inc(s_cwc, 1)
            with dve.Fori(0, PASSES) as it:
                for n in range(N):
                    dve.wait_ge(s_silu, it * N + n + 1)
                    dve.wait_ge(s_down, it * N + max(n - 1, 0))
                    gated = tt(hid[n % 2][:, :], ubank[n % 2][:, :], silu[n % 2][:, :], ALU.mult)
                    if n == NPAIR:
                        gated.then_inc(s_hid, 1)
                    else:
                        gated.then_inc(s_gate, 1)
                        dve.wait_ge(s_gate, it * NPAIR + n + 1)
                        tt(hid[n % 2][:, :], cbank[n % 2][:, :], hid[n % 2][:, :], ALU.mult).then_inc(s_hid, 1)
                dve.wait_ge(s_turn, it + 1)
                x = resid[:, ds(it * TG, TG), :]
                tt(x, tbank[:, :].rearrange("p (t d) -> p t d", d=D), x, ALU.add).then_inc(s_r, 1)


def program(nc, a, out):
    B, SQ, D = a["x"].shape
    TT = B * SQ // P
    with ExitStack() as ctx:
        resid = ctx.enter_context(nc.sbuf_tensor("resid", [P, TT, D], F32))
        xnT = ctx.enter_context(nc.sbuf_tensor("xnT", [D, B * SQ], F32))
        ident = ctx.enter_context(nc.sbuf_tensor("ident", [P, P], F32))
        s_in = ctx.enter_context(nc.semaphore("x_in"))
        s_id = ctx.enter_context(nc.semaphore("ident_steps"))
        s_out = ctx.enter_context(nc.semaphore("out_written"))
        x_tiles = a["x"].rearrange("b (q p) d -> p (b q) d", p=P)
        out_tiles = out.rearrange("b (q p) d -> p (b q) d", p=P)

        with nc.Block() as block:
            @block.sync
            def _(sp):
                sp.dma_start(resid[:, :, :], x_tiles).then_inc(s_in, 16)
                sp.wait_ge(s_in, 16)

            @block.gpsimd
            def _(pool):
                nc.gpsimd.memset(ident[:, :], 0.0).then_inc(s_id, 1)
                pool.wait_ge(s_id, 1)
                nc.gpsimd.affine_select(out=ident[:, :], in_=ident[:, :], compare_op=ALU.not_equal, fill=1.0,
                                        base=0, pattern=[[-1, P]], channel_multiplier=1).then_inc(s_id, 1)
                pool.wait_ge(s_id, 2)
        nc.all_engine_barrier()
        layernorm(nc, resid, xnT, ident, TT, "ln0")
        nc.all_engine_barrier()
        cross_attention_0(nc, resid, xnT, ident, a["ctx_1024"], a["mask_BxSxS2_ik1"],
                          *(a["L0_xattn_" + n] for n in ("Wq", "bq", "Wk", "bk", "Wv", "bv", "Wo", "bo")), B, SQ)
        nc.all_engine_barrier()
        layernorm(nc, resid, xnT, ident, TT, "ln1")
        nc.all_engine_barrier()
        moe_ffn_0(nc, resid, xnT, ident, *(a["L0_ffn_" + n] for n in (
            "gate_w", "gate_b", "dp_w1", "dp_b1", "dp_w2", "dp_b2", "ew1", "eb1", "ew2", "eb2")), TT)
        nc.all_engine_barrier()
        layernorm(nc, resid, xnT, ident, TT, "ln2")
        nc.all_engine_barrier()
        cross_attention_1(nc, resid, xnT, ident, a["ctx_1024"], a["mask_BxS_ik0"],
                          *(a["L1_xattn_" + n] for n in ("Wq", "Wkv", "Wout", "bout")), B, SQ)
        nc.all_engine_barrier()
        layernorm(nc, resid, xnT, ident, TT, "ln3")
        nc.all_engine_barrier()
        moe_ffn_1(nc, resid, xnT, ident, *(a["L1_ffn_" + n] for n in ("Wr", "Wg", "Wu", "Wd", "Sg", "Su", "Sd")), TT)
        nc.all_engine_barrier()
        with nc.Block() as block:
            @block.sync
            def _(sp):
                sp.dma_start(out_tiles, resid[:, :, :]).then_inc(s_out, 16)
                sp.wait_ge(s_out, 16)


_INS = ("x", "ctx_1024", "mask_BxSxS2_ik1", "mask_BxS_ik0",
        "L0_xattn_Wq", "L0_xattn_bq", "L0_xattn_Wk", "L0_xattn_bk", "L0_xattn_Wv", "L0_xattn_bv",
        "L0_xattn_Wo", "L0_xattn_bo", "L0_ffn_gate_w", "L0_ffn_gate_b", "L0_ffn_dp_w1", "L0_ffn_dp_b1",
        "L0_ffn_dp_w2", "L0_ffn_dp_b2", "L0_ffn_ew1", "L0_ffn_eb1", "L0_ffn_ew2", "L0_ffn_eb2",
        "L1_xattn_Wq", "L1_xattn_Wkv", "L1_xattn_Wout", "L1_xattn_bout", "L1_ffn_Wr", "L1_ffn_Wg",
        "L1_ffn_Wu", "L1_ffn_Wd", "L1_ffn_Sg", "L1_ffn_Su", "L1_ffn_Sd")


def kernel(**inputs):
    import numpy as _np
    import concourse.bacc as _bacc
    from concourse import mybir as _mybir
    from concourse.bass_utils import run_bass_kernel_spmd as _run

    nc = _bacc.Bacc("TRN2", target_bir_lowering=False, num_devices=1)
    arrays, a = {}, {}
    for name in _INS:
        arr = _np.ascontiguousarray(inputs[name])
        arrays["in_" + name + "_dram"] = arr
        a[name] = nc.dram_tensor("in_" + name + "_dram", arr.shape, _mybir.dt.from_np(arr.dtype),
                                 kind="ExternalInput").ap()
    out = nc.dram_tensor("out_0_dram", inputs["x"].shape, _mybir.dt.float32, kind="ExternalOutput").ap()
    program(nc, a, out)
    return _run(nc, [arrays], core_ids=[0]).results[0]["out_0_dram"]
```

```python
from contextlib import ExitStack

import numpy as np
import concourse.bass as bass
from concourse import mybir
from concourse.bass import ds

F32 = mybir.dt.float32
F16 = mybir.dt.float16
BF16 = mybir.dt.bfloat16
I32 = mybir.dt.int32
ALU = mybir.AluOpType
ACT = mybir.ActivationFunctionType
AX = mybir.AxisListType
P = 128
BANK = 512

MASK_FILL = -1e30
MASK_NEG = 1e6
LN_EPS = 1e-5


class Steps:

    def __init__(self):
        self.n = 0

    def up(self):
        self.n += 1
        return self.n


class Jobs:

    def __init__(self, first, per, banks):
        self.lists, self.banks = (first, per), banks

    def filled(self, n, it=None):
        return n + 1 if it is None else it * len(self.lists[1]) + (len(self.lists[0]) + n + 1)

    def emptied(self, who, n, it=None):
        first, per = ([w == who for _, w in x] for x in self.lists)
        return sum(first[:n]) if it is None else it * sum(per) + (sum(first) + sum(per[:n]))

    def free(self, n, it=None):
        if n >= self.banks:
            who = self.lists[it is not None][n - self.banks][1]
            return [(who, self.emptied(who, n - self.banks + 1, it))]
        if it is None:
            return []
        (who,) = {w for x in self.lists for _, w in x[-self.banks:]}
        later = min((len(x) - 1 - n) % self.banks for x in self.lists)
        return [(who, self.emptied(who, 0, it) - later)]



def tiles(n, size=P):
    return [(a, min(size, n - a)) for a in range(0, n, size)]


def layernorm(nc, resid, xnT, ident, stats, TT, tag, first=False):
    G = 4
    K = min(4, TT // G)
    with ExitStack() as ctx:
        mean, var, tmp, rstd, shift = (ctx.enter_context(nc.sbuf_tensor(f"{tag}_{n}", [P, TT], F32))
                                       for n in ("mean", "var", "tmp", "rstd", "shift"))
        xn = [ctx.enter_context(nc.sbuf_tensor(f"{tag}_xn{i}", [P, G, P], F32)) for i in range(K)]
        turned = [ctx.enter_context(nc.psum_tensor(f"{tag}_turned{i}", [P, BANK], F32)) for i in range(K)]
        s_stats = ctx.enter_context(nc.semaphore(f"{tag}_stats_done"))
        s_var = ctx.enter_context(nc.semaphore(f"{tag}_var_done"))
        s_std = ctx.enter_context(nc.semaphore(f"{tag}_std_done"))
        s_xd = ctx.enter_context(nc.semaphore(f"{tag}_xn_tile_by_dve"))
        s_xa = ctx.enter_context(nc.semaphore(f"{tag}_xn_tiles_by_act"))
        s_turned = ctx.enter_context(nc.semaphore(f"{tag}_xn_free"))
        s_out = ctx.enter_context(nc.semaphore(f"{tag}_banks_free"))
        block = ctx.enter_context(nc.Block())

        def tile(x, t):
            return x[:, ds(t, 1), :].rearrange("p t d -> p (t d)")

        @block.gpsimd
        def _(pool):
            pool.sem_inc(s_turned, K)
            pool.sem_inc(s_out, K)

        @block.vector
        def _(dve):
            if first:
                with dve.Fori(0, TT // 8) as i:
                    for j in range(8):
                        nc.vector.bn_stats(tile(stats, i * 8 + j), tile(resid, i * 8 + j)).then_inc(s_stats, 1)
                dve.wait_ge(s_stats, TT)
            c = Steps()
            nc.vector.tensor_tensor(mean[:, :], stats[:, :, 1], stats[:, :, 4], ALU.add).then_inc(s_var, 1)
            nc.vector.tensor_tensor(var[:, :], stats[:, :, 2], stats[:, :, 5], ALU.add).then_inc(s_var, 1)
            c.up()
            dve.wait_ge(s_var, c.up())
            nc.vector.tensor_scalar(mean[:, :], mean[:, :], 0.5, None, ALU.mult).then_inc(s_var, 1)
            nc.vector.tensor_scalar(var[:, :], var[:, :], 1.0 / P, LN_EPS, ALU.mult, ALU.add).then_inc(s_var, 1)
            c.up()
            dve.wait_ge(s_var, c.up())
            nc.vector.tensor_tensor(tmp[:, :], stats[:, :, 1], mean[:, :], ALU.subtract).then_inc(s_var, 1)
            dve.wait_ge(s_var, c.up())
            nc.vector.tensor_tensor(tmp[:, :], tmp[:, :], tmp[:, :], ALU.mult).then_inc(s_var, 1)
            dve.wait_ge(s_var, c.up())
            nc.vector.tensor_tensor(var[:, :], var[:, :], tmp[:, :], ALU.add).then_inc(s_var, 1)
            dve.wait_ge(s_var, c.up())
            dve.wait_ge(s_std, 1)
            nc.vector.reciprocal(rstd[:, :], tmp[:, :]).then_inc(s_var, 1)
            dve.wait_ge(s_var, c.up())
            nc.vector.scalar_tensor_tensor(out=shift[:, :], in0=mean[:, :], scalar=-1.0, in1=rstd[:, :],
                                           op0=ALU.mult, op1=ALU.mult).then_inc(s_var, 1)
            with dve.Fori(0, TT // G // K) as i:
                for k in range(K):
                    dve.wait_ge(s_turned, i * K + (k + 1))
                    t = i * (K * G) + k * G
                    nc.vector.tensor_scalar(xn[k][:, 0, :], tile(resid, t), mean[:, ds(t, 1)], rstd[:, ds(t, 1)],
                                            ALU.subtract, ALU.mult).then_inc(s_xd, 1)
                for k in range(K):
                    dve.wait_ge(s_turned, i * K + (K + k + 1))
                    nc.vector.tensor_copy(xnT[:, ds((i * K + k) * BANK, BANK)], turned[k][:, :]).then_inc(s_out, 1)

        @block.tensor
        def _(pe):
            with pe.Fori(0, TT // G // K) as i:
                for k in range(K):
                    pe.wait_ge(s_xd, i * K + (k + 1))
                    pe.wait_ge(s_xa, i * (K * (G - 1)) + (k + 1) * (G - 1))
                    pe.wait_ge(s_out, i * K + (k + 1))
                    for j in range(G):
                        mm = nc.tensor.transpose(turned[k][:, j * P:(j + 1) * P], xn[k][:, j, :], ident[:, :])
                    mm.then_inc(s_turned, 1)

        @block.scalar
        def _(act):
            act.wait_ge(s_var, 7)
            nc.scalar.activation(tmp[:, :], var[:, :], ACT.Sqrt).then_inc(s_std, 1)
            act.wait_ge(s_var, 9)
            with act.Fori(0, TT // G // K) as i:
                for k in range(K):
                    act.wait_ge(s_turned, i * K + (k + 1))
                    for j in range(1, G):
                        t = i * (K * G) + (k * G + j)
                        nc.scalar.activation(xn[k][:, j, :], tile(resid, t), ACT.Identity, bias=shift[:, ds(t, 1)],
                                             scale=rstd[:, ds(t, 1)]).then_inc(s_xa, 1)


def cross_attention_0(nc, resid, stats, xnT, ident, ctx_in, mask_in, Wq, bq, Wk, bk, Wv, bv, Wo, bo, B, SQ):
    SK = ctx_in.shape[1]
    H, D, DK = Wq.shape
    G, HG, CP = 4, 4, 4
    KT = tiles(SK)
    NT = len(KT)
    CH = tiles(SK, BANK)
    U = G * NT
    QT = SQ // P
    ROW = HG * CP * DK
    assert ROW == P and H == G * HG and H * DK == P

    at = {u: [] for u in range(U)}
    at[1].append(("mask", 1))
    at[2].append(("v", 1))
    at[5].append(("mask", 2))
    at[6].append(("v", 2))
    at[9].append(("mask", 3))
    at[10].append(("v", 3))
    for n, u in enumerate((3, 4, 7, 8, 11)):
        at[u].append(("k", 3, n - 1) if n else ("q", 3))
    for c in range(4):
        at[NT + c].append(("ctxT", c))
    for g in range(3):
        at[NT * (g + 1) + 4].append(("q", g))
        for c in range(4):
            at[NT * (g + 1) + 5 + c].append(("k", g, c))
    at[U - 4].append(("mask", 0))
    at[U - 3].append(("v", 0))
    per = [(j, "dve") for u in range(U) for j in at[u]] + [(("y",), "dve")]
    first = [(("ctxT", c), "dve") for c in range(4)]
    for g in range(3):
        first += [(("q", g), "dve")] + [(("k", g, c), "dve") for c in range(4)]
    first += [(("mask", 0), "dve"), (("v", 0), "dve")]
    jobs = Jobs(first, per, 2)
    is_next = {j: u >= NT for u in range(U) for j in at[u]}

    with ExitStack() as ctx:
        def sb(name, shape, dt=F32):
            return ctx.enter_context(nc.sbuf_tensor("a0_" + name, shape, dt))

        def ps(name, shape, dt=F32):
            return ctx.enter_context(nc.psum_tensor("a0_" + name, shape, dt))

        def sem(name):
            return ctx.enter_context(nc.semaphore("a0_" + name))

        w_in = sb("w_in", [D, 3, H, DK])
        wq_rows = sb("wq_rows", [D, G, HG, CP, DK])
        wk_rows = sb("wk_rows", [D, G, HG, CP, DK])
        wo_in = sb("wo_in", [P, P])
        wo_wide = sb("wo_wide", [P, G, HG, 32])
        wo_T = sb("wo_T", [P, G, P])
        b_row = sb("b_row", [1, 2, P])
        HEAD = 2 * G + 2
        rows = sb("rows", [1, HEAD + HG, HG, CP, DK])
        cols = sb("cols", [P, HEAD + HG])
        lo_bias = sb("lo_bias", [P, 2 * G])
        bv_all = sb("bv_all", [P, P])
        bo_all = sb("bo_all", [P, P])
        ident16 = sb("ident16", [P, P], BF16)
        ctx_rows = sb("ctx_rows", [P, NT, D])
        ctxT = sb("ctxT", [D, SK])
        mask_i = sb("mask_i", [P, QT, SK], I32)
        fill = sb("fill", [P, QT, SK], BF16)
        fillT = sb("fillT", [P, NT, SQ], BF16)
        hi = [sb(f"hi{i}", [P, BANK], F16) for i in range(2)]
        q_mix = sb("q_mix", [P, SQ], F16)
        k_op = [sb(f"k_op{g}", [P, SK], F16) for g in range(G)]
        q_op = [sb(f"q_op{g}", [P, HG, SQ], F16) for g in range(G)]
        v = sb("v", [P, NT, P])
        SLOTS, SCORES, LAG, PV_LAG = 4, 5, 2, 3
        AHEAD = 2
        neg_max = [sb(f"neg_max{i}", [P, HG]) for i in range(SLOTS)]
        total = [sb(f"total{i}", [P, HG]) for i in range(SLOTS)]
        recip = [sb(f"recip{i}", [P, HG]) for i in range(SLOTS)]
        e = [sb(f"e{i}", [P, HG, SQ]) for i in range(SLOTS)]
        vn = [sb(f"vn{i}", [P, HG, 32]) for i in range(SLOTS)]
        attn = sb("attn", [P, G, SQ])
        yb = sb("yb", [P, QT, P])

        score = [ps(f"score{i}", [P, HG // 2, SQ]) for i in range(SCORES)]
        attn_acc = ps("attn_acc", [P, 2, SQ])
        bank = [ps(f"bank{i}", [P, BANK]) for i in range(2)]

        s_w = sem("weights_in")
        s_zero = sem("zeros_set")
        s_pool = sem("pool_steps_begun")
        s_id = sem("ident16_set")
        s_const = sem("const_steps")
        s_cpe = sem("const_products")
        s_rec0 = sem("const_parts")
        s_ctx = sem("ctx_in")
        s_mask = sem("mask_in")
        s_fill = sem("fill_ready")
        s_filled = sem("bank_filled")
        s_emptied = sem("bank_emptied")
        s_hi = sem("hi_part_ready")
        s_mix = sem("q_mix_ready")
        s_qop = sem("q_op_rows_written")
        s_score = sem("scores_ready")
        s_max = sem("neg_max_ready")
        s_exp = sem("exp_done")
        s_rec = sem("recip_ready")
        s_vn = sem("vn_ready")
        s_pv = sem("pv_slots_free")
        s_att = sem("attn_copied")
        s_y = sem("resid_steps")
        block = ctx.enter_context(nc.Block())

        N1, NP = len(first), len(per)
        assert U % SLOTS == 0
        names = [[n for n, _ in x] for x in (first, per)]
        CTX_DMAS = 2 if SK % P else 1

        def after_job(job, it):
            return jobs.emptied("dve", names[1].index(job) + 1, it)

        def group_free(job, it):
            return it * (2 * U) + (2 * NT * (job[1] + 1) if job[1] < G - 1 else 0)

        @block.sync
        def _(sp):
            for i, w in enumerate((Wq, Wk, Wv)):
                sp.dma_start(w_in[:, i, :, :], w.rearrange("h d k -> d h k")).then_inc(s_w, 16)
            for i, b in enumerate((bk, bq)):
                sp.dma_start(b_row[:, i, :], b.rearrange("(o h) k -> o (h k)", o=1)).then_inc(s_w, 16)
            sp.dma_start(wo_in[:, :], Wo).then_inc(s_w, 16)
            sp.dma_start(bv_all[:, :], bv.rearrange("(o h) k -> o (h k)", o=1).to_broadcast([P, P])).then_inc(s_w, 16)
            sp.dma_start(bo_all[:, :], bo.rearrange("(o d) -> o d", o=1).to_broadcast([P, P])).then_inc(s_w, 16)

            def load_ctx(b):
                c = ctx_in[ds(b, 1), :, :]
                whole = SK // P
                sp.dma_start(ctx_rows[:, 0:whole, :],
                             c[:, 0:whole * P, :].rearrange("o (t p) d -> p (o t) d", p=P)).then_inc(s_ctx, 16)
                if SK % P:
                    sp.dma_start(ctx_rows[0:SK % P, whole, :],
                                 c[:, whole * P:SK, :].rearrange("o p d -> (o p) d")).then_inc(s_ctx, 16)

            def load_mask(b):
                m = mask_in[ds(b, 1), :, :]
                sp.dma_start(mask_i[:, :, :], m.rearrange("o (t p) s -> p (o t) s", p=P)).then_inc(s_mask, 16)

            load_ctx(0)
            load_mask(0)
            with sp.Fori(0, B) as it:
                sp.wait_ge(s_filled, it * NP + N1)
                load_ctx((it + 1) % B)
                sp.wait_ge(s_fill, (it + 1) * QT)
                load_mask((it + 1) % B)
            sp.wait_ge(s_ctx, 16 * CTX_DMAS * (B + 1))
            sp.wait_ge(s_mask, 16 * (B + 1))

        @block.gpsimd
        def _(pool):
            pool.sem_inc(s_pv, SLOTS)
            nc.gpsimd.memset(wo_wide[:, :, :, :], 0.0).then_inc(s_zero, 1)
            for x in vn:
                nc.gpsimd.memset(x[:, :, :], 0.0).then_inc(s_zero, 1)
            nc.gpsimd.tensor_scalar(ident16[:, :], ident[:, :], 1.0, 1.0, ALU.mult, ALU.mult).then_inc(s_id, 1)

            def make_fill(before):
                pool.wait_ge(s_mask, 16 * before + 16)
                pool.sem_inc(s_pool, 1)
                pool.wait_ge(s_zero, 1 + SLOTS)
                for q in range(QT):
                    nc.gpsimd.tensor_scalar(fill[:, q, :], mask_i[:, q, :], 0.0, MASK_FILL,
                                            ALU.is_equal, ALU.mult).then_inc(s_fill, 1)

            def place_q(g, before, it=None):
                pool.wait_ge(s_mix, before + 1)
                if it is not None:
                    pool.wait_ge(s_score, group_free(("q", g), it))
                    pool.sem_inc(s_pool, 1)
                for i in range(HG):
                    nc.gpsimd.tensor_scalar(q_op[g][:, i, :], q_mix[:, :], cols[:, HEAD + i:HEAD + i + 1], 1.0,
                                            ALU.mult, ALU.mult).then_inc(s_qop, 1)

            make_fill(0)
            pool.wait_ge(s_const, 4)
            for g in range(G - 1):
                place_q(g, g)
            with pool.Fori(0, B) as it:
                place_q(G - 1, it * G + (G - 1), it)
                pool.wait_ge(s_filled, jobs.filled(names[1].index(("mask", 3)), it))
                make_fill(it + 1)
                for g in range(G - 1):
                    place_q(g, it * G + (G + g), it)

        @block.tensor
        def _(pe):
            pe.wait_ge(s_const, 1)
            for j in range(HEAD + HG):
                mm = nc.tensor.matmul(bank[0][:, j:j + 1], rows[0:1, j, :, :, :].rearrange("o h c k -> o (h c k)"),
                                      ident[0:1, 0:1], start=True, stop=True)
            mm.then_inc(s_cpe, 1)
            pe.wait_ge(s_const, 3)
            for g in range(G):
                mm = nc.tensor.transpose(bank[0][:, g * P:(g + 1) * P],
                                         wo_wide[:, g, :, :].rearrange("p h k -> p (h k)"), ident[:, :])
            mm.then_inc(s_cpe, 1)
            pe.wait_ge(s_const, 4)
            pe.wait_ge(s_id, 1)

            def job(n, j, it=None):
                for _, count in jobs.free(n, it):
                    pe.wait_ge(s_emptied, count)
                bk_ = bank[n % 2]
                if j[0] == "ctxT":
                    if it is None:
                        pe.wait_ge(s_ctx, 16 * CTX_DMAS)
                    else:
                        pe.wait_ge(s_ctx, it * (16 * CTX_DMAS) + 32 * CTX_DMAS)
                    for t in range(4 * j[1], min(4 * j[1] + 4, NT)):
                        r = KT[t][1]
                        mm = nc.tensor.transpose(bk_[:, (t % 4) * P:(t % 4) * P + r], ctx_rows[0:r, t, :],
                                                 ident[0:r, 0:r])
                elif j[0] == "mask":
                    turned = bk_[:, :].bitcast(BF16)
                    if it is None or is_next[j]:
                        pe.wait_ge(s_fill, QT if it is None else it * QT + 2 * QT)
                    for t in range(4 * j[1], min(4 * j[1] + 4, NT)):
                        s0, r = KT[t]
                        for q in range(QT):
                            at_ = (t % 4) * SQ + q * P
                            mm = nc.tensor.transpose(turned[0:r, at_:at_ + P], fill[:, q, s0:s0 + r], ident16[:, :])
                elif j[0] == "q":
                    b = 0 if it is None else (it + 1) % B if is_next[j] else it
                    mm = nc.tensor.matmul(bk_[:, 0:SQ], wq_rows[:, j[1], :, :, :].rearrange("p h c k -> p (h c k)"),
                                          xnT[:, ds(b * SQ, SQ)], start=True, stop=True)
                elif j[0] == "k":
                    s0, r = CH[j[2]]
                    pe.wait_ge(s_emptied, jobs.emptied("dve", 4) if it is None else
                               after_job(("ctxT", 3), it) if is_next[j] else it * NP + N1)
                    mm = nc.tensor.matmul(bk_[:, 0:r], wk_rows[:, j[1], :, :, :].rearrange("p h c k -> p (h c k)"),
                                          ctxT[:, s0:s0 + r], start=True, stop=True)
                elif j[0] == "v":
                    pe.wait_ge(s_emptied, jobs.emptied("dve", 4) if it is None else
                               after_job(("ctxT", 3), it) if is_next[j] else it * NP + N1)
                    for t in range(4 * j[1], min(4 * j[1] + 4, NT)):
                        s0, r = KT[t]
                        mm = nc.tensor.matmul(bk_[0:r, (t % 4) * P:(t % 4 + 1) * P], ctxT[:, s0:s0 + r],
                                              w_in[:, 2, :, :].rearrange("p h k -> p (h k)"), start=True, stop=True)
                mm.then_inc(s_filled, 1)

            def project(groups, it):
                bk_ = bank[(NP - 1) % 2]
                if groups[0] == 0:
                    for _, count in jobs.free(NP - 1, it):
                        pe.wait_ge(s_emptied, count)
                pe.wait_ge(s_att, it * G + groups[-1] + 1)
                for g in groups:
                    for q in range(QT):
                        mm = nc.tensor.matmul(bk_[:, q * P:(q + 1) * P], attn[:, g, q * P:(q + 1) * P],
                                              wo_T[:, g, :], start=(q == 0 and g == 0), stop=(g == G - 1),
                                              skip_group_check=True)
                if groups[-1] == G - 1:
                    mm.then_inc(s_filled, 1)

            def scores(u, it):
                ahead, u = divmod(u, U)
                g, t = divmod(u, NT)
                s0, r = KT[t]
                row = 0 if it is None else it
                if t == 0:
                    pe.wait_ge(s_qop, row * (HG * G) + HG * (G * ahead + g + 1))
                if it is None or ahead:
                    src = names[it is not None].index(("mask", 0))
                    pe.wait_ge(s_emptied, jobs.emptied("dve", src + 1, it))
                elif g == 0 and t % 4 == 0:
                    pe.wait_ge(s_emptied, after_job(("mask", t // 4), it))
                elif u == NT * (G - 1):
                    pe.wait_ge(s_emptied, after_job(("k", G - 1, 3), it))
                for half in range(2):
                    w = 2 * u + half
                    last = w - SCORES + 2 * U * ahead if w >= SCORES else 2 * U - 1 - (2 * U - 1 - w) % SCORES
                    if it is not None:
                        pe.wait_ge(s_exp, it * (2 * U) + (last + 1 if ahead or w >= SCORES else 0))
                    elif w >= SCORES:
                        pe.wait_ge(s_exp, last + 1)
                    o = score[w % SCORES][0:r, :, :]
                    nc.tensor.matmul(o, k_op[g][:, s0:s0 + r], q_op[g][:, 2 * half:2 * half + 2, :],
                                     start=True, stop=False)
                    mm = nc.tensor.matmul(o, ident16[0:r, 0:r],
                                          fillT[0:r, t, :].unsqueeze(1).to_broadcast([r, 2, SQ]),
                                          start=False, stop=True)
                    mm.then_inc(s_score, 1)

            def pv(u, it):
                g, t = divmod(u, NT)
                r = KT[t][1]
                pe.wait_ge(s_vn, it * U + u + 1)
                if t == 0:
                    pe.wait_ge(s_att, it * G + g)
                for i in range(HG):
                    mm = nc.tensor.matmul(attn_acc[32 * i:32 * i + 32, g % 2, :], vn[u % SLOTS][0:r, i, :],
                                          e[u % SLOTS][0:r, i, :], start=(t == 0),
                                          stop=(t == NT - 1))
                mm.then_inc(s_pv, 1)

            for n, (j, _) in enumerate(first):
                job(n, j)
            for u in range(AHEAD):
                scores(u, None)
            with pe.Fori(0, B) as it:
                n = 0
                for u in range(U):
                    if u >= AHEAD:
                        scores(u, it)
                    for j in at[u]:
                        job(n, j, it)
                        n += 1
                    if u >= PV_LAG:
                        pv(u - PV_LAG, it)
                for n_, u in enumerate(range(U - PV_LAG, U)):
                    if n_ < AHEAD:
                        scores(U + n_, it)
                    if u == U - 1:
                        project(range(G - 1), it)
                    pv(u, it)
                project([G - 1], it)

        @block.scalar
        def _(act):
            def hi_part(n, j, k, it=None):
                N = SQ if j[0] == "q" else CH[j[2]][1]
                act.wait_ge(s_filled, jobs.filled(n, it))
                if k >= 2:
                    act.wait_ge(s_emptied, jobs.emptied("dve", hi_at[it is not None][k - 2] + 1, it))
                elif it is not None:
                    act.wait_ge(s_emptied, it * NP + N1)
                c = j[1] + (G if j[0] == "q" else 0)
                m = 2 * G + (1 if j[0] == "q" else 0)
                nc.scalar.activation(hi[k % 2][:, 0:N], bank[n % 2][:, 0:N], ACT.Identity,
                                     bias=lo_bias[:, c:c + 1], scale=cols[:, m:m + 1]).then_inc(s_hi, 1)

            hi_at = [[n for n, j in enumerate(x) if j[0] in "qk"] for x in names]
            act.wait_ge(s_const, 4)
            for k, n in enumerate(hi_at[0]):
                hi_part(n, names[0][n], k)
            with act.Fori(0, B) as it:
                n = 0
                for u in range(U):
                    for j in at[u - 1] if u else []:
                        if n in hi_at[1]:
                            hi_part(n, j, hi_at[1].index(n), it)
                        n += 1
                    r = KT[u % NT][1]
                    act.wait_ge(s_pv, it * U + u + 1)
                    for i in range(HG):
                        w = 2 * u + i // 2
                        if i % 2 == 0:
                            act.wait_ge(s_max, it * (2 * U) + w + 1)
                        ex = nc.scalar.activation(e[u % SLOTS][0:r, i, :], score[w % SCORES][0:r, i % 2, :], ACT.Exp,
                                                  bias=neg_max[u % SLOTS][0:r, i:i + 1],
                                                  accum_out=total[u % SLOTS][0:r, i:i + 1])
                        if i % 2 == 1:
                            ex.then_inc(s_exp, 1)

        @block.vector
        def _(dve):
            dve.wait_ge(s_w, 8 * 16)
            nc.vector.memset(rows[:, 2 * G:, :, :, :], 0.0).then_inc(s_rec0, 1)
            dve.wait_ge(s_rec0, 1)
            nc.vector.memset(rows[:, 2 * G, :, 2:4, :], 1.0)
            for i in range(HG):
                nc.vector.memset(rows[:, HEAD + i, i, :, :], 1.0)
            for c in (1, 3):
                nc.vector.memset(rows[:, 2 * G + 1, :, c, :], 1.0)
            for i, scale in ((0, 1.0), (1, 0.125)):
                for g in range(G):
                    src = b_row[0:1, i, g * HG * DK:(g + 1) * HG * DK].rearrange("o (h k) -> o h k", h=HG)
                    last = nc.vector.tensor_scalar(rows[:, i * G + g, :, :, :],
                                                   src.unsqueeze(2).to_broadcast([1, HG, CP, DK]),
                                                   scale, None, ALU.mult)
            last.then_inc(s_const, 1)
            dve.wait_ge(s_zero, 1 + SLOTS)
            for g in range(G):
                last = nc.vector.tensor_copy(wo_wide[:, g, :, 0:DK],
                                             wo_in[:, g * HG * DK:(g + 1) * HG * DK].rearrange("p (h k) -> p h k", h=HG))
            last.then_inc(s_const, 1)
            for i, (dst, scale) in enumerate(((wq_rows, 0.125), (wk_rows, 1.0))):
                for g in range(G):
                    nc.vector.tensor_scalar(dst[:, g, :, :, :],
                                            w_in[:, i, g * HG:(g + 1) * HG, :].unsqueeze(2).to_broadcast([D, HG, CP, DK]),
                                            scale, None, ALU.mult)
            dve.wait_ge(s_cpe, 1)
            nc.vector.tensor_copy(cols[:, :], bank[0][:, 0:HEAD + HG]).then_inc(s_rec0, 1)
            dve.wait_ge(s_rec0, 2)
            for i in range(2):
                last = nc.vector.tensor_scalar(lo_bias[:, i * G:(i + 1) * G], cols[:, i * G:(i + 1) * G],
                                               cols[:, 2 * G + i:2 * G + i + 1], None, ALU.mult)
            last.then_inc(s_const, 1)
            dve.wait_ge(s_cpe, 2)
            nc.vector.tensor_copy(wo_T[:, :, :], bank[0][:, :].rearrange("p (g d) -> p g d", g=G)).then_inc(s_const, 1)

            def empty(n, j, it=None):
                bk_ = bank[n % 2]
                dve.wait_ge(s_filled, jobs.filled(n, it))
                if j[0] == "ctxT":
                    s0, r = CH[j[1]]
                    if it is not None and j[1] == 0:
                        dve.wait_ge(s_filled, it * NP + N1 + n)
                    ins = nc.vector.tensor_copy(ctxT[:, s0:s0 + r], bk_[:, 0:r])
                elif j[0] == "mask":
                    turned = bk_[:, :].bitcast(BF16)
                    if it is not None:
                        dve.wait_ge(s_score, it * (2 * U) + (2 * (NT * (G - 1) + 4) if is_next[j] else 0))
                    lo, hi_ = 4 * j[1], min(4 * j[1] + 4, NT)
                    r = KT[hi_ - 1][1]
                    ins = nc.vector.tensor_copy(fillT[0:r, lo:hi_, :],
                                                turned[0:r, 0:(hi_ - lo) * SQ].rearrange("p (t q) -> p t q", q=SQ))
                elif j[0] == "v":
                    lo, hi_ = 4 * j[1], min(4 * j[1] + 4, NT)
                    r = KT[hi_ - 1][1]
                    ins = nc.vector.tensor_tensor(v[0:r, lo:hi_, :], bk_[0:r, 0:(hi_ - lo) * P].rearrange("p (t d) -> p t d", d=P),
                                                  bv_all[0:r, :].unsqueeze(1).to_broadcast([r, hi_ - lo, P]), ALU.add)
                elif j[0] in "qk":
                    k = hi_at[it is not None].index(n)
                    before = len(hi_at[0]) if it is not None else 0
                    dve.wait_ge(s_hi, k + 1 if it is None else it * len(hi_at[1]) + (before + k + 1))
                    q_jobs = sum(x[0] == "q" for x in names[it is not None][:n])
                    if j[0] == "q":
                        N, c, dst = SQ, G + j[1], q_mix[:, :]
                        dve.wait_ge(s_qop, HG * q_jobs if it is None else it * (HG * G) + HG * (G - 1 + q_jobs))
                    else:
                        s0, N = CH[j[2]]
                        c, dst = j[1], k_op[j[1]][:, s0:s0 + N]
                        if it is not None and j[2] == 0:
                            dve.wait_ge(s_score, group_free(j, it))
                    ins = nc.vector.scalar_tensor_tensor(out=dst, in0=bk_[:, 0:N], scalar=cols[:, c:c + 1],
                                                         in1=hi[k % 2][:, 0:N], op0=ALU.add, op1=ALU.subtract)
                ins.then_inc(s_emptied, 1)
                if j[0] == "q":
                    dve.wait_ge(s_emptied, jobs.emptied("dve", n + 1, it))
                    dve.sem_inc(s_mix, 1)

            def maximum(u, it):
                r = KT[u % NT][1] if u < U else KT[u - U][1]
                for w in (2 * u, 2 * u + 1):
                    dve.wait_ge(s_score, w + 1 if it is None else it * (2 * U) + w + 1)
                    k = w % (2 * U) % SCORES
                    nc.vector.tensor_reduce(neg_max[u % SLOTS][0:r, w % 2 * 2:w % 2 * 2 + 2],
                                            score[k][0:r, :, :], AX.X, ALU.max,
                                            negate=True).then_inc(s_max, 1)

            def scaled_v(u, it):
                g, t = divmod(u, NT)
                r, slot = KT[t][1], u % SLOTS
                dve.wait_ge(s_exp, it * (2 * U) + 2 * u + 2)
                nc.vector.reciprocal(recip[slot][0:r, :], total[slot][0:r, :]).then_inc(s_rec, 1)
                dve.wait_ge(s_rec, it * U + u + 1)
                if u == 0:
                    dve.wait_ge(s_emptied, it * NP + N1)
                elif g == 0 and t % 4 == 0:
                    dve.wait_ge(s_emptied, after_job(("v", t // 4), it))
                dve.wait_ge(s_pv, it * U + u + 1)
                w = HG * DK
                nc.vector.tensor_tensor(vn[slot][0:r, :, 0:DK],
                                        v[0:r, t, g * w:(g + 1) * w].rearrange("p (h k) -> p h k", h=HG),
                                        recip[slot][0:r, :].unsqueeze(2).to_broadcast([r, HG, DK]),
                                        ALU.mult).then_inc(s_vn, 1)

            def copy_attn(g, it):
                dve.wait_ge(s_pv, it * U + (SLOTS + (g + 1) * NT))
                dve.wait_ge(s_filled, it * NP + N1)
                nc.vector.tensor_copy(attn[:, g, :], attn_acc[:, g % 2, :]).then_inc(s_att, 1)

            hi_at = [[n for n, j in enumerate(x) if j[0] in "qk"] for x in names]
            for n, (j, _) in enumerate(first):
                empty(n, j)
            for u in range(AHEAD):
                maximum(u, None)
            with dve.Fori(0, B) as it:
                n = 0
                for u in range(U):
                    if u > NT and u % NT == PV_LAG:
                        copy_attn(u // NT - 1, it)
                    if u >= AHEAD:
                        maximum(u, it)
                    for j in at[u - 1] if u else []:
                        empty(n, j, it)
                        n += 1
                    if u >= LAG:
                        scaled_v(u - LAG, it)
                for n_, u in enumerate(range(U - LAG, U)):
                    if n_ < AHEAD:
                        maximum(U + n_, it)
                    scaled_v(u, it)
                for u in range(LAG, AHEAD):
                    maximum(U + u, it)
                copy_attn(G - 1, it)
                dve.wait_ge(s_filled, jobs.filled(n, it))
                nc.vector.tensor_tensor(yb[:, :, :], bank[n % 2][:, 0:QT * P].rearrange("p (q d) -> p q d", q=QT),
                                        bo_all[:, :].unsqueeze(1).to_broadcast([P, QT, P]), ALU.add).then_inc(s_emptied, 1)
                dve.wait_ge(s_emptied, jobs.emptied("dve", n + 1, it))
                x = resid[:, ds(it * QT, QT), :]
                nc.vector.tensor_tensor(x, x, yb[:, :, :], ALU.add).then_inc(s_y, 1)
                dve.wait_ge(s_y, it * (1 + QT) + 1)
                for q in range(QT):
                    st, x = (a_[:, ds(it * QT + q, 1), :].rearrange("p t d -> p (t d)") for a_ in (stats, resid))
                    nc.vector.bn_stats(st, x).then_inc(s_y, 1)


def moe_ffn_0(nc, resid, stats, xnT, ident, gate_w, gate_b, dp_w1, dp_b1, dp_w2, dp_b2, ew1, eb1, ew2, eb2, TT):
    D, E = gate_w.shape
    DH = dp_w1.shape[1]
    HE = ew1.shape[2]
    HC = HE // P
    TG = BANK // P
    PASSES = TT // TG
    LROW = 96
    assert HC == 2 and E == 4
    Z_STEPS = 2
    L_STEPS = Z_STEPS + 1 + E + E - 1 + E
    with ExitStack() as ctx:
        def sb(name, shape, dt=F32):
            return ctx.enter_context(nc.sbuf_tensor("f0_" + name, shape, dt))

        def sem(name):
            return ctx.enter_context(nc.semaphore("f0_" + name))

        w_dp1 = sb("w_dp1", [D, P])
        w_dp2 = sb("w_dp2", [P, P])
        b_dp1 = sb("b_dp1", [P, 1])
        b_dp2 = sb("b_dp2", [P, 1])
        b_gate = sb("b_gate", [P, E])
        w_e1 = sb("w_e1", [D, E, HE])
        w_e2 = sb("w_e2", [P, E, HC, D])
        b_e1 = sb("b_e1", [P, E * HC])
        b_e2 = sb("b_e2", [P, E, D])
        dp_h = sb("dp_h", [P, BANK])
        lz_rows = sb("lz_rows", [P, BANK])
        logit = sb("logit", [P, TT, E + 1])
        lg = [sb(f"lg{i}", [P, TT]) for i in range(E)]
        weight = sb("weight", [P, E, TT])
        pos = [sb(f"pos{i}", [P, TT]) for i in range(E)]
        top = sb("top", [P, TT])
        z = sb("z", [P, TT])
        ez = sb("ez", [P, TT])
        k_tok = sb("k_tok", [P, TT])
        t0 = sb("t0", [P, TT])
        t1 = sb("t1", [P, TT])
        hid = [sb(f"hid{i}", [P, BANK]) for i in range(E * HC)]
        y_b = [sb(f"y_b{i}", [P, E, D]) for i in range(TG)]
        hbank = [ctx.enter_context(nc.psum_tensor(f"f0_hbank{i}", [P, BANK], F32)) for i in range(4)]
        ybank = [ctx.enter_context(nc.psum_tensor(f"f0_ybank{i}", [P, E, D], F32)) for i in range(TG)]
        s_w = sem("weights_in")
        s_zero = sem("lz_rows_zeroed")
        s_dp = sem("difficulty_hidden")
        s_dph = sem("dp_h_ready")
        s_lz = sem("logits_and_z")
        s_lzr = sem("lz_rows_ready")
        s_turn = sem("logits_turned")
        s_log = sem("logit_written")
        s_g = sem("gate_steps")
        s_ea = sem("exp_abs_z")
        s_ln = sem("softplus_log")
        s_el = sem("exp_logits")
        s_h = sem("hidden_filled")
        s_ha = sem("hidden_relu_act")
        s_hv = sem("hidden_relu_dve")
        s_y = sem("y_filled")
        s_yb = sem("y_biased")
        s_r = sem("resid_steps")
        s_st = sem("stats_done")
        block = ctx.enter_context(nc.Block())

        @block.sync
        def _(sp):
            sp.wait_ge(s_zero, 4)
            with nc.allow_non_contiguous_dma(reason="narrow weights"):
                sp.dma_start(w_dp1[:, LROW:LROW + E], gate_w).then_inc(s_w, 16)
                sp.dma_start(w_dp1[:, 0:DH], dp_w1).then_inc(s_w, 16)
                sp.dma_start(w_dp2[0:DH, LROW + E:LROW + E + 1], dp_w2).then_inc(s_w, 16)
                sp.dma_start(b_dp1[0:DH, :], dp_b1.rearrange("(p o) -> p o", o=1)).then_inc(s_w, 16)
            sp.dma_start(b_dp2[:, :], dp_b2.rearrange("(o p) -> o p", o=1).to_broadcast([P, 1])).then_inc(s_w, 16)
            sp.dma_start(b_gate[:, :], gate_b.rearrange("(o e) -> o e", o=1).to_broadcast([P, E])).then_inc(s_w, 16)
            sp.dma_start(w_e1[:, :, :], ew1.rearrange("e d h -> d e h")).then_inc(s_w, 16)
            sp.dma_start(w_e2[:, :, :, :], ew2.rearrange("e (c p) d -> p e c d", p=P)).then_inc(s_w, 16)
            for e in range(E):
                with nc.allow_non_contiguous_dma(reason="a bias to a partition"):
                    sp.dma_start(b_e1[:, e * HC:(e + 1) * HC],
                                 eb1[e, :].rearrange("(c p) -> p c", p=P)).then_inc(s_w, 16)
            sp.dma_start(b_e2[:, :, :], eb2.rearrange("(o e) d -> o e d", o=1).to_broadcast([P, E, D])).then_inc(s_w, 16)
            sp.wait_ge(s_w, 16 * (9 + E))

        @block.tensor
        def _(pe):
            pe.wait_ge(s_w, 16 * (9 + E))
            with pe.Fori(0, PASSES) as it:
                x = xnT[:, ds(it * BANK, BANK)]
                pe.wait_ge(s_lzr, 2 * it)
                nc.tensor.matmul(hbank[0][:, :], w_dp1[:, :], x, start=True, stop=True).then_inc(s_dp, 1)
                pe.wait_ge(s_dph, it + 1)
                nc.tensor.matmul(hbank[1][:, :], w_dp2[:, :], dp_h[:, :], start=True, stop=True).then_inc(s_lz, 1)
                pe.wait_ge(s_lzr, 2 * it + 2)
                pe.wait_ge(s_log, it)
                for j in range(TG):
                    mm = nc.tensor.transpose(hbank[2][:, j * P:(j + 1) * P], lz_rows[:, j * P:(j + 1) * P],
                                             ident[:, :])
                mm.then_inc(s_turn, 1)
            pe.wait_ge(s_log, PASSES)
            with pe.Fori(0, PASSES) as it:
                x = xnT[:, ds(it * BANK, BANK)]
                for n in range(E * HC):
                    e, c = divmod(n, HC)
                    pe.wait_ge(s_hv if n % 2 else s_ha, it * (E * HC // 2) + max(n // 2 - 1, 0))
                    nc.tensor.matmul(hbank[n % 4][:, :], w_e1[:, e, c * P:(c + 1) * P], x,
                                     start=True, stop=True).then_inc(s_h, 1)
                for j in range(TG):
                    pe.wait_ge(s_yb, it * TG + j)
                    for n in range(E * HC):
                        if j == 0:
                            pe.wait_ge(s_hv if n % 2 else s_ha, it * (E * HC // 2) + (n // 2 + 1))
                        e, c = divmod(n, HC)
                        mm = nc.tensor.matmul(ybank[j][:, e, :], hid[n][:, j * P:(j + 1) * P], w_e2[:, e, c, :],
                                              start=(n == 0), stop=(c == HC - 1), skip_group_check=True)
                    mm.then_inc(s_y, 1)

        @block.scalar
        def _(act):
            with act.Fori(0, PASSES) as it:
                act.wait_ge(s_dp, it + 1)
                act.wait_ge(s_lz, it)
                nc.scalar.activation(dp_h[:, :], hbank[0][:, :], ACT.Relu, bias=b_dp1[:, 0:1]).then_inc(s_dph, 1)
            act.wait_ge(s_g, Z_STEPS)
            nc.scalar.activation(ez[:, :], t0[:, :], ACT.Exp, scale=-1.0).then_inc(s_ea, 1)
            act.wait_ge(s_g, Z_STEPS + 1)
            nc.scalar.activation(t0[:, :], ez[:, :], ACT.Ln).then_inc(s_ln, 1)
            act.wait_ge(s_g, L_STEPS)
            nc.scalar.activation(weight[:, :, :], weight[:, :, :], ACT.Exp).then_inc(s_el, 1)
            with act.Fori(0, PASSES) as it:
                for n in range(0, E * HC, 2):
                    act.wait_ge(s_h, it * (E * HC) + n + 1)
                    act.wait_ge(s_y, it * TG)
                    nc.scalar.activation(hid[n][:, :], hbank[n % 4][:, :], ACT.Relu,
                                         bias=b_e1[:, n:n + 1]).then_inc(s_ha, 1)

        @block.vector
        def _(dve):
            for x in (lz_rows, w_dp1, w_dp2, b_dp1):
                nc.vector.memset(x[:, :], 0.0).then_inc(s_zero, 1)
            dve.wait_ge(s_zero, 4)
            dve.wait_ge(s_w, 16 * (9 + E))
            with dve.Fori(0, PASSES) as it:
                rows = slice(LROW, P)
                dve.wait_ge(s_turn, it)
                dve.wait_ge(s_dph, it + 1)
                nc.vector.tensor_copy(lz_rows[rows, :], hbank[0][rows, :]).then_inc(s_lzr, 1)
                dve.wait_ge(s_lzr, 2 * it + 1)
                dve.wait_ge(s_lz, it + 1)
                nc.vector.tensor_tensor(lz_rows[rows, :], hbank[1][rows, :], lz_rows[rows, :], ALU.add).then_inc(s_lzr, 1)
                dve.wait_ge(s_turn, it + 1)
                nc.vector.tensor_copy(logit[:, ds(it * TG, TG), :],
                                      hbank[2][:, :].rearrange("p (t r) -> p t r", t=TG)[:, :, LROW:LROW + E + 1]).then_inc(s_log, 1)
            dve.wait_ge(s_log, PASSES)
            c = Steps()
            tt, ts = nc.vector.tensor_tensor, nc.vector.tensor_scalar
            ts(z[:, :], logit[:, :, E], b_dp2[:, 0:1], None, ALU.add).then_inc(s_g, 1)
            dve.wait_ge(s_g, c.up())
            nc.vector.scalar_tensor_tensor(out=t0[:, :], in0=z[:, :], scalar=-1.0, in1=z[:, :],
                                           op0=ALU.mult, op1=ALU.max).then_inc(s_g, 1)
            dve.wait_ge(s_g, c.up())
            assert c.n == Z_STEPS
            dve.wait_ge(s_ea, 1)
            ts(ez[:, :], ez[:, :], 1.0, None, ALU.add).then_inc(s_g, 1)
            dve.wait_ge(s_g, c.up())
            for i in range(E):
                ts(lg[i][:, :], logit[:, :, i], b_gate[:, i:i + 1], None, ALU.add).then_inc(s_g, 1)
                dve.wait_ge(s_g, c.up())
            tt(top[:, :], lg[0][:, :], lg[1][:, :], ALU.max).then_inc(s_g, 1)
            dve.wait_ge(s_g, c.up())
            for i in range(2, E):
                tt(top[:, :], top[:, :], lg[i][:, :], ALU.max).then_inc(s_g, 1)
                dve.wait_ge(s_g, c.up())
            for i in range(E):
                tt(weight[:, i, :], lg[i][:, :], top[:, :], ALU.subtract).then_inc(s_g, 1)
                c.up()
            dve.wait_ge(s_g, c.n)
            assert c.n == L_STEPS
            for i in range(E):
                nc.vector.memset(pos[i][:, :], float(E - 1 - i)).then_inc(s_g, 1)
                dve.wait_ge(s_g, c.up())
            for i in range(E):
                for j in range(i + 1, E):
                    tt(t1[:, :], lg[i][:, :], lg[j][:, :], ALU.is_ge).then_inc(s_g, 1)
                    dve.wait_ge(s_g, c.up())
                    tt(pos[j][:, :], pos[j][:, :], t1[:, :], ALU.add).then_inc(s_g, 1)
                    dve.wait_ge(s_g, c.up())
                    tt(pos[i][:, :], pos[i][:, :], t1[:, :], ALU.subtract).then_inc(s_g, 1)
                    dve.wait_ge(s_g, c.up())
            dve.wait_ge(s_ln, 1)
            nc.vector.scalar_tensor_tensor(out=z[:, :], in0=z[:, :], scalar=0.0, in1=t0[:, :],
                                           op0=ALU.max, op1=ALU.add).then_inc(s_g, 1)
            dve.wait_ge(s_g, c.up())
            ts(z[:, :], z[:, :], -0.5, 1.0 / 1.5, ALU.add, ALU.mult).then_inc(s_g, 1)
            dve.wait_ge(s_g, c.up())
            ts(z[:, :], z[:, :], 0.0, 1.0, ALU.max, ALU.min).then_inc(s_g, 1)
            dve.wait_ge(s_g, c.up())
            ts(z[:, :], z[:, :], float(E - 1), 1.0, ALU.mult, ALU.add).then_inc(s_g, 1)
            dve.wait_ge(s_g, c.up())
            ts(k_tok[:, :], z[:, :], 1.5, 1.0, ALU.is_ge, ALU.add).then_inc(s_g, 1)
            dve.wait_ge(s_g, c.up())
            for edge, compare in ((2.5, ALU.is_gt), (3.5, ALU.is_ge)):
                ts(t1[:, :], z[:, :], edge, None, compare).then_inc(s_g, 1)
                dve.wait_ge(s_g, c.up())
                tt(k_tok[:, :], k_tok[:, :], t1[:, :], ALU.add).then_inc(s_g, 1)
                dve.wait_ge(s_g, c.up())
            dve.wait_ge(s_el, 1)
            for i in range(E):
                tt(t1[:, :], pos[i][:, :], k_tok[:, :], ALU.is_lt).then_inc(s_g, 1)
                dve.wait_ge(s_g, c.up())
                tt(weight[:, i, :], weight[:, i, :], t1[:, :], ALU.mult).then_inc(s_g, 1)
                dve.wait_ge(s_g, c.up())
            nc.vector.tensor_reduce(t0[:, :], weight[:, :, :].rearrange("p e t -> p t e"), AX.X, ALU.add).then_inc(s_g, 1)
            dve.wait_ge(s_g, c.up())
            nc.vector.reciprocal(t1[:, :], t0[:, :]).then_inc(s_g, 1)
            dve.wait_ge(s_g, c.up())
            for i in range(E):
                tt(weight[:, i, :], weight[:, i, :], t1[:, :], ALU.mult).then_inc(s_g, 1)
                dve.wait_ge(s_g, c.up())
            with dve.Fori(0, PASSES) as it:
                for n in range(1, E * HC, 2):
                    dve.wait_ge(s_h, it * (E * HC) + n + 1)
                    dve.wait_ge(s_y, it * TG)
                    ts(hid[n][:, :], hbank[n % 4][:, :], b_e1[:, n:n + 1], 0.0, ALU.add, ALU.max).then_inc(s_hv, 1)
                for j in range(TG):
                    dve.wait_ge(s_y, it * TG + j + 1)
                    dve.wait_ge(s_r, it * (E * TG))
                    tt(y_b[j][:, :, :], ybank[j][:, :, :], b_e2[:, :, :], ALU.add).then_inc(s_yb, 1)
                dve.wait_ge(s_yb, it * TG + TG)
                for i in range(E):
                    dve.wait_ge(s_r, it * (E * TG) + i * TG)
                    for j in range(TG):
                        x = resid[:, ds(it * TG + j, 1), :].rearrange("p t d -> p (t d)")
                        w = weight[:, i, ds(it * TG + j, 1)]
                        nc.vector.scalar_tensor_tensor(out=x, in0=y_b[j][:, i, :], scalar=w, in1=x,
                                                       op0=ALU.mult, op1=ALU.add).then_inc(s_r, 1)
                dve.wait_ge(s_r, it * (E * TG) + E * TG)
                for j in range(TG):
                    st, x = (a_[:, ds(it * TG + j, 1), :].rearrange("p t d -> p (t d)") for a_ in (stats, resid))
                    nc.vector.bn_stats(st, x).then_inc(s_st, 1)


def cross_attention_1(nc, resid, stats, xnT, ident, ctx_in, mask_in, Wq, Wkv, Wout, bout, B, SQ):
    SK, D = ctx_in.shape[1:]
    INNER = Wq.shape[1]
    DH = 64
    H = INNER // DH
    HP = H // 2
    KT = tiles(SK)
    NT = len(KT)
    CH = tiles(SK, BANK)
    NC = len(CH)
    QT = SQ // P
    TT = B * QT
    U = HP * 2 * QT
    PU = 2 * QT
    VH = INNER // BANK
    LAG = 3
    T_BY = ("act", "act", "dve", "dve")

    V_BY = ["act" if t % 2 and t < NT - 2 else "dve" for t in range(NT)]
    at = {s: [] for s in range(U + LAG)}
    for t in range(NT):
        at[t * 3 // NT].append((("v", 1, t), V_BY[t]))
        if t < NT - 1:
            at[U + t * LAG // (NT - 1)].append((("v", 0, t), V_BY[t]))
    before_pv = {s: [] for s in range(U + LAG)}
    for p in range(HP - 1):
        before_pv[LAG + PU * (p + 1)].append((("q", p), "dve"))
    at[U] = [(("ctxT", c), "dve") for c in range(NC)] + [(("q", HP - 1), "dve")] + at[U]
    turns = {s: [(("t", s - LAG, c), T_BY[c]) for c in range(NC)] if s >= LAG else [] for s in range(U + LAG)}
    steps = {s: before_pv[s] + turns[s] + at[s] for s in range(U + LAG)}
    per = [j for s in range(U + LAG) for j in steps[s]]
    per += [(("v", 0, NT - 1), V_BY[NT - 1]), (("y",), "dve")]
    first = [(("ctxT", c), "dve") for c in range(NC)]
    first += [(("v", 0, t), V_BY[t]) for t in range(NT)] + [(("q", p), "dve") for p in range(HP)]
    jobs = Jobs(first, per, 3)
    owner = dict(per)
    first, per = ([j for j, _ in x] for x in (first, per))
    N1, NP = len(first), len(per)
    CTX_DMAS = 2 if SK % P else 1

    with ExitStack() as ctx:
        def sb(name, shape, dt=F32, stack=ctx):
            return stack.enter_context(nc.sbuf_tensor("a1_" + name, shape, dt))

        def ps(name, shape, dt=F32, stack=ctx):
            return stack.enter_context(nc.psum_tensor("a1_" + name, shape, dt))

        def sem(name, stack=ctx):
            return stack.enter_context(nc.semaphore("a1_" + name))

        A = sb("A", [D, H, D])
        wv = [sb(f"wv{i}", [D, INNER], F16) for i in range(2)]
        w_out = sb("w_out", [P, HP, D])
        b_out = sb("b_out", [P, D])
        mask_fill = sb("mask_fill", [P, TT])

        with ExitStack() as tmp:
            wq_in = sb("wq_in", [D, INNER], stack=tmp)
            wkv_in = sb("wkv_in", [D, 2 * INNER], stack=tmp)
            wq_T = sb("wq_T", [P, HP, D], stack=tmp)
            wk_T = sb("wk_T", [P, HP, D], stack=tmp)
            mask_i = sb("mask_i", [TT, P], I32, stack=tmp)
            mask_f = sb("mask_f", [TT, P], stack=tmp)
            sbank = [ps(f"sbank{i}", [P, BANK], stack=tmp) for i in range(8)]
            s_w = sem("weights_in", tmp)
            s_t = sem("weights_turned", tmp)
            s_c = sem("turned_copied", tmp)
            s_a = sem("A_filled", tmp)
            s_v = sem("wv_parts", tmp)
            s_m = sem("mask_steps", tmp)
            s_e = sem("A_copied", tmp)
            TB = BANK // P
            block = tmp.enter_context(nc.Block())

            @block.sync
            def _(sp):
                sp.dma_start(wq_in[:, :], Wq).then_inc(s_w, 16)
                sp.dma_start(mask_i[:, :], mask_in.rearrange("b (q p) -> (b q) p", p=P)).then_inc(s_w, 16)
                sp.dma_start(wkv_in[:, :], Wkv).then_inc(s_w, 16)
                sp.dma_start(w_out[:, :, :], Wout.rearrange("(h p) d -> p h d", p=P)).then_inc(s_w, 16)
                sp.dma_start(b_out[:, :], bout.rearrange("(o d) -> o d", o=1).to_broadcast([P, D])).then_inc(s_w, 16)

            @block.tensor
            def _(pe):
                pe.wait_ge(s_w, 5 * 16)
                for w, x in enumerate((wq_in, wkv_in)):
                    for p in range(HP):
                        mm = nc.tensor.transpose(sbank[2 * w + p // TB][:, p % TB * P:(p % TB + 1) * P],
                                                 x[:, p * P:(p + 1) * P], ident[:, :])
                        if p % TB == TB - 1:
                            mm.then_inc(s_t, 1)
                pe.wait_ge(s_c, 4)
                for i in range(2):
                    half = slice(DH * i, DH * i + DH)
                    for p in range(HP):
                        mm = nc.tensor.matmul(sbank[4 + i * HP // TB + p // TB][:, p % TB * P:(p % TB + 1) * P],
                                              wq_T[half, p, :], wk_T[half, p, :], start=True, stop=True)
                        if p % TB == TB - 1:
                            mm.then_inc(s_a, 1)
                pe.wait_ge(s_m, 2)
                nc.tensor.transpose(sbank[0][:, 0:TT], mask_f[:, :], ident[0:TT, 0:TT]).then_inc(s_t, 1)

            @block.scalar
            def _(act):
                for n in range(4):
                    act.wait_ge(s_t, n + 1)
                    dst = (wq_T, wk_T)[n // 2][:, n % 2 * TB:(n % 2 + 1) * TB, :]
                    nc.scalar.activation(dst, sbank[n][:, :].rearrange("p (h d) -> p h d", h=TB), ACT.Copy,
                                         scale=(-0.125, 1.0)[n // 2]).then_inc(s_c, 1)
                for n in range(H // TB):
                    act.wait_ge(s_a, n + 1)
                    i, k = divmod(n, HP // TB)
                    nc.scalar.activation(A[:, :, :].rearrange("p (h i) d -> p i h d", i=2)[:, i, k * TB:(k + 1) * TB, :],
                                         sbank[4 + n][:, :].rearrange("p (h d) -> p h d", h=TB), ACT.Copy).then_inc(s_e, 1)

            @block.vector
            def _(dve):
                dve.wait_ge(s_w, 5 * 16)
                nc.vector.tensor_scalar(mask_f[:, :], mask_i[:, :], -1.0, 1.0, ALU.mult, ALU.add).then_inc(s_m, 1)
                dve.wait_ge(s_m, 1)
                nc.vector.tensor_scalar(mask_f[:, :], mask_f[:, :], MASK_NEG, None, ALU.mult).then_inc(s_m, 1)
                nc.vector.tensor_copy(wv[0][:, :], wkv_in[:, INNER:]).then_inc(s_v, 1)
                dve.wait_ge(s_v, 1)
                nc.vector.tensor_tensor(wv[1][:, :], wkv_in[:, INNER:], wv[0][:, :], ALU.subtract).then_inc(s_v, 1)
                dve.wait_ge(s_t, 5)
                nc.vector.tensor_copy(mask_fill[:, :], sbank[0][:, 0:TT]).then_inc(s_v, 1)
        nc.all_engine_barrier()

        ctx_rows = sb("ctx_rows", [P, NT, D])
        ctxT = [sb(f"ctxT{i}", [D, SK], F16) for i in range(2)]
        qA = [sb(f"qA{i}", [D, H, SQ], F16) for i in range(2)]
        v = sb("v", [P, NT, INNER])
        SLOTS = 4
        e = [sb(f"e{i}", [P, SK]) for i in range(SLOTS)]
        least2 = [sb(f"least2_{i}", [P, 2]) for i in range(SLOTS)]
        least = [sb(f"least{i}", [P, 1]) for i in range(SLOTS)]
        total = [sb(f"total{i}", [P, 1]) for i in range(SLOTS)]
        recip = [sb(f"recip{i}", [P, 1]) for i in range(SLOTS)]
        eT = [sb(f"eT{i}", [P, NT, SQ]) for i in range(2)]
        outT = sb("outT", [P, HP, SQ])
        yb = sb("yb", [P, QT, D])
        score = ps("score", [P, NC * BANK])
        bank = [ps(f"bank{i}", [P, BANK]) for i in range(3)]
        out_acc = ps("out_acc", [P, BANK])

        s_ctx = sem("ctx_in")
        s_pool = sem("pool_steps_begun")
        s_filled = sem("bank_filled")
        s_emptied = {"act": sem("bank_emptied_act"), "dve": sem("bank_emptied_dve")}
        s_hi = sem("hi_part_ready")
        s_score = sem("scores_ready")
        s_sub = sem("score_halves_taken")
        s_least = sem("least_ready")
        s_exp = sem("exp_done")
        s_rec = sem("recip_ready")
        s_norm = sem("weights_normalised")
        s_pv = sem("pv_done")
        s_out = sem("outT_copied")
        s_y = sem("resid_steps")
        block = ctx.enter_context(nc.Block())

        def after_jobs(eng, last, it):
            for who in ("act", "dve"):
                eng.wait_ge(s_emptied[who], jobs.emptied(who, per.index(last) + 1, it))

        HALVES = (slice(0, 2 * BANK), slice(2 * BANK, SK))

        def unit(u):
            p, r = divmod(u, PU)
            return p, r // 2, r % 2

        @block.sync
        def _(sp):
            def load(b):
                c = ctx_in[ds(b, 1), :, :]
                whole = SK // P
                sp.dma_start(ctx_rows[:, 0:whole, :],
                             c[:, 0:whole * P, :].rearrange("o (t p) d -> p (o t) d", p=P)).then_inc(s_ctx, 16)
                if SK % P:
                    sp.dma_start(ctx_rows[0:SK % P, whole, :],
                                 c[:, whole * P:SK, :].rearrange("o p d -> (o p) d")).then_inc(s_ctx, 16)

            load(0)
            with sp.Fori(0, B) as it:
                sp.wait_ge(s_filled, it * NP + N1)
                load((it + 1) % B)
            sp.wait_ge(s_ctx, 16 * CTX_DMAS * (B + 1))

        @block.tensor
        def _(pe):
            def job(n, j, it=None):
                for who, count in jobs.free(n, it):
                    pe.wait_ge(s_emptied[who], count)
                bk_ = bank[n % 3]
                if j[0] == "ctxT":
                    if it is None:
                        pe.wait_ge(s_ctx, 16 * CTX_DMAS)
                    else:
                        pe.wait_ge(s_ctx, it * (16 * CTX_DMAS) + 32 * CTX_DMAS)
                    for t in range(4 * j[1], min(4 * j[1] + 4, NT)):
                        r = KT[t][1]
                        mm = nc.tensor.transpose(bk_[:, (t % 4) * P:(t % 4) * P + r], ctx_rows[0:r, t, :],
                                                 ident[0:r, 0:r])
                elif j[0] == "q":
                    b = 0 if it is None else (it + 1) % B
                    for i in range(2):
                        mm = nc.tensor.matmul(bk_[:, i * SQ:(i + 1) * SQ], A[:, 2 * j[1] + i, :],
                                              xnT[:, ds(b * SQ, SQ)], start=True, stop=True)
                elif j[0] == "v":
                    if j[1:] == (0, 0):
                        src = first if it is None else per
                        pe.wait_ge(s_emptied["dve"], jobs.emptied("dve", src.index(("ctxT", NC - 1)) + 1, it))
                    s0, r = KT[j[2]]
                    w = slice(j[1] * BANK, (j[1] + 1) * BANK)
                    for i, (a_, b_) in enumerate(((0, 0), (0, 1), (1, 0))):
                        mm = nc.tensor.matmul(bk_[0:r, :], ctxT[a_][:, s0:s0 + r], wv[b_][:, w],
                                              start=(i == 0), stop=(i == 2))
                elif j[0] == "t":
                    u = j[1]
                    if j[2] == 0:
                        pe.wait_ge(s_norm, it * U + u + 1)
                    for t in range(4 * j[2], min(4 * j[2] + 4, NT)):
                        s0, r = KT[t]
                        mm = nc.tensor.transpose(bk_[0:r, (t % 4) * P:(t % 4 + 1) * P], e[u % SLOTS][:, s0:s0 + r],
                                                 ident[:, :])
                elif j[0] == "y":
                    pe.wait_ge(s_out, it * HP + HP)
                    pe.wait_ge(s_emptied["dve"], jobs.emptied("dve", per.index(("q", HP - 1)) + 1, it))
                    for q in range(QT):
                        for p in range(HP):
                            mm = nc.tensor.matmul(bk_[:, q * P:(q + 1) * P], outT[:, p, q * P:(q + 1) * P],
                                                  w_out[:, p, :], start=(q == 0 and p == 0), stop=(p == HP - 1),
                                                  skip_group_check=True)
                mm.then_inc(s_filled, 1)

            def scores(u, it):
                p, q, i = unit(u)
                h = 2 * p + i
                qs = slice(q * P, (q + 1) * P)
                for k, (s0, r) in enumerate(CH):
                    if k % 2 == 0:
                        pe.wait_ge(s_sub, it * (2 * U) + max(2 * u - 1 + k // 2, 0))
                    for n, (a_, b_) in enumerate(((0, 0), (0, 1), (1, 0))):
                        mm = nc.tensor.matmul(score[:, s0:s0 + r], qA[a_][:, h, qs], ctxT[b_][:, s0:s0 + r],
                                              start=(n == 0), stop=(n == 2))
                    if k % 2:
                        mm.then_inc(s_score, 1)

            def pv(p, it):
                pe.wait_ge(s_out, it * HP + p)
                after_jobs(pe, ("t", PU * p + PU - 1, NC - 1), it)
                for t, (_, r) in enumerate(KT):
                    for i in range(2):
                        w = (2 * p + i) * DH
                        mm = nc.tensor.matmul(out_acc[DH * i:DH * i + DH, 0:SQ], v[0:r, t, w:w + DH],
                                              eT[i][0:r, t, :], start=(t == 0), stop=(t == NT - 1))
                mm.then_inc(s_pv, 1)

            for n, j in enumerate(first):
                job(n, j)
            pe.wait_ge(s_emptied["dve"], jobs.emptied("dve", N1))
            with pe.Fori(0, B) as it:
                n = 0
                for s in range(U + LAG):
                    if s < U:
                        scores(s, it)
                    for j, _ in before_pv[s]:
                        job(n, j, it)
                        n += 1
                    if s > LAG and (s - LAG) % PU == 0:
                        pv((s - LAG) // PU - 1, it)
                    for j, _ in steps[s][len(before_pv[s]):]:
                        job(n, j, it)
                        n += 1
                pv(HP - 1, it)
                for j in per[n:]:
                    job(n, j, it)
                    n += 1

        def split(n, j, it):
            bk_ = bank[n % 3]
            if j[0] == "ctxT":
                s0, r = CH[j[1]]
                return [x[:, s0:s0 + r] for x in ctxT], bk_[:, 0:r]
            return [x[:, 2 * j[1]:2 * j[1] + 2, :] for x in qA], bk_[:, :].rearrange("p (h q) -> p h q", h=2)

        def whole(n, j):
            bk_ = bank[n % 3]
            if j[0] == "v":
                r = KT[j[2]][1]
                return v[0:r, j[2], j[1] * BANK:(j[1] + 1) * BANK], bk_[0:r, :]
            _, q, i = unit(j[1])
            lo, hi_ = 4 * j[2], min(4 * j[2] + 4, NT)
            r = KT[hi_ - 1][1]
            return eT[i][0:r, lo:hi_, q * P:(q + 1) * P], bk_[0:r, 0:(hi_ - lo) * P].rearrange("p (t q) -> p t q", q=P)

        def pv_before(j, it):
            return it * HP + (j[1] // PU if j[0] == "t" else 0 if j[1] else HP // 2)

        def scores_before(j, it):
            return it * (2 * U) + 2 * (PU * (j[1] + 1) if j[0] == "q" else U)

        hi_jobs = [[n for n, j in enumerate(x) if j[0] in ("ctxT", "q")] for x in (first, per)]

        @block.scalar
        def _(act):
            def part(n, j, it=None):
                if j[0] in ("ctxT", "q"):
                    act.wait_ge(s_filled, jobs.filled(n, it))
                    if it is not None:
                        act.wait_ge(s_score, scores_before(j, it))
                    (hi_, _), src = split(n, j, it)
                    nc.scalar.activation(hi_, src, ACT.Copy).then_inc(s_hi, 1)
                elif owner[j] == "act":
                    act.wait_ge(s_filled, jobs.filled(n, it))
                    if it is not None:
                        act.wait_ge(s_pv, pv_before(j, it))
                    dst, src = whole(n, j)
                    nc.scalar.activation(dst, src, ACT.Copy).then_inc(s_emptied["act"], 1)

            for n, j in enumerate(first):
                part(n, j)
            with act.Fori(0, B) as it:
                n = 0
                for s in range(U + LAG):
                    for _ in steps[s]:
                        part(n, per[n], it)
                        n += 1
                    if s < U:
                        act.wait_ge(s_least, it * U + s + 1)
                        nc.scalar.activation(e[s % SLOTS][:, :], e[s % SLOTS][:, :], ACT.Exp, bias=least[s % SLOTS][:, 0:1],
                                             scale=-1.0, accum_out=total[s % SLOTS][:, 0:1]).then_inc(s_exp, 1)
                while n < NP:
                    part(n, per[n], it)
                    n += 1

        @block.gpsimd
        def _(pool):
            with pool.Fori(0, B) as it:
                for u in range(U):
                    pool.wait_ge(s_rec, it * U + u + 1)
                    pool.sem_inc(s_pool, 1)
                    x = e[u % SLOTS][:, :]
                    nc.gpsimd.tensor_scalar(x, x, recip[u % SLOTS][:, 0:1], 1.0, ALU.mult, ALU.mult).then_inc(s_norm, 1)

        @block.vector
        def _(dve):
            def part(n, j, it=None):
                if j[0] == "y":
                    dve.wait_ge(s_filled, jobs.filled(n, it))
                    nc.vector.tensor_tensor(yb[:, :, :], bank[n % 3][:, 0:QT * D].rearrange("p (q d) -> p q d", q=QT),
                                            b_out[:, :].unsqueeze(1).to_broadcast([P, QT, D]), ALU.add).then_inc(s_emptied["dve"], 1)
                elif j[0] in ("ctxT", "q"):
                    k = hi_jobs[it is not None].index(n)
                    dve.wait_ge(s_hi, k + 1 if it is None else it * len(hi_jobs[1]) + (len(hi_jobs[0]) + k + 1))
                    (hi_, lo), src = split(n, j, it)
                    nc.vector.tensor_tensor(lo, src, hi_, ALU.subtract).then_inc(s_emptied["dve"], 1)
                elif owner[j] == "dve":
                    dve.wait_ge(s_filled, jobs.filled(n, it))
                    if it is not None:
                        dve.wait_ge(s_pv, pv_before(j, it))
                    dst, src = whole(n, j)
                    nc.vector.tensor_copy(dst, src).then_inc(s_emptied["dve"], 1)

            def reciprocal(u, it):
                dve.wait_ge(s_exp, it * U + u + 1)
                nc.vector.reciprocal(recip[u % SLOTS][:, :], total[u % SLOTS][:, :]).then_inc(s_rec, 1)

            def take(u, half, it):
                _, q, _ = unit(u)
                dve.wait_ge(s_score, it * (2 * U) + 2 * u + half + 1)
                if half == 0:
                    dve.wait_ge(s_filled, jobs.filled(per.index(("t", u - SLOTS, NC - 1)), it) if u >= SLOTS
                                else it * NP + N1)
                w = HALVES[half]
                nc.vector.tensor_scalar(e[u % SLOTS][:, w], score[:, w], mask_fill[:, ds(it * QT + q, 1)], None,
                                        ALU.add, ALU.min, accum_out=least2[u % SLOTS][:, half:half + 1]).then_inc(s_sub, 1)

            def copy_out(p, it):
                dve.wait_ge(s_pv, it * HP + p + 1)
                dve.wait_ge(s_filled, it * NP + N1)
                nc.vector.tensor_copy(outT[:, p, :], out_acc[:, 0:SQ]).then_inc(s_out, 1)

            for n, j in enumerate(first):
                part(n, j)
            with dve.Fori(0, B) as it:
                n = 0
                for s in range(U + LAG):
                    if s < U:
                        take(s, 0, it)
                    if 0 < s <= U:
                        reciprocal(s - 1, it)
                    if s < U:
                        take(s, 1, it)
                        dve.wait_ge(s_sub, it * (2 * U) + 2 * s + 2)
                        x = least2[s % SLOTS]
                        nc.vector.tensor_tensor(least[s % SLOTS][:, :], x[:, 0:1], x[:, 1:2], ALU.min).then_inc(s_least, 1)
                    for _ in before_pv[s]:
                        part(n, per[n], it)
                        n += 1
                    if s > LAG and (s - LAG) % PU == 0:
                        copy_out((s - LAG) // PU - 1, it)
                    for _ in steps[s][len(before_pv[s]):]:
                        part(n, per[n], it)
                        n += 1
                copy_out(HP - 1, it)
                while n < NP:
                    part(n, per[n], it)
                    n += 1
                dve.wait_ge(s_emptied["dve"], jobs.emptied("dve", per.index(("y",)) + 1, it))
                x = resid[:, ds(it * QT, QT), :]
                nc.vector.tensor_tensor(x, x, yb[:, :, :], ALU.add).then_inc(s_y, 1)
                dve.wait_ge(s_y, it * (1 + QT) + 1)
                for q in range(QT):
                    st, x = (a_[:, ds(it * QT + q, 1), :].rearrange("p t d -> p (t d)") for a_ in (stats, resid))
                    nc.vector.bn_stats(st, x).then_inc(s_y, 1)


def moe_ffn_1(nc, resid, xnT, ident, Wr, Wg, Wu, Wd, Sg, Su, Sd, TT):
    D, E = Wr.shape
    F = Wg.shape[2]
    NPAIR = E * F // P
    N = NPAIR + 1
    TG = BANK // P
    PASSES = TT // TG
    TOP = 2
    assert 2 * F == P and Sg.shape[1] == P and TG * 2 * E == P and TT * E <= BANK
    with ExitStack() as ctx:
        def sb(name, shape, dt=F32):
            return ctx.enter_context(nc.sbuf_tensor("f1_" + name, shape, dt))

        def ps(name):
            return ctx.enter_context(nc.psum_tensor("f1_" + name, [P, BANK], F32))

        def sem(name):
            return ctx.enter_context(nc.semaphore("f1_" + name))

        w_in = sb("w_in", [D, 2, N, P])
        w_gu = [sb(f"w_gu{i}", [D, 2, N, P], F16) for i in range(2)]
        wr_in = sb("wr_in", [D, E])
        w_r = [sb(f"w_r{i}", [D, E], F16) for i in range(2)]
        w_d = sb("w_d", [P, N, D])
        x16 = [sb(f"x16_{i}", [D, TT * P], F16) for i in range(2)]
        ident16 = sb("ident16", [P, P], F16)
        select = sb("select", [P, TG, E, F], F16)
        order = sb("order", [P, E])
        prob = sb("prob", [P, TT, E])
        left = sb("left", [P, TT, E])
        mark = sb("mark", [P, TT, E])
        pick = sb("pick", [P, TT, E])
        cw = sb("cw", [P, TT, E])
        best = sb("best", [P, TT])
        cw16 = sb("cw16", [P, TT, 2, E], F16)
        cwT = sb("cwT", [P, PASSES, P], F16)
        silu = [sb(f"silu{i}", [P, BANK]) for i in range(2)]
        hid = [sb(f"hid{i}", [P, BANK]) for i in range(2)]
        yT = sb("yT", [D, BANK])
        gbank = [ps(f"gbank{i}") for i in range(2)]
        ubank = [ps(f"ubank{i}") for i in range(2)]
        cbank = [ps(f"cbank{i}") for i in range(2)]
        ybank = ps("ybank")
        tbank = ps("tbank")
        s_w = sem("weights_in")
        s_split = sem("weight_parts")
        s_id = sem("constants_set")
        s_xh = sem("x_hi_ready")
        s_xl = sem("x_lo_ready")
        s_logit = sem("logits_filled")
        s_route = sem("routing_steps")
        s_exp = sem("exp_done")
        s_cwt = sem("cw_turned")
        s_cwc = sem("cwT_written")
        s_fill = sem("pair_filled")
        s_silu = sem("silu_ready")
        s_gate = sem("gated")
        s_hid = sem("hidden_ready")
        s_down = sem("down_added")
        s_yt = sem("yT_copied")
        s_turn = sem("y_turned")
        s_r = sem("resid_added")
        block = ctx.enter_context(nc.Block())
        LOADS = 7

        @block.sync
        def _(sp):
            sp.dma_start(wr_in[:, :], Wr).then_inc(s_w, 16)
            for i, (w, s) in enumerate(((Wg, Sg), (Wu, Su))):
                sp.dma_start(w_in[:, i, 0:NPAIR, :].rearrange("d n (i f) -> d (n i) f", f=F),
                             w.rearrange("e d f -> d e f")).then_inc(s_w, 16)
                sp.dma_start(w_in[:, i, NPAIR, :], s).then_inc(s_w, 16)
            sp.dma_start(w_d[:, 0:NPAIR, :], Wd.rearrange("(n i) f d -> (i f) n d", i=2)).then_inc(s_w, 16)
            sp.dma_start(w_d[:, NPAIR, :], Sd).then_inc(s_w, 16)
            sp.wait_ge(s_w, 16 * LOADS)

        @block.gpsimd
        def _(pool):
            for e in range(E):
                nc.gpsimd.memset(order[:, e:e + 1], float(E - e)).then_inc(s_id, 1)
            nc.gpsimd.tensor_scalar(ident16[:, :], ident[:, :], 1.0, 1.0, ALU.mult, ALU.mult).then_inc(s_id, 1)
            rows = ident[:, :].rearrange("p (j s e) -> p j s e", j=TG, s=2)
            for j in range(TG):
                hi_, lo = (rows[:, j, s, :].unsqueeze(2).to_broadcast([P, E, F]) for s in range(2))
                nc.gpsimd.tensor_tensor(select[:, j, :, :], hi_, lo, ALU.add).then_inc(s_id, 1)

        def fill_free(eng, n, it):
            eng.wait_ge(s_hid, it * N + max(n - 1, 0))

        @block.tensor
        def _(pe):
            pe.wait_ge(s_split, 2)
            with pe.Fori(0, PASSES) as it:
                pe.wait_ge(s_xl, it + 1)
                for j in range(TG):
                    t = it * TG + j
                    for i, (a_, b_) in enumerate(((0, 0), (0, 1), (1, 0))):
                        mm = nc.tensor.matmul(gbank[0][:, ds(t * E, E)], x16[a_][:, ds(t * P, P)], w_r[b_][:, :],
                                              start=(i == 0), stop=(i == 2))
                mm.then_inc(s_logit, 1)
            pe.wait_ge(s_id, E + 1 + TG)
            pe.wait_ge(s_split, 6)
            turned = cbank[0][:, :].bitcast(F16)
            for i in range(PASSES):
                mm = nc.tensor.transpose(turned[:, i * P:(i + 1) * P],
                                         cw16[:, i * TG:(i + 1) * TG, :, :].rearrange("p t s e -> p (t s e)"),
                                         ident16[:, :])
            mm.then_inc(s_cwt, 1)
            pe.wait_ge(s_w, 16 * LOADS)
            pe.wait_ge(s_cwc, 1)

            def down(n, it):
                pe.wait_ge(s_hid, it * N + n + 1)
                if n == 0:
                    pe.wait_ge(s_yt, it)
                nc.tensor.matmul(ybank[:, :], w_d[:, n, :], hid[n % 2][:, :], start=(n == 0),
                                 stop=(n == N - 1)).then_inc(s_down, 1)

            with pe.Fori(0, PASSES) as it:
                for n in range(N):
                    fill_free(pe, n, it)
                    for k, dst in enumerate((gbank[n % 2], ubank[n % 2])):
                        for i, (a_, b_) in enumerate(((0, 0), (0, 1), (1, 0))):
                            mm = nc.tensor.matmul(dst[:, :], w_gu[a_][:, k, n, :], x16[b_][:, ds(it * BANK, BANK)],
                                                  start=(i == 0), stop=(i == 2))
                    if n < NPAIR:
                        for j in range(TG):
                            mm = nc.tensor.matmul(cbank[n % 2][:, j * P:(j + 1) * P],
                                                  select[:, j, 2 * n:2 * n + 2, :].rearrange("p e f -> p (e f)"),
                                                  cwT[:, ds(it, 1), :].rearrange("p t d -> p (t d)"), start=True, stop=True)
                    mm.then_inc(s_fill, 1)
                    if n:
                        down(n - 1, it)
                down(N - 1, it)
                pe.wait_ge(s_yt, it + 1)
                pe.wait_ge(s_r, it)
                for j in range(TG):
                    mm = nc.tensor.transpose(tbank[:, j * P:(j + 1) * P], yT[:, j * P:(j + 1) * P], ident[:, :])
                mm.then_inc(s_turn, 1)

        @block.scalar
        def _(act):
            with act.Fori(0, PASSES) as it:
                w = ds(it * BANK, BANK)
                nc.scalar.activation(x16[0][:, w], xnT[:, w], ACT.Copy).then_inc(s_xh, 1)
            act.wait_ge(s_route, 2)
            nc.scalar.activation(prob[:, :, :], prob[:, :, :], ACT.Exp).then_inc(s_exp, 1)
            with act.Fori(0, PASSES) as it:
                for n in range(N):
                    act.wait_ge(s_fill, it * N + n + 1)
                    fill_free(act, n, it)
                    nc.scalar.activation(silu[n % 2][:, :], gbank[n % 2][:, :], ACT.Silu).then_inc(s_silu, 1)
                act.wait_ge(s_down, it * N + N)
                act.wait_ge(s_turn, it)
                nc.scalar.activation(yT[:, :], ybank[:, :], ACT.Copy).then_inc(s_yt, 1)

        @block.vector
        def _(dve):
            tt = nc.vector.tensor_tensor
            dve.wait_ge(s_w, 16 * LOADS)
            nc.vector.tensor_copy(w_r[0][:, :], wr_in[:, :]).then_inc(s_split, 1)
            dve.wait_ge(s_split, 1)
            tt(w_r[1][:, :], wr_in[:, :], w_r[0][:, :], ALU.subtract).then_inc(s_split, 1)
            with dve.Fori(0, PASSES) as it:
                w = ds(it * BANK, BANK)
                dve.wait_ge(s_xh, it + 1)
                tt(x16[1][:, w], xnT[:, w], x16[0][:, w], ALU.subtract).then_inc(s_xl, 1)
            nc.vector.tensor_copy(w_gu[0][:, :, :, :], w_in[:, :, :, :]).then_inc(s_split, 1)
            dve.wait_ge(s_split, 3)
            tt(w_gu[1][:, :, :, :], w_in[:, :, :, :], w_gu[0][:, :, :, :], ALU.subtract).then_inc(s_split, 1)

            def each(x):
                return x[:, :].unsqueeze(2).to_broadcast([P, TT, E])

            def reduce(dst, src, op):
                return nc.vector.tensor_reduce(dst[:, :], src[:, :, :], AX.X, op)

            c = Steps()
            dve.wait_ge(s_logit, PASSES)
            logits = gbank[0][:, 0:TT * E].rearrange("p (t e) -> p t e", e=E)
            nc.vector.tensor_reduce(best[:, :], logits, AX.X, ALU.max).then_inc(s_route, 1)
            dve.wait_ge(s_route, c.up())
            tt(prob[:, :, :], logits, each(best), ALU.subtract).then_inc(s_route, 1)
            dve.wait_ge(s_route, c.up())
            dve.wait_ge(s_exp, 1)
            reduce(best, prob, ALU.add).then_inc(s_route, 1)
            dve.wait_ge(s_route, c.up())
            nc.vector.reciprocal(best[:, :], best[:, :]).then_inc(s_route, 1)
            dve.wait_ge(s_route, c.up())
            tt(prob[:, :, :], prob[:, :, :], each(best), ALU.mult).then_inc(s_route, 1)
            dve.wait_ge(s_route, c.up())
            dve.wait_ge(s_id, E)
            lower_first = order[:, :].unsqueeze(1).to_broadcast([P, TT, E])
            for k in range(TOP):
                src = left if k else prob
                reduce(best, src, ALU.max).then_inc(s_route, 1)
                dve.wait_ge(s_route, c.up())
                tt(mark[:, :, :], src[:, :, :], each(best), ALU.is_equal).then_inc(s_route, 1)
                dve.wait_ge(s_route, c.up())
                tt(mark[:, :, :], mark[:, :, :], lower_first, ALU.mult).then_inc(s_route, 1)
                dve.wait_ge(s_route, c.up())
                reduce(best, mark, ALU.max).then_inc(s_route, 1)
                dve.wait_ge(s_route, c.up())
                tt(pick[:, :, :], lower_first, each(best), ALU.is_equal).then_inc(s_route, 1)
                dve.wait_ge(s_route, c.up())
                if k == 0:
                    tt(cw[:, :, :], prob[:, :, :], pick[:, :, :], ALU.mult).then_inc(s_route, 1)
                    dve.wait_ge(s_route, c.up())
                    nc.vector.scalar_tensor_tensor(out=left[:, :, :], in0=pick[:, :, :], scalar=-2.0,
                                                   in1=prob[:, :, :], op0=ALU.mult, op1=ALU.add).then_inc(s_route, 1)
                    dve.wait_ge(s_route, c.up())
                else:
                    tt(mark[:, :, :], prob[:, :, :], pick[:, :, :], ALU.mult).then_inc(s_route, 1)
                    dve.wait_ge(s_route, c.up())
                    tt(cw[:, :, :], cw[:, :, :], mark[:, :, :], ALU.add).then_inc(s_route, 1)
                    dve.wait_ge(s_route, c.up())
            nc.vector.tensor_copy(cw16[:, :, 0, :], cw[:, :, :]).then_inc(s_split, 1)
            dve.wait_ge(s_split, 5)
            tt(cw16[:, :, 1, :], cw[:, :, :], cw16[:, :, 0, :], ALU.subtract).then_inc(s_split, 1)
            dve.wait_ge(s_cwt, 1)
            nc.vector.tensor_copy(cwT[:, :, :], cbank[0][:, :].bitcast(F16)[:, 0:PASSES * P].rearrange("p (i d) -> p i d", d=P)).then_inc(s_cwc, 1)
            with dve.Fori(0, PASSES) as it:
                for n in range(N):
                    dve.wait_ge(s_silu, it * N + n + 1)
                    dve.wait_ge(s_down, it * N + max(n - 1, 0))
                    gated = tt(hid[n % 2][:, :], ubank[n % 2][:, :], silu[n % 2][:, :], ALU.mult)
                    if n == NPAIR:
                        gated.then_inc(s_hid, 1)
                    else:
                        gated.then_inc(s_gate, 1)
                        dve.wait_ge(s_gate, it * NPAIR + n + 1)
                        tt(hid[n % 2][:, :], cbank[n % 2][:, :], hid[n % 2][:, :], ALU.mult).then_inc(s_hid, 1)
                dve.wait_ge(s_turn, it + 1)
                x = resid[:, ds(it * TG, TG), :]
                tt(x, tbank[:, :].rearrange("p (t d) -> p t d", d=D), x, ALU.add).then_inc(s_r, 1)


def program(nc, a, out):
    B, SQ, D = a["x"].shape
    TT = B * SQ // P
    with ExitStack() as ctx:
        resid = ctx.enter_context(nc.sbuf_tensor("resid", [P, TT, D], F32))
        xnT = ctx.enter_context(nc.sbuf_tensor("xnT", [D, B * SQ], F32))
        stats = ctx.enter_context(nc.sbuf_tensor("stats", [P, TT, 6], F32))
        ident = ctx.enter_context(nc.sbuf_tensor("ident", [P, P], F32))
        s_in = ctx.enter_context(nc.semaphore("x_in"))
        s_id = ctx.enter_context(nc.semaphore("ident_steps"))
        s_out = ctx.enter_context(nc.semaphore("out_written"))
        x_tiles = a["x"].rearrange("b (q p) d -> p (b q) d", p=P)
        out_tiles = out.rearrange("b (q p) d -> p (b q) d", p=P)

        with nc.Block() as block:
            @block.sync
            def _(sp):
                sp.dma_start(resid[:, :, :], x_tiles).then_inc(s_in, 16)
                sp.wait_ge(s_in, 16)

            @block.gpsimd
            def _(pool):
                nc.gpsimd.memset(ident[:, :], 0.0).then_inc(s_id, 1)
                pool.wait_ge(s_id, 1)
                nc.gpsimd.affine_select(out=ident[:, :], in_=ident[:, :], compare_op=ALU.not_equal, fill=1.0,
                                        base=0, pattern=[[-1, P]], channel_multiplier=1).then_inc(s_id, 1)
                pool.wait_ge(s_id, 2)
        nc.all_engine_barrier()
        layernorm(nc, resid, xnT, ident, stats, TT, "ln0", first=True)
        nc.all_engine_barrier()
        cross_attention_0(nc, resid, stats, xnT, ident, a["ctx_1024"], a["mask_BxSxS2_ik1"],
                          *(a["L0_xattn_" + n] for n in ("Wq", "bq", "Wk", "bk", "Wv", "bv", "Wo", "bo")), B, SQ)
        nc.all_engine_barrier()
        layernorm(nc, resid, xnT, ident, stats, TT, "ln1")
        nc.all_engine_barrier()
        moe_ffn_0(nc, resid, stats, xnT, ident, *(a["L0_ffn_" + n] for n in (
            "gate_w", "gate_b", "dp_w1", "dp_b1", "dp_w2", "dp_b2", "ew1", "eb1", "ew2", "eb2")), TT)
        nc.all_engine_barrier()
        layernorm(nc, resid, xnT, ident, stats, TT, "ln2")
        nc.all_engine_barrier()
        cross_attention_1(nc, resid, stats, xnT, ident, a["ctx_1024"], a["mask_BxS_ik0"],
                          *(a["L1_xattn_" + n] for n in ("Wq", "Wkv", "Wout", "bout")), B, SQ)
        nc.all_engine_barrier()
        layernorm(nc, resid, xnT, ident, stats, TT, "ln3")
        nc.all_engine_barrier()
        moe_ffn_1(nc, resid, xnT, ident, *(a["L1_ffn_" + n] for n in ("Wr", "Wg", "Wu", "Wd", "Sg", "Su", "Sd")), TT)
        nc.all_engine_barrier()
        with nc.Block() as block:
            @block.sync
            def _(sp):
                sp.dma_start(out_tiles, resid[:, :, :]).then_inc(s_out, 16)
                sp.wait_ge(s_out, 16)


_INS = ("x", "ctx_1024", "mask_BxSxS2_ik1", "mask_BxS_ik0",
        "L0_xattn_Wq", "L0_xattn_bq", "L0_xattn_Wk", "L0_xattn_bk", "L0_xattn_Wv", "L0_xattn_bv",
        "L0_xattn_Wo", "L0_xattn_bo", "L0_ffn_gate_w", "L0_ffn_gate_b", "L0_ffn_dp_w1", "L0_ffn_dp_b1",
        "L0_ffn_dp_w2", "L0_ffn_dp_b2", "L0_ffn_ew1", "L0_ffn_eb1", "L0_ffn_ew2", "L0_ffn_eb2",
        "L1_xattn_Wq", "L1_xattn_Wkv", "L1_xattn_Wout", "L1_xattn_bout", "L1_ffn_Wr", "L1_ffn_Wg",
        "L1_ffn_Wu", "L1_ffn_Wd", "L1_ffn_Sg", "L1_ffn_Su", "L1_ffn_Sd")


def kernel(**inputs):
    import numpy as _np
    import concourse.bacc as _bacc
    from concourse import mybir as _mybir
    from concourse.bass_utils import run_bass_kernel_spmd as _run

    nc = _bacc.Bacc("TRN2", target_bir_lowering=False, num_devices=1)
    arrays, a = {}, {}
    for name in _INS:
        arr = _np.ascontiguousarray(inputs[name])
        arrays["in_" + name + "_dram"] = arr
        a[name] = nc.dram_tensor("in_" + name + "_dram", arr.shape, _mybir.dt.from_np(arr.dtype),
                                 kind="ExternalInput").ap()
    out = nc.dram_tensor("out_0_dram", inputs["x"].shape, _mybir.dt.float32, kind="ExternalOutput").ap()
    program(nc, a, out)
    return _run(nc, [arrays], core_ids=[0]).results[0]["out_0_dram"]
```

```python
from contextlib import ExitStack

import concourse.bass as bass
from concourse import mybir
from concourse.bass import ds

F32 = mybir.dt.float32
F16 = mybir.dt.float16
BF16 = mybir.dt.bfloat16
I32 = mybir.dt.int32
ALU = mybir.AluOpType
ACT = mybir.ActivationFunctionType
AX = mybir.AxisListType
P = 128
BANK = 512

MASK_FILL = -1e30
MASK_NEG = 1e6
LN_EPS = 1e-5


class Steps:

    def __init__(self):
        self.n = 0

    def up(self):
        self.n += 1
        return self.n


class Jobs:

    def __init__(self, first, per, banks):
        self.lists, self.banks = (first, per), banks

    def filled(self, n, it=None):
        return n + 1 if it is None else it * len(self.lists[1]) + (len(self.lists[0]) + n + 1)

    def emptied(self, who, n, it=None):
        first, per = ([w == who for _, w in x] for x in self.lists)
        return sum(first[:n]) if it is None else it * sum(per) + (sum(first) + sum(per[:n]))

    def free(self, n, it=None):
        if n >= self.banks:
            who = self.lists[it is not None][n - self.banks][1]
            return [(who, self.emptied(who, n - self.banks + 1, it))]
        if it is None:
            return []
        (who,) = {w for x in self.lists for _, w in x[-self.banks:]}
        later = min((len(x) - 1 - n) % self.banks for x in self.lists)
        return [(who, self.emptied(who, 0, it) - later)]



def tiles(n, size=P):
    return [(a, min(size, n - a)) for a in range(0, n, size)]


def layernorm(nc, resid, xnT, ident, stats, TT, tag, first=False):
    G = 4
    K = min(4, TT // G)
    with ExitStack() as ctx:
        mean, var, tmp, rstd, shift = (ctx.enter_context(nc.sbuf_tensor(f"{tag}_{n}", [P, TT], F32))
                                       for n in ("mean", "var", "tmp", "rstd", "shift"))
        xn = [ctx.enter_context(nc.sbuf_tensor(f"{tag}_xn{i}", [P, G, P], F32)) for i in range(K)]
        turned = [ctx.enter_context(nc.psum_tensor(f"{tag}_turned{i}", [P, BANK], F32)) for i in range(K)]
        s_stats = ctx.enter_context(nc.semaphore(f"{tag}_stats_done"))
        s_var = ctx.enter_context(nc.semaphore(f"{tag}_var_done"))
        s_std = ctx.enter_context(nc.semaphore(f"{tag}_std_done"))
        s_xd = ctx.enter_context(nc.semaphore(f"{tag}_xn_tile_by_dve"))
        s_xa = ctx.enter_context(nc.semaphore(f"{tag}_xn_tiles_by_act"))
        s_turned = ctx.enter_context(nc.semaphore(f"{tag}_xn_free"))
        s_out = ctx.enter_context(nc.semaphore(f"{tag}_banks_free"))
        block = ctx.enter_context(nc.Block())

        def tile(x, t):
            return x[:, ds(t, 1), :].rearrange("p t d -> p (t d)")

        @block.gpsimd
        def _(pool):
            pool.sem_inc(s_turned, K)
            pool.sem_inc(s_out, K)

        @block.vector
        def _(dve):
            if first:
                with dve.Fori(0, TT // 8) as i:
                    for j in range(8):
                        nc.vector.bn_stats(tile(stats, i * 8 + j), tile(resid, i * 8 + j)).then_inc(s_stats, 1)
                dve.wait_ge(s_stats, TT)
            c = Steps()
            nc.vector.tensor_tensor(mean[:, :], stats[:, :, 1], stats[:, :, 4], ALU.add).then_inc(s_var, 1)
            nc.vector.tensor_tensor(var[:, :], stats[:, :, 2], stats[:, :, 5], ALU.add).then_inc(s_var, 1)
            c.up()
            dve.wait_ge(s_var, c.up())
            nc.vector.tensor_scalar(mean[:, :], mean[:, :], 0.5, None, ALU.mult).then_inc(s_var, 1)
            nc.vector.tensor_scalar(var[:, :], var[:, :], 1.0 / P, LN_EPS, ALU.mult, ALU.add).then_inc(s_var, 1)
            c.up()
            dve.wait_ge(s_var, c.up())
            nc.vector.tensor_tensor(tmp[:, :], stats[:, :, 1], mean[:, :], ALU.subtract).then_inc(s_var, 1)
            dve.wait_ge(s_var, c.up())
            nc.vector.tensor_tensor(tmp[:, :], tmp[:, :], tmp[:, :], ALU.mult).then_inc(s_var, 1)
            dve.wait_ge(s_var, c.up())
            nc.vector.tensor_tensor(var[:, :], var[:, :], tmp[:, :], ALU.add).then_inc(s_var, 1)
            dve.wait_ge(s_var, c.up())
            dve.wait_ge(s_std, 1)
            nc.vector.reciprocal(rstd[:, :], tmp[:, :]).then_inc(s_var, 1)
            dve.wait_ge(s_var, c.up())
            nc.vector.scalar_tensor_tensor(out=shift[:, :], in0=mean[:, :], scalar=-1.0, in1=rstd[:, :],
                                           op0=ALU.mult, op1=ALU.mult).then_inc(s_var, 1)
            with dve.Fori(0, TT // G // K) as i:
                for k in range(K):
                    dve.wait_ge(s_turned, i * K + (k + 1))
                    t = i * (K * G) + k * G
                    nc.vector.tensor_scalar(xn[k][:, 0, :], tile(resid, t), mean[:, ds(t, 1)], rstd[:, ds(t, 1)],
                                            ALU.subtract, ALU.mult).then_inc(s_xd, 1)
                for k in range(K):
                    dve.wait_ge(s_turned, i * K + (K + k + 1))
                    nc.vector.tensor_copy(xnT[:, ds((i * K + k) * BANK, BANK)], turned[k][:, :]).then_inc(s_out, 1)

        @block.tensor
        def _(pe):
            with pe.Fori(0, TT // G // K) as i:
                for k in range(K):
                    pe.wait_ge(s_xd, i * K + (k + 1))
                    pe.wait_ge(s_xa, i * (K * (G - 1)) + (k + 1) * (G - 1))
                    pe.wait_ge(s_out, i * K + (k + 1))
                    for j in range(G):
                        mm = nc.tensor.transpose(turned[k][:, j * P:(j + 1) * P], xn[k][:, j, :], ident[:, :])
                    mm.then_inc(s_turned, 1)

        @block.scalar
        def _(act):
            act.wait_ge(s_var, 7)
            nc.scalar.activation(tmp[:, :], var[:, :], ACT.Sqrt).then_inc(s_std, 1)
            act.wait_ge(s_var, 9)
            with act.Fori(0, TT // G // K) as i:
                for k in range(K):
                    act.wait_ge(s_turned, i * K + (k + 1))
                    for j in range(1, G):
                        t = i * (K * G) + (k * G + j)
                        nc.scalar.activation(xn[k][:, j, :], tile(resid, t), ACT.Identity, bias=shift[:, ds(t, 1)],
                                             scale=rstd[:, ds(t, 1)]).then_inc(s_xa, 1)


def cross_attention_0(nc, resid, stats, xnT, ident, ctx_in, mask_in, Wq, bq, Wk, bk, Wv, bv, Wo, bo, B, SQ):
    SK = ctx_in.shape[1]
    H, D, DK = Wq.shape
    G, HG, CP = 4, 4, 4
    KT = tiles(SK)
    NT = len(KT)
    CH = tiles(SK, BANK)
    U = G * NT
    QT = SQ // P
    ROW = HG * CP * DK
    assert ROW == P and H == G * HG and H * DK == P

    at = {u: [] for u in range(U)}
    at[1].append(("mask", 1))
    at[2].append(("v", 1))
    at[5].append(("mask", 2))
    at[6].append(("v", 2))
    at[9].append(("mask", 3))
    at[10].append(("v", 3))
    for n, u in enumerate((3, 4, 7, 8, 11)):
        at[u].append(("k", 3, n - 1) if n else ("q", 3))
    for c in range(4):
        at[NT + c].append(("ctxT", c))
    for g in range(3):
        at[NT * (g + 1) + 4].append(("q", g))
        for c in range(4):
            at[NT * (g + 1) + 5 + c].append(("k", g, c))
    at[U - 4].append(("mask", 0))
    at[U - 3].append(("v", 0))
    per = [(j, "dve") for u in range(U) for j in at[u]] + [(("y",), "dve")]
    first = [(("ctxT", c), "dve") for c in range(4)]
    for g in range(3):
        first += [(("q", g), "dve")] + [(("k", g, c), "dve") for c in range(4)]
    first += [(("mask", 0), "dve"), (("v", 0), "dve")]
    jobs = Jobs(first, per, 2)
    is_next = {j: u >= NT for u in range(U) for j in at[u]}

    with ExitStack() as ctx:
        def sb(name, shape, dt=F32):
            return ctx.enter_context(nc.sbuf_tensor("a0_" + name, shape, dt))

        def ps(name, shape, dt=F32):
            return ctx.enter_context(nc.psum_tensor("a0_" + name, shape, dt))

        def sem(name):
            return ctx.enter_context(nc.semaphore("a0_" + name))

        w_in = sb("w_in", [D, 3, H, DK])
        wq_rows = sb("wq_rows", [D, G, HG, CP, DK])
        wk_rows = sb("wk_rows", [D, G, HG, CP, DK])
        wo_in = sb("wo_in", [P, P])
        wo_wide = sb("wo_wide", [P, G, HG, 32])
        wo_T = sb("wo_T", [P, G, P])
        b_row = sb("b_row", [1, 2, P])
        HEAD = 2 * G + 2
        rows = sb("rows", [1, HEAD + HG, HG, CP, DK])
        cols = sb("cols", [P, HEAD + HG])
        lo_bias = sb("lo_bias", [P, 2 * G])
        bv_all = sb("bv_all", [P, P])
        bo_all = sb("bo_all", [P, P])
        ident16 = sb("ident16", [P, P], BF16)
        ctx_rows = sb("ctx_rows", [P, NT, D])
        ctxT = sb("ctxT", [D, SK])
        mask_i = sb("mask_i", [P, QT, SK], I32)
        fill = sb("fill", [P, QT, SK], BF16)
        fillT = sb("fillT", [P, NT, SQ], BF16)
        hi = [sb(f"hi{i}", [P, BANK], F16) for i in range(3)]
        q_mix = sb("q_mix", [P, SQ], F16)
        k_op = [sb(f"k_op{g}", [P, SK], F16) for g in range(G)]
        q_op = [sb(f"q_op{g}", [P, HG, SQ], F16) for g in range(G)]
        v = sb("v", [P, NT, P])
        SLOTS, SCORES, LAG, PV_LAG = 4, 5, 2, 3
        K_BY_DVE = (1,)
        AHEAD = 2
        neg_max = [sb(f"neg_max{i}", [P, HG]) for i in range(SLOTS)]
        total = [sb(f"total{i}", [P, HG]) for i in range(SLOTS)]
        recip = [sb(f"recip{i}", [P, HG]) for i in range(SLOTS)]
        e = [sb(f"e{i}", [P, HG, SQ]) for i in range(SLOTS)]
        vn = [sb(f"vn{i}", [P, HG, 32]) for i in range(SLOTS)]
        attn = sb("attn", [P, G, SQ])
        yb = sb("yb", [P, QT, P])

        score = [ps(f"score{i}", [P, HG // 2, SQ]) for i in range(SCORES)]
        attn_acc = ps("attn_acc", [P, 2, SQ])
        bank = [ps(f"bank{i}", [P, BANK]) for i in range(2)]

        s_w = sem("weights_in")
        s_zero = sem("zeros_set")
        s_pool = sem("pool_steps_begun")
        s_id = sem("ident16_set")
        s_const = sem("const_steps")
        s_cpe = sem("const_products")
        s_rec0 = sem("const_parts")
        s_ctx = sem("ctx_in")
        s_mask = sem("mask_in")
        s_fill = sem("fill_ready")
        s_filled = sem("bank_filled")
        s_emptied = sem("bank_emptied")
        s_hi = sem("hi_part_ready")
        s_hi_dve = sem("hi_part_ready_dve")
        s_mix = sem("q_mix_ready")
        s_qop = sem("q_op_rows_written")
        s_score = sem("scores_ready")
        s_max = sem("neg_max_ready")
        s_exp = sem("exp_done")
        s_rec = sem("recip_ready")
        s_vn = sem("vn_ready")
        s_pv = sem("pv_slots_free")
        s_att = sem("attn_copied")
        s_y = sem("resid_steps")
        block = ctx.enter_context(nc.Block())

        N1, NP = len(first), len(per)
        PIECES = QT * len(CH)
        FILL_AT = [u for u in range(2 * NT - 5, U, 2) if u % NT > 8 or u % NT < 5][:PIECES]
        assert U % SLOTS == 0
        names = [[n for n, _ in x] for x in (first, per)]
        CTX_DMAS = 2 if SK % P else 1

        def after_job(job, it):
            return jobs.emptied("dve", names[1].index(job) + 1, it)

        def group_free(job, it):
            return it * (2 * U) + (2 * NT * (job[1] + 1) if job[1] < G - 1 else 0)

        @block.sync
        def _(sp):
            for i, w in enumerate((Wq, Wk, Wv)):
                sp.dma_start(w_in[:, i, :, :], w.rearrange("h d k -> d h k")).then_inc(s_w, 16)
            for i, b in enumerate((bk, bq)):
                sp.dma_start(b_row[:, i, :], b.rearrange("(o h) k -> o (h k)", o=1)).then_inc(s_w, 16)
            sp.dma_start(wo_in[:, :], Wo).then_inc(s_w, 16)
            sp.dma_start(bv_all[:, :], bv.rearrange("(o h) k -> o (h k)", o=1).to_broadcast([P, P])).then_inc(s_w, 16)
            sp.dma_start(bo_all[:, :], bo.rearrange("(o d) -> o d", o=1).to_broadcast([P, P])).then_inc(s_w, 16)

            def load_ctx(b):
                c = ctx_in[ds(b, 1), :, :]
                whole = SK // P
                sp.dma_start(ctx_rows[:, 0:whole, :],
                             c[:, 0:whole * P, :].rearrange("o (t p) d -> p (o t) d", p=P)).then_inc(s_ctx, 16)
                if SK % P:
                    sp.dma_start(ctx_rows[0:SK % P, whole, :],
                                 c[:, whole * P:SK, :].rearrange("o p d -> (o p) d")).then_inc(s_ctx, 16)

            def load_mask(b):
                m = mask_in[ds(b, 1), :, :]
                sp.dma_start(mask_i[:, :, :], m.rearrange("o (t p) s -> p (o t) s", p=P)).then_inc(s_mask, 16)

            load_ctx(0)
            load_mask(0)
            with sp.Fori(0, B) as it:
                sp.wait_ge(s_filled, it * NP + N1)
                load_ctx((it + 1) % B)
                sp.wait_ge(s_fill, (it + 1) * PIECES)
                load_mask((it + 1) % B)
            sp.wait_ge(s_ctx, 16 * CTX_DMAS * (B + 1))
            sp.wait_ge(s_mask, 16 * (B + 1))

        @block.gpsimd
        def _(pool):
            pool.sem_inc(s_pv, SLOTS)
            nc.gpsimd.memset(wo_wide[:, :, :, :], 0.0).then_inc(s_zero, 1)
            for x in vn:
                nc.gpsimd.memset(x[:, :, :], 0.0).then_inc(s_zero, 1)
            nc.gpsimd.tensor_scalar(ident16[:, :], ident[:, :], 1.0, 1.0, ALU.mult, ALU.mult).then_inc(s_id, 1)

            def fill_piece(k, before):
                if k == 0:
                    pool.wait_ge(s_mask, 16 * before + 16)
                    pool.sem_inc(s_pool, 1)
                q, (s0, r) = k // len(CH), CH[k % len(CH)]
                nc.gpsimd.tensor_scalar(fill[:, q, s0:s0 + r], mask_i[:, q, s0:s0 + r], 0.0, MASK_FILL,
                                        ALU.is_equal, ALU.mult).then_inc(s_fill, 1)

            def place_q(g, before, it=None):
                pool.wait_ge(s_mix, before + 1)
                if it is not None:
                    pool.wait_ge(s_score, group_free(("q", g), it))
                    pool.sem_inc(s_pool, 1)
                for i in range(HG):
                    nc.gpsimd.tensor_scalar(q_op[g][:, i, :], q_mix[:, :], cols[:, HEAD + i:HEAD + i + 1], 1.0,
                                            ALU.mult, ALU.mult).then_inc(s_qop, 1)

            def scaled_v(u, it):
                g, t = divmod(u, NT)
                r, slot = KT[t][1], u % SLOTS
                if g == 0 and t % 4 == 0:
                    pool.wait_ge(s_emptied, after_job(("v", t // 4), it) if u else it * NP + (N1 - 1))
                pool.wait_ge(s_pv, it * U + u + 1)
                pool.wait_ge(s_rec, it * U + u + 1)
                pool.sem_inc(s_pool, 1)
                w = HG * DK
                nc.gpsimd.tensor_tensor(vn[slot][0:r, :, 0:DK],
                                        v[0:r, t, g * w:(g + 1) * w].rearrange("p (h k) -> p h k", h=HG),
                                        recip[slot][0:r, :].unsqueeze(2).to_broadcast([r, HG, DK]),
                                        ALU.mult).then_inc(s_vn, 1)

            pool.wait_ge(s_zero, 1 + SLOTS)
            for k in range(PIECES // 2):
                fill_piece(k, 0)
            pool.wait_ge(s_const, 4)
            place_q(0, 0)
            for k in range(PIECES // 2, PIECES):
                fill_piece(k, 0)
            for g in range(1, G - 1):
                place_q(g, g)
            with pool.Fori(0, B) as it:
                for u in range(U):
                    scaled_v(u, it)
                    if u == 5:
                        place_q(G - 1, it * G + (G - 1), it)
                    if u == FILL_AT[0]:
                        pool.wait_ge(s_filled, jobs.filled(names[1].index(("mask", 3)), it))
                    if u in FILL_AT:
                        fill_piece(FILL_AT.index(u), it + 1)
                    for g in range(G - 1):
                        if u == NT * (g + 1) + 6:
                            place_q(g, it * G + (G + g), it)

        @block.tensor
        def _(pe):
            pe.wait_ge(s_const, 1)
            for j in range(HEAD + HG):
                mm = nc.tensor.matmul(bank[0][:, j:j + 1], rows[0:1, j, :, :, :].rearrange("o h c k -> o (h c k)"),
                                      ident[0:1, 0:1], start=True, stop=True)
            mm.then_inc(s_cpe, 1)
            pe.wait_ge(s_const, 3)
            for g in range(G):
                mm = nc.tensor.transpose(bank[0][:, g * P:(g + 1) * P],
                                         wo_wide[:, g, :, :].rearrange("p h k -> p (h k)"), ident[:, :])
            mm.then_inc(s_cpe, 1)
            pe.wait_ge(s_const, 4)
            pe.wait_ge(s_id, 1)

            def job(n, j, it=None):
                for _, count in jobs.free(n, it):
                    pe.wait_ge(s_emptied, count)
                bk_ = bank[n % 2]
                if j[0] == "ctxT":
                    if it is None:
                        pe.wait_ge(s_ctx, 16 * CTX_DMAS)
                    else:
                        pe.wait_ge(s_ctx, it * (16 * CTX_DMAS) + 32 * CTX_DMAS)
                    for t in range(4 * j[1], min(4 * j[1] + 4, NT)):
                        r = KT[t][1]
                        mm = nc.tensor.transpose(bk_[:, (t % 4) * P:(t % 4) * P + r], ctx_rows[0:r, t, :],
                                                 ident[0:r, 0:r])
                elif j[0] == "mask":
                    turned = bk_[:, :].bitcast(BF16)
                    if it is None or is_next[j]:
                        pe.wait_ge(s_fill, PIECES if it is None else it * PIECES + 2 * PIECES)
                    for t in range(4 * j[1], min(4 * j[1] + 4, NT)):
                        s0, r = KT[t]
                        for q in range(QT):
                            at_ = (t % 4) * SQ + q * P
                            mm = nc.tensor.transpose(turned[0:r, at_:at_ + P], fill[:, q, s0:s0 + r], ident16[:, :])
                elif j[0] == "q":
                    b = 0 if it is None else (it + 1) % B if is_next[j] else it
                    mm = nc.tensor.matmul(bk_[:, 0:SQ], wq_rows[:, j[1], :, :, :].rearrange("p h c k -> p (h c k)"),
                                          xnT[:, ds(b * SQ, SQ)], start=True, stop=True)
                elif j[0] == "k":
                    s0, r = CH[j[2]]
                    pe.wait_ge(s_emptied, jobs.emptied("dve", 4) if it is None else
                               after_job(("ctxT", 3), it) if is_next[j] else it * NP + N1)
                    mm = nc.tensor.matmul(bk_[:, 0:r], wk_rows[:, j[1], :, :, :].rearrange("p h c k -> p (h c k)"),
                                          ctxT[:, s0:s0 + r], start=True, stop=True)
                elif j[0] == "v":
                    pe.wait_ge(s_emptied, jobs.emptied("dve", 4) if it is None else
                               after_job(("ctxT", 3), it) if is_next[j] else it * NP + N1)
                    for t in range(4 * j[1], min(4 * j[1] + 4, NT)):
                        s0, r = KT[t]
                        mm = nc.tensor.matmul(bk_[0:r, (t % 4) * P:(t % 4 + 1) * P], ctxT[:, s0:s0 + r],
                                              w_in[:, 2, :, :].rearrange("p h k -> p (h k)"), start=True, stop=True)
                mm.then_inc(s_filled, 1)

            def project(groups, it):
                bk_ = bank[(NP - 1) % 2]
                if groups[0] == 0:
                    for _, count in jobs.free(NP - 1, it):
                        pe.wait_ge(s_emptied, count)
                pe.wait_ge(s_att, it * G + groups[-1] + 1)
                for g in groups:
                    for q in range(QT):
                        mm = nc.tensor.matmul(bk_[:, q * P:(q + 1) * P], attn[:, g, q * P:(q + 1) * P],
                                              wo_T[:, g, :], start=(q == 0 and g == 0), stop=(g == G - 1),
                                              skip_group_check=True)
                if groups[-1] == G - 1:
                    mm.then_inc(s_filled, 1)

            def scores(u, it):
                ahead, u = divmod(u, U)
                g, t = divmod(u, NT)
                s0, r = KT[t]
                row = 0 if it is None else it
                if t == 0:
                    pe.wait_ge(s_qop, row * (HG * G) + HG * (G * ahead + g + 1))
                if it is None or ahead:
                    src = names[it is not None].index(("mask", 0))
                    pe.wait_ge(s_emptied, jobs.emptied("dve", src + 1, it))
                elif g == 0 and t % 4 == 0:
                    pe.wait_ge(s_emptied, after_job(("mask", t // 4), it))
                elif u == NT * (G - 1):
                    pe.wait_ge(s_emptied, after_job(("k", G - 1, 3), it))
                for half in range(2):
                    w = 2 * u + half
                    last = w - SCORES + 2 * U * ahead if w >= SCORES else 2 * U - 1 - (2 * U - 1 - w) % SCORES
                    if it is not None:
                        pe.wait_ge(s_exp, it * (2 * U) + (last + 1 if ahead or w >= SCORES else 0))
                    elif w >= SCORES:
                        pe.wait_ge(s_exp, last + 1)
                    o = score[w % SCORES][0:r, :, :]
                    nc.tensor.matmul(o, k_op[g][:, s0:s0 + r], q_op[g][:, 2 * half:2 * half + 2, :],
                                     start=True, stop=False)
                    mm = nc.tensor.matmul(o, ident16[0:r, 0:r],
                                          fillT[0:r, t, :].unsqueeze(1).to_broadcast([r, 2, SQ]),
                                          start=False, stop=True)
                    mm.then_inc(s_score, 1)

            def pv(u, it):
                g, t = divmod(u, NT)
                r = KT[t][1]
                pe.wait_ge(s_vn, it * U + u + 1)
                if t == 0:
                    pe.wait_ge(s_att, it * G + g)
                for i in range(HG):
                    mm = nc.tensor.matmul(attn_acc[32 * i:32 * i + 32, g % 2, :], vn[u % SLOTS][0:r, i, :],
                                          e[u % SLOTS][0:r, i, :], start=(t == 0),
                                          stop=(t == NT - 1))
                mm.then_inc(s_pv, 1)

            for n, (j, _) in enumerate(first):
                job(n, j)
            for u in range(AHEAD):
                scores(u, None)
            with pe.Fori(0, B) as it:
                n = 0
                for u in range(U):
                    if u >= AHEAD:
                        scores(u, it)
                    for j in at[u]:
                        job(n, j, it)
                        n += 1
                    if u >= PV_LAG:
                        pv(u - PV_LAG, it)
                for n_, u in enumerate(range(U - PV_LAG, U)):
                    if n_ < AHEAD:
                        scores(U + n_, it)
                    if u == U - 1:
                        project(range(G - 1), it)
                    pv(u, it)
                project([G - 1], it)

        hi_at = [[n for n, j in enumerate(x) if j[0] == "q" or (j[0] == "k" and j[2] not in K_BY_DVE)] for x in names]

        def hi_constants(j):
            return (SQ, j[1] + G, 2 * G + 1) if j[0] == "q" else (CH[j[2]][1], j[1], 2 * G)

        @block.scalar
        def _(act):
            def hi_part(n, j, k, it=None):
                N, c, m = hi_constants(j)
                act.wait_ge(s_filled, jobs.filled(n, it))
                if k >= 2:
                    act.wait_ge(s_emptied, jobs.emptied("dve", hi_at[it is not None][k - 2] + 1, it))
                elif it is not None:
                    act.wait_ge(s_emptied, it * NP + (N1 - 1))
                nc.scalar.activation(hi[k % 2][:, 0:N], bank[n % 2][:, 0:N], ACT.Identity,
                                     bias=lo_bias[:, c:c + 1], scale=cols[:, m:m + 1]).then_inc(s_hi, 1)

            act.wait_ge(s_const, 4)
            for k, n in enumerate(hi_at[0]):
                hi_part(n, names[0][n], k)
            with act.Fori(0, B) as it:
                n = 0
                for u in range(U):
                    for j in at[u - 1] if u else []:
                        if n in hi_at[1]:
                            hi_part(n, j, hi_at[1].index(n), it)
                        n += 1
                    r = KT[u % NT][1]
                    act.wait_ge(s_pv, it * U + u + 1)
                    for i in range(HG):
                        w = 2 * u + i // 2
                        if i % 2 == 0:
                            act.wait_ge(s_max, it * (2 * U) + w + 1)
                        ex = nc.scalar.activation(e[u % SLOTS][0:r, i, :], score[w % SCORES][0:r, i % 2, :], ACT.Exp,
                                                  bias=neg_max[u % SLOTS][0:r, i:i + 1],
                                                  accum_out=total[u % SLOTS][0:r, i:i + 1])
                        if i % 2 == 1:
                            ex.then_inc(s_exp, 1)

        @block.vector
        def _(dve):
            dve.wait_ge(s_w, 8 * 16)
            nc.vector.memset(rows[:, 2 * G:, :, :, :], 0.0).then_inc(s_rec0, 1)
            dve.wait_ge(s_rec0, 1)
            nc.vector.memset(rows[:, 2 * G, :, 2:4, :], 1.0)
            for i in range(HG):
                nc.vector.memset(rows[:, HEAD + i, i, :, :], 1.0)
            for c in (1, 3):
                nc.vector.memset(rows[:, 2 * G + 1, :, c, :], 1.0)
            for i, scale in ((0, 1.0), (1, 0.125)):
                for g in range(G):
                    src = b_row[0:1, i, g * HG * DK:(g + 1) * HG * DK].rearrange("o (h k) -> o h k", h=HG)
                    last = nc.vector.tensor_scalar(rows[:, i * G + g, :, :, :],
                                                   src.unsqueeze(2).to_broadcast([1, HG, CP, DK]),
                                                   scale, None, ALU.mult)
            last.then_inc(s_const, 1)
            dve.wait_ge(s_zero, 1 + SLOTS)
            for g in range(G):
                last = nc.vector.tensor_copy(wo_wide[:, g, :, 0:DK],
                                             wo_in[:, g * HG * DK:(g + 1) * HG * DK].rearrange("p (h k) -> p h k", h=HG))
            last.then_inc(s_const, 1)
            for i, (dst, scale) in enumerate(((wq_rows, 0.125), (wk_rows, 1.0))):
                for g in range(G):
                    nc.vector.tensor_scalar(dst[:, g, :, :, :],
                                            w_in[:, i, g * HG:(g + 1) * HG, :].unsqueeze(2).to_broadcast([D, HG, CP, DK]),
                                            scale, None, ALU.mult)
            dve.wait_ge(s_cpe, 1)
            nc.vector.tensor_copy(cols[:, :], bank[0][:, 0:HEAD + HG]).then_inc(s_rec0, 1)
            dve.wait_ge(s_rec0, 2)
            for i in range(2):
                last = nc.vector.tensor_scalar(lo_bias[:, i * G:(i + 1) * G], cols[:, i * G:(i + 1) * G],
                                               cols[:, 2 * G + i:2 * G + i + 1], None, ALU.mult)
            last.then_inc(s_const, 1)
            dve.wait_ge(s_cpe, 2)
            nc.vector.tensor_copy(wo_T[:, :, :], bank[0][:, :].rearrange("p (g d) -> p g d", g=G)).then_inc(s_const, 1)

            def empty(n, j, it=None):
                bk_ = bank[n % 2]
                dve.wait_ge(s_filled, jobs.filled(n, it))
                if j[0] == "ctxT":
                    s0, r = CH[j[1]]
                    if it is not None and j[1] == 0:
                        dve.wait_ge(s_filled, it * NP + N1 + n)
                    ins = nc.vector.tensor_copy(ctxT[:, s0:s0 + r], bk_[:, 0:r])
                elif j[0] == "mask":
                    turned = bk_[:, :].bitcast(BF16)
                    if it is not None:
                        dve.wait_ge(s_score, it * (2 * U) + (2 * (NT * (G - 1) + 4) if is_next[j] else 0))
                    lo, hi_ = 4 * j[1], min(4 * j[1] + 4, NT)
                    r = KT[hi_ - 1][1]
                    ins = nc.vector.tensor_copy(fillT[0:r, lo:hi_, :],
                                                turned[0:r, 0:(hi_ - lo) * SQ].rearrange("p (t q) -> p t q", q=SQ))
                elif j[0] == "v":
                    lo, hi_ = 4 * j[1], min(4 * j[1] + 4, NT)
                    r = KT[hi_ - 1][1]
                    ins = nc.vector.tensor_tensor(v[0:r, lo:hi_, :], bk_[0:r, 0:(hi_ - lo) * P].rearrange("p (t d) -> p t d", d=P),
                                                  bv_all[0:r, :].unsqueeze(1).to_broadcast([r, hi_ - lo, P]), ALU.add)
                elif j[0] in "qk":
                    if n in hi_at[it is not None]:
                        k = hi_at[it is not None].index(n)
                        hi_ = hi[k % 2]
                        before = len(hi_at[0]) if it is not None else 0
                        dve.wait_ge(s_hi, k + 1 if it is None else it * len(hi_at[1]) + (before + k + 1))
                    else:
                        hi_ = hi[2]
                        N, c, m = hi_constants(j)
                        nc.vector.tensor_scalar(hi_[:, 0:N], bk_[:, 0:N], cols[:, m:m + 1], lo_bias[:, c:c + 1],
                                                ALU.mult, ALU.add).then_inc(s_hi_dve, 1)
                        own = [[i for i, x in enumerate(y) if x[0] == "k" and x[2] in K_BY_DVE] for y in names]
                        done = own[it is not None].index(n) + 1
                        dve.wait_ge(s_hi_dve, done if it is None else it * len(own[1]) + (len(own[0]) + done))
                    q_jobs = sum(x[0] == "q" for x in names[it is not None][:n])
                    if j[0] == "q":
                        N, c, dst = SQ, G + j[1], q_mix[:, :]
                        dve.wait_ge(s_qop, HG * q_jobs if it is None else it * (HG * G) + HG * (G - 1 + q_jobs))
                    else:
                        s0, N = CH[j[2]]
                        c, dst = j[1], k_op[j[1]][:, s0:s0 + N]
                        if it is not None and j[2] == 0:
                            dve.wait_ge(s_score, group_free(j, it))
                    ins = nc.vector.scalar_tensor_tensor(out=dst, in0=bk_[:, 0:N], scalar=cols[:, c:c + 1],
                                                         in1=hi_[:, 0:N], op0=ALU.add, op1=ALU.subtract)
                ins.then_inc(s_emptied, 1)
                if j[0] == "q":
                    dve.wait_ge(s_emptied, jobs.emptied("dve", n + 1, it))
                    dve.sem_inc(s_mix, 1)

            def maximum(u, it):
                r = KT[u % NT][1] if u < U else KT[u - U][1]
                for w in (2 * u, 2 * u + 1):
                    dve.wait_ge(s_score, w + 1 if it is None else it * (2 * U) + w + 1)
                    k = w % (2 * U) % SCORES
                    nc.vector.tensor_reduce(neg_max[u % SLOTS][0:r, w % 2 * 2:w % 2 * 2 + 2],
                                            score[k][0:r, :, :], AX.X, ALU.max,
                                            negate=True).then_inc(s_max, 1)

            def reciprocal(u, it):
                g, t = divmod(u, NT)
                r, slot = KT[t][1], u % SLOTS
                dve.wait_ge(s_exp, it * (2 * U) + 2 * u + 2)
                dve.wait_ge(s_pv, it * U + u + 1)
                nc.vector.reciprocal(recip[slot][0:r, :], total[slot][0:r, :]).then_inc(s_rec, 1)

            def copy_attn(g, it):
                dve.wait_ge(s_pv, it * U + (SLOTS + (g + 1) * NT))
                dve.wait_ge(s_filled, it * NP + N1)
                nc.vector.tensor_copy(attn[:, g, :], attn_acc[:, g % 2, :]).then_inc(s_att, 1)

            for n, (j, _) in enumerate(first):
                empty(n, j)
            for u in range(AHEAD):
                maximum(u, None)
            with dve.Fori(0, B) as it:
                n = 0
                for u in range(U):
                    if u > NT and u % NT == PV_LAG:
                        copy_attn(u // NT - 1, it)
                    if u >= AHEAD:
                        maximum(u, it)
                    for j in at[u - 1] if u else []:
                        empty(n, j, it)
                        n += 1
                    if u >= LAG:
                        reciprocal(u - LAG, it)
                for n_, u in enumerate(range(U - LAG, U)):
                    if n_ < AHEAD:
                        maximum(U + n_, it)
                    reciprocal(u, it)
                for u in range(LAG, AHEAD):
                    maximum(U + u, it)
                copy_attn(G - 1, it)
                dve.wait_ge(s_filled, jobs.filled(n, it))
                nc.vector.tensor_tensor(yb[:, :, :], bank[n % 2][:, 0:QT * P].rearrange("p (q d) -> p q d", q=QT),
                                        bo_all[:, :].unsqueeze(1).to_broadcast([P, QT, P]), ALU.add).then_inc(s_emptied, 1)
                dve.wait_ge(s_emptied, jobs.emptied("dve", n + 1, it))
                x = resid[:, ds(it * QT, QT), :]
                nc.vector.tensor_tensor(x, x, yb[:, :, :], ALU.add).then_inc(s_y, 1)
                dve.wait_ge(s_y, it * (1 + QT) + 1)
                for q in range(QT):
                    st, x = (a_[:, ds(it * QT + q, 1), :].rearrange("p t d -> p (t d)") for a_ in (stats, resid))
                    nc.vector.bn_stats(st, x).then_inc(s_y, 1)


def moe_ffn_0(nc, resid, stats, xnT, ident, gate_w, gate_b, dp_w1, dp_b1, dp_w2, dp_b2, ew1, eb1, ew2, eb2, TT):
    D, E = gate_w.shape
    DH = dp_w1.shape[1]
    HE = ew1.shape[2]
    HC = HE // P
    TG = BANK // P
    PASSES = TT // TG
    N = E * HC
    RING = 4
    LAG = 2
    AHEAD = 2
    PARTS = P // (TG * E)
    LROW = 96
    assert HC == 2 and E == 4 and N % RING == 0
    Z_STEPS = 2
    L_STEPS = Z_STEPS + 1 + E + E - 1 + E
    with ExitStack() as ctx:
        def sb(name, shape, dt=F32):
            return ctx.enter_context(nc.sbuf_tensor("f0_" + name, shape, dt))

        def sem(name):
            return ctx.enter_context(nc.semaphore("f0_" + name))

        w_dp1 = sb("w_dp1", [D, P])
        w_dp2 = sb("w_dp2", [P, P])
        b_dp1 = sb("b_dp1", [P, 1])
        b_dp2 = sb("b_dp2", [P, 1])
        b_gate = sb("b_gate", [P, E])
        w_e1 = sb("w_e1", [D, E, HE])
        w_e2 = sb("w_e2", [P, E, HC, D])
        b_e1 = sb("b_e1", [P, E * HC])
        w_e1_16 = [sb(f"w_e1_16_{i}", [D, E, HE], F16) for i in range(2)]
        x16 = [sb(f"x16_{i}", [D, TT * P], F16) for i in range(2)]
        b2_rows = sb("b2_rows", [P, TG, D])
        b2_16 = sb("b2_16", [P, TG, D], F16)
        b2_op = sb("b2_op", [P, TG, D], F16)
        less_lo = sb("less_lo", [P, TG])
        ident16 = sb("ident16", [P, P], F16)
        select = sb("select", [P, TG, E, P], F16)
        w16 = sb("w16", [P, TT, PARTS, E], F16)
        wT = sb("wT", [P, PASSES, P], F16)
        dp_h = [sb(f"dp_h{i}", [P, BANK]) for i in range(2)]
        lz_rows = [sb(f"lz_rows{i}", [P, BANK]) for i in range(2)]
        logit = sb("logit", [P, TT, E + 1])
        lg = [sb(f"lg{i}", [P, TT]) for i in range(E)]
        weight = sb("weight", [P, E, TT])
        pos = [sb(f"pos{i}", [P, TT]) for i in range(E)]
        top = sb("top", [P, TT])
        z = sb("z", [P, TT])
        ez = sb("ez", [P, TT])
        k_tok = sb("k_tok", [P, TT])
        t0 = sb("t0", [P, TT])
        t1 = sb("t1", [P, TT])
        relu = [sb(f"relu{i}", [P, BANK]) for i in range(RING)]
        hid = [sb(f"hid{i}", [P, BANK]) for i in range(RING)]
        yT = sb("yT", [D, BANK])
        hbank = [ctx.enter_context(nc.psum_tensor(f"f0_hbank{i}", [P, BANK], F32)) for i in range(RING)]
        wbank = [ctx.enter_context(nc.psum_tensor(f"f0_wbank{i}", [P, BANK], F32)) for i in range(2)]
        ybank = ctx.enter_context(nc.psum_tensor("f0_ybank", [P, BANK], F32))
        tbank = ctx.enter_context(nc.psum_tensor("f0_tbank", [P, BANK], F32))
        s_wr = sem("router_weights_in")
        s_w = sem("weights_in")
        s_zero = sem("lz_rows_zeroed")
        s_dp = sem("difficulty_hidden")
        s_dph = sem("dp_h_ready")
        s_lz = sem("logits_and_z")
        s_lzr = sem("lz_rows_ready")
        s_turn = sem("logits_turned")
        s_log = sem("logit_written")
        s_g = sem("gate_steps")
        s_ea = sem("exp_abs_z")
        s_ln = sem("softplus_log")
        s_el = sem("exp_logits")
        s_xh = sem("x_hi_ready")
        s_xl = sem("x_lo_ready")
        s_split = sem("weight_parts")
        s_const = sem("constants_set")
        s_w16 = sem("w16_parts")
        s_wt = sem("w16_turned")
        s_wtc = sem("wT_written")
        s_h = sem("hidden_filled")
        s_relu = sem("hbanks_free")
        s_hid = sem("relus_used_hid_ready")
        s_down = sem("hids_used")
        s_yt = sem("yT_copied")
        s_turn_y = sem("y_turned")
        s_r = sem("resid_added")
        s_st = sem("stats_done")
        block = ctx.enter_context(nc.Block())
        ROUTER_LOADS, LOADS = 4, 5 + TG

        @block.gpsimd
        def _(pool):
            for s_ in (s_relu, s_hid, s_down):
                pool.sem_inc(s_, RING)
            nc.gpsimd.memset(w16[:, :, :, :], 0.0).then_inc(s_const, 1)
            nc.gpsimd.tensor_scalar(ident16[:, :], ident[:, :], 1.0, 1.0, ALU.mult, ALU.mult).then_inc(s_const, 1)
            rows = ident[:, :].rearrange("p (j s e) -> p j s e", j=TG, s=PARTS)
            for j in range(TG):
                hi_, lo = (rows[:, j, s, :].unsqueeze(2).to_broadcast([P, E, P]) for s in range(2))
                nc.gpsimd.tensor_tensor(select[:, j, :, :], hi_, lo, ALU.add).then_inc(s_const, 1)

        @block.sync
        def _(sp):
            sp.wait_ge(s_zero, 6)
            with nc.allow_non_contiguous_dma(reason="narrow weights"):
                sp.dma_start(w_dp1[:, LROW:LROW + E], gate_w).then_inc(s_wr, 16)
                sp.dma_start(w_dp1[:, 0:DH], dp_w1).then_inc(s_wr, 16)
                sp.dma_start(w_dp2[0:DH, LROW + E:LROW + E + 1], dp_w2).then_inc(s_wr, 16)
                sp.dma_start(b_dp1[0:DH, :], dp_b1.rearrange("(p o) -> p o", o=1)).then_inc(s_wr, 16)
            sp.dma_start(w_e1[:, :, :], ew1.rearrange("e d h -> d e h")).then_inc(s_w, 16)
            for j in range(TG):
                row = j * PARTS * E
                sp.dma_start(b2_rows[row:row + 3 * E, j, :],
                             eb2.rearrange("(o e) d -> o e d", o=1).to_broadcast([3, E, D])).then_inc(s_w, 16)
            sp.dma_start(b_dp2[:, :], dp_b2.rearrange("(o p) -> o p", o=1).to_broadcast([P, 1])).then_inc(s_w, 16)
            sp.dma_start(b_gate[:, :], gate_b.rearrange("(o e) -> o e", o=1).to_broadcast([P, E])).then_inc(s_w, 16)
            sp.dma_start(w_e2[:, :, :, :], ew2.rearrange("e (c p) d -> p e c d", p=P)).then_inc(s_w, 16)
            with nc.allow_non_contiguous_dma(reason="a bias to a partition"):
                sp.dma_start(b_e1[:, :], eb1.rearrange("e (c p) -> p (e c)", p=P)).then_inc(s_w, 16)
            sp.wait_ge(s_w, 16 * LOADS)

        @block.tensor
        def _(pe):
            pe.wait_ge(s_wr, 16 * ROUTER_LOADS)
            with pe.Fori(0, PASSES // 2) as it:
                pe.wait_ge(s_lzr, 4 * it)
                for k in range(2):
                    x = xnT[:, ds(it * (2 * BANK) + k * BANK, BANK)]
                    nc.tensor.matmul(hbank[k][:, :], w_dp1[:, :], x, start=True, stop=True).then_inc(s_dp, 1)
                for k in range(2):
                    pe.wait_ge(s_dph, 2 * it + (k + 1))
                    nc.tensor.matmul(hbank[2 + k][:, :], w_dp2[:, :], dp_h[k][:, :], start=True,
                                     stop=True).then_inc(s_lz, 1)
                pe.wait_ge(s_log, 2 * it)
                for k in range(2):
                    pe.wait_ge(s_lzr, 4 * it + (k + 3))
                    for j in range(TG):
                        mm = nc.tensor.transpose(wbank[k][:, j * P:(j + 1) * P], lz_rows[k][:, j * P:(j + 1) * P],
                                                 ident[:, :])
                    mm.then_inc(s_turn, 1)
            pe.wait_ge(s_log, PASSES)
            pe.wait_ge(s_w, 16 * LOADS)
            pe.wait_ge(s_w16, 3)
            pe.wait_ge(s_const, 2 + TG)
            turned = wbank[0][:, :].bitcast(F16)
            for i in range(PASSES):
                mm = nc.tensor.transpose(turned[:, i * P:(i + 1) * P],
                                         w16[:, i * TG:(i + 1) * TG, :, :].rearrange("p t s e -> p (t s e)"),
                                         ident16[:, :])
            mm.then_inc(s_wt, 1)
            pe.wait_ge(s_wtc, 1)
            pe.wait_ge(s_split, 4)

            def rows_of(it):
                return wT[:, ds(it, 1), :].rearrange("p t d -> p (t d)")

            def hidden(n, it):
                ahead, k = divmod(n, N)
                e, c = divmod(k, HC)
                before = 0 if it is None else it * N
                at_ = 0 if it is None else (it + 1) % PASSES if ahead else it
                if c == 0:
                    pe.wait_ge(s_hid, before + n + 2)
                    for j in range(TG):
                        nc.tensor.matmul(wbank[e % 2][:, j * P:(j + 1) * P], select[:, j, e, :], rows_of(at_),
                                         start=True, stop=True)
                pe.wait_ge(s_relu, before + n + 1)
                for i, (a_, b_) in enumerate(((0, 0), (0, 1), (1, 0))):
                    mm = nc.tensor.matmul(hbank[n % RING][:, :], w_e1_16[a_][:, e, c * P:(c + 1) * P],
                                          x16[b_][:, ds(at_ * BANK, BANK)], start=(i == 0), stop=(i == 2))
                mm.then_inc(s_h, 1)

            def down(n, it):
                pe.wait_ge(s_hid, it * N + (RING + n + 1))
                if n == 0:
                    pe.wait_ge(s_yt, it)
                nc.tensor.matmul(ybank[:, :], w_e2[:, n // HC, n % HC, :], hid[n % RING][:, :], start=(n == 0),
                                 stop=False, skip_group_check=True).then_inc(s_down, 1)
                if n == 0:
                    for j in range(TG):
                        nc.tensor.matmul(ybank[:, j * P:(j + 1) * P], b2_op[:, j, :], rows_of(it),
                                         start=False, stop=False, skip_group_check=True)

            for n in range(AHEAD):
                hidden(n, None)
            with pe.Fori(0, PASSES) as it:
                for n in range(AHEAD, N):
                    hidden(n, it)
                    down(n - LAG, it)
                hidden(N, it)
                for n in range(N - LAG, N):
                    down(n, it)
                hidden(N + 1, it)
                pe.wait_ge(s_yt, it + 1)
                pe.wait_ge(s_r, it)
                for j in range(TG):
                    mm = nc.tensor.transpose(tbank[:, j * P:(j + 1) * P], yT[:, j * P:(j + 1) * P], ident[:, :])
                mm.then_inc(s_turn_y, 1)

        @block.scalar
        def _(act):
            with act.Fori(0, PASSES) as it:
                w = ds(it * BANK, BANK)
                nc.scalar.activation(x16[0][:, w], xnT[:, w], ACT.Copy).then_inc(s_xh, 1)
            act.wait_ge(s_wr, 16 * ROUTER_LOADS)
            with act.Fori(0, PASSES // 2) as it:
                act.wait_ge(s_lz, 2 * it)
                for k in range(2):
                    act.wait_ge(s_dp, 2 * it + (k + 1))
                    nc.scalar.activation(dp_h[k][:, :], hbank[k][:, :], ACT.Relu, bias=b_dp1[:, 0:1]).then_inc(s_dph, 1)
            act.wait_ge(s_w, 16 * LOADS)
            act.wait_ge(s_g, Z_STEPS)
            nc.scalar.activation(ez[:, :], t0[:, :], ACT.Exp, scale=-1.0).then_inc(s_ea, 1)
            act.wait_ge(s_g, Z_STEPS + 1)
            nc.scalar.activation(t0[:, :], ez[:, :], ACT.Ln).then_inc(s_ln, 1)
            act.wait_ge(s_g, L_STEPS)
            nc.scalar.activation(weight[:, :, :], weight[:, :, :], ACT.Exp).then_inc(s_el, 1)

            def rectify(n, before):
                act.wait_ge(s_h, before + n + 1)
                act.wait_ge(s_hid, before + n + 1)
                nc.scalar.activation(relu[n % RING][:, :], hbank[n % RING][:, :], ACT.Relu,
                                     bias=b_e1[:, n % N:n % N + 1]).then_inc(s_relu, 1)

            for n in range(AHEAD):
                rectify(n, 0)
            with act.Fori(0, PASSES) as it:
                for n in range(AHEAD, N + AHEAD):
                    rectify(n, it * N)
                act.wait_ge(s_down, it * N + (RING + N))
                act.wait_ge(s_turn_y, it)
                nc.scalar.activation(yT[:, :], ybank[:, :], ACT.Copy).then_inc(s_yt, 1)

        @block.vector
        def _(dve):
            for x in (*lz_rows, w_dp1, w_dp2, b_dp1):
                nc.vector.memset(x[:, :], 0.0).then_inc(s_zero, 1)
            nc.vector.memset(b2_rows[:, :, :], 0.0).then_inc(s_zero, 1)
            dve.wait_ge(s_zero, 6)
            with dve.Fori(0, PASSES) as it:
                w = ds(it * BANK, BANK)
                dve.wait_ge(s_xh, it + 1)
                nc.vector.tensor_tensor(x16[1][:, w], xnT[:, w], x16[0][:, w], ALU.subtract).then_inc(s_xl, 1)
            dve.wait_ge(s_wr, 16 * ROUTER_LOADS)
            with dve.Fori(0, PASSES // 2) as it:
                rows = slice(LROW, P)
                dve.wait_ge(s_turn, 2 * it)
                for k in range(2):
                    dve.wait_ge(s_dph, 2 * it + (k + 1))
                    nc.vector.tensor_copy(lz_rows[k][rows, :], hbank[k][rows, :]).then_inc(s_lzr, 1)
                for k in range(2):
                    dve.wait_ge(s_lzr, 4 * it + (k + 1))
                    dve.wait_ge(s_lz, 2 * it + (k + 1))
                    nc.vector.tensor_tensor(lz_rows[k][rows, :], hbank[2 + k][rows, :], lz_rows[k][rows, :],
                                            ALU.add).then_inc(s_lzr, 1)
                for k in range(2):
                    dve.wait_ge(s_turn, 2 * it + (k + 1))
                    turned = wbank[k][:, :].rearrange("p (t r) -> p t r", t=TG)
                    nc.vector.tensor_copy(logit[:, ds(it * (2 * TG) + k * TG, TG), :],
                                          turned[:, :, LROW:LROW + E + 1]).then_inc(s_log, 1)
            dve.wait_ge(s_w, 16 * LOADS)
            nc.vector.tensor_copy(w_e1_16[0][:, :, :], w_e1[:, :, :]).then_inc(s_split, 1)
            nc.vector.tensor_copy(b2_16[:, :, :], b2_rows[:, :, :]).then_inc(s_split, 1)
            third = ident[:, :].rearrange("p (j s e) -> p j s e", j=TG, s=PARTS)[:, :, 2, :]
            nc.vector.tensor_reduce(less_lo[:, :], third, AX.X, ALU.add, negate=True).then_inc(s_split, 1)
            dve.wait_ge(s_split, 3)
            nc.vector.tensor_tensor(w_e1_16[1][:, :, :], w_e1[:, :, :], w_e1_16[0][:, :, :], ALU.subtract)
            for j in range(TG):
                last = nc.vector.scalar_tensor_tensor(out=b2_op[:, j, :], in0=b2_16[:, j, :], scalar=less_lo[:, j:j + 1],
                                                      in1=b2_rows[:, j, :], op0=ALU.mult, op1=ALU.add)
            last.then_inc(s_split, 1)
            dve.wait_ge(s_log, PASSES)
            c = Steps()
            tt, ts = nc.vector.tensor_tensor, nc.vector.tensor_scalar
            ts(z[:, :], logit[:, :, E], b_dp2[:, 0:1], None, ALU.add).then_inc(s_g, 1)
            dve.wait_ge(s_g, c.up())
            nc.vector.scalar_tensor_tensor(out=t0[:, :], in0=z[:, :], scalar=-1.0, in1=z[:, :],
                                           op0=ALU.mult, op1=ALU.max).then_inc(s_g, 1)
            dve.wait_ge(s_g, c.up())
            assert c.n == Z_STEPS
            dve.wait_ge(s_ea, 1)
            ts(ez[:, :], ez[:, :], 1.0, None, ALU.add).then_inc(s_g, 1)
            dve.wait_ge(s_g, c.up())
            for i in range(E):
                ts(lg[i][:, :], logit[:, :, i], b_gate[:, i:i + 1], None, ALU.add).then_inc(s_g, 1)
                dve.wait_ge(s_g, c.up())
            tt(top[:, :], lg[0][:, :], lg[1][:, :], ALU.max).then_inc(s_g, 1)
            dve.wait_ge(s_g, c.up())
            for i in range(2, E):
                tt(top[:, :], top[:, :], lg[i][:, :], ALU.max).then_inc(s_g, 1)
                dve.wait_ge(s_g, c.up())
            for i in range(E):
                tt(weight[:, i, :], lg[i][:, :], top[:, :], ALU.subtract).then_inc(s_g, 1)
                c.up()
            dve.wait_ge(s_g, c.n)
            assert c.n == L_STEPS
            for i in range(E):
                nc.vector.memset(pos[i][:, :], float(E - 1 - i)).then_inc(s_g, 1)
                dve.wait_ge(s_g, c.up())
            for i in range(E):
                for j in range(i + 1, E):
                    tt(t1[:, :], lg[i][:, :], lg[j][:, :], ALU.is_ge).then_inc(s_g, 1)
                    dve.wait_ge(s_g, c.up())
                    tt(pos[j][:, :], pos[j][:, :], t1[:, :], ALU.add).then_inc(s_g, 1)
                    dve.wait_ge(s_g, c.up())
                    tt(pos[i][:, :], pos[i][:, :], t1[:, :], ALU.subtract).then_inc(s_g, 1)
                    dve.wait_ge(s_g, c.up())
            dve.wait_ge(s_ln, 1)
            nc.vector.scalar_tensor_tensor(out=z[:, :], in0=z[:, :], scalar=0.0, in1=t0[:, :],
                                           op0=ALU.max, op1=ALU.add).then_inc(s_g, 1)
            dve.wait_ge(s_g, c.up())
            ts(z[:, :], z[:, :], -0.5, 1.0 / 1.5, ALU.add, ALU.mult).then_inc(s_g, 1)
            dve.wait_ge(s_g, c.up())
            ts(z[:, :], z[:, :], 0.0, 1.0, ALU.max, ALU.min).then_inc(s_g, 1)
            dve.wait_ge(s_g, c.up())
            ts(z[:, :], z[:, :], float(E - 1), 1.0, ALU.mult, ALU.add).then_inc(s_g, 1)
            dve.wait_ge(s_g, c.up())
            ts(k_tok[:, :], z[:, :], 1.5, 1.0, ALU.is_ge, ALU.add).then_inc(s_g, 1)
            dve.wait_ge(s_g, c.up())
            for edge, compare in ((2.5, ALU.is_gt), (3.5, ALU.is_ge)):
                ts(t1[:, :], z[:, :], edge, None, compare).then_inc(s_g, 1)
                dve.wait_ge(s_g, c.up())
                tt(k_tok[:, :], k_tok[:, :], t1[:, :], ALU.add).then_inc(s_g, 1)
                dve.wait_ge(s_g, c.up())
            dve.wait_ge(s_el, 1)
            for i in range(E):
                tt(t1[:, :], pos[i][:, :], k_tok[:, :], ALU.is_lt).then_inc(s_g, 1)
                dve.wait_ge(s_g, c.up())
                tt(weight[:, i, :], weight[:, i, :], t1[:, :], ALU.mult).then_inc(s_g, 1)
                dve.wait_ge(s_g, c.up())
            nc.vector.tensor_reduce(t0[:, :], weight[:, :, :].rearrange("p e t -> p t e"), AX.X, ALU.add).then_inc(s_g, 1)
            dve.wait_ge(s_g, c.up())
            nc.vector.reciprocal(t1[:, :], t0[:, :]).then_inc(s_g, 1)
            dve.wait_ge(s_g, c.up())
            for i in range(E):
                tt(weight[:, i, :], weight[:, i, :], t1[:, :], ALU.mult).then_inc(s_g, 1)
                dve.wait_ge(s_g, c.up())
            by_token = weight[:, :, :].rearrange("p e t -> p t e")
            dve.wait_ge(s_const, 1)
            nc.vector.tensor_copy(w16[:, :, 0, :], by_token).then_inc(s_w16, 1)
            nc.vector.tensor_copy(w16[:, :, 2, :], by_token).then_inc(s_w16, 1)
            dve.wait_ge(s_w16, 1)
            nc.vector.tensor_tensor(w16[:, :, 1, :], by_token, w16[:, :, 0, :], ALU.subtract).then_inc(s_w16, 1)
            dve.wait_ge(s_wt, 1)
            nc.vector.tensor_copy(wT[:, :, :], wbank[0][:, :].bitcast(F16)[:, 0:PASSES * P].rearrange("p (i d) -> p i d", d=P)).then_inc(s_wtc, 1)

            def weigh(n, before):
                dve.wait_ge(s_relu, before + (RING + n + 1))
                dve.wait_ge(s_down, before + n + 1)
                tt(hid[n % RING][:, :], wbank[n // HC % 2][:, :], relu[n % RING][:, :], ALU.mult).then_inc(s_hid, 1)

            for n in range(AHEAD):
                weigh(n, 0)
            with dve.Fori(0, PASSES) as it:
                for n in range(AHEAD, N + AHEAD):
                    weigh(n, it * N)
                dve.wait_ge(s_turn_y, it + 1)
                x = resid[:, ds(it * TG, TG), :]
                tt(x, tbank[:, :].rearrange("p (t d) -> p t d", d=D), x, ALU.add).then_inc(s_r, 1)
                dve.wait_ge(s_r, it + 1)
                for j in range(TG):
                    st, x = (a_[:, ds(it * TG + j, 1), :].rearrange("p t d -> p (t d)") for a_ in (stats, resid))
                    nc.vector.bn_stats(st, x).then_inc(s_st, 1)


def cross_attention_1(nc, resid, stats, xnT, ident, ctx_in, mask_in, Wq, Wkv, Wout, bout, B, SQ):
    SK, D = ctx_in.shape[1:]
    INNER = Wq.shape[1]
    DH = 64
    H = INNER // DH
    HP = H // 2
    KT = tiles(SK)
    NT = len(KT)
    CH = tiles(SK, BANK)
    NC = len(CH)
    QT = SQ // P
    TT = B * QT
    U = HP * 2 * QT
    PU = 2 * QT
    LAG = 3
    T_BY = ("act", "act", "dve", "dve")

    V_BY = ["act" if t % 2 and t < NT - 2 else "dve" for t in range(NT)]
    at = {s: [] for s in range(U + LAG)}
    for t in range(NT):
        at[t * 3 // NT].append((("v", 1, t), V_BY[t]))
        if t < NT - 1:
            at[U + t * LAG // (NT - 1)].append((("v", 0, t), V_BY[t]))
    before_pv = {s: [] for s in range(U + LAG)}
    for p in range(HP - 1):
        before_pv[LAG + PU * (p + 1)].append((("q", p), "dve"))
    at[U] = [(("ctxT", c), "dve") for c in range(NC)] + [(("q", HP - 1), "dve")] + at[U]
    turns = {s: [(("t", s - LAG, c), T_BY[c]) for c in range(NC)] if s >= LAG else [] for s in range(U + LAG)}
    steps = {s: before_pv[s] + turns[s] + at[s] for s in range(U + LAG)}
    per = [j for s in range(U + LAG) for j in steps[s]]
    per += [(("v", 0, NT - 1), V_BY[NT - 1]), (("y",), "dve")]
    first = [(("ctxT", c), "dve") for c in range(NC)]
    first += [(("v", 0, t), V_BY[t]) for t in range(NT)] + [(("q", p), "dve") for p in range(HP)]
    jobs = Jobs(first, per, 3)
    owner = dict(per)
    first, per = ([j for j, _ in x] for x in (first, per))
    N1, NP = len(first), len(per)
    CTX_DMAS = 2 if SK % P else 1

    with ExitStack() as ctx:
        def sb(name, shape, dt=F32, stack=ctx):
            return stack.enter_context(nc.sbuf_tensor("a1_" + name, shape, dt))

        def ps(name, shape, dt=F32, stack=ctx):
            return stack.enter_context(nc.psum_tensor("a1_" + name, shape, dt))

        def sem(name, stack=ctx):
            return stack.enter_context(nc.semaphore("a1_" + name))

        A = sb("A", [D, H, D])
        wv = [sb(f"wv{i}", [D, INNER], F16) for i in range(2)]
        w_out = sb("w_out", [P, HP, D])
        b_out = sb("b_out", [P, D])
        mask_fill = sb("mask_fill", [P, TT])

        with ExitStack() as tmp:
            wq_in = sb("wq_in", [D, INNER], stack=tmp)
            wkv_in = sb("wkv_in", [D, 2 * INNER], stack=tmp)
            wq_T = sb("wq_T", [P, HP, D], stack=tmp)
            wk_T = sb("wk_T", [P, HP, D], stack=tmp)
            mask_i = sb("mask_i", [TT, P], I32, stack=tmp)
            mask_f = sb("mask_f", [TT, P], stack=tmp)
            sbank = [ps(f"sbank{i}", [P, BANK], stack=tmp) for i in range(8)]
            s_w = sem("weights_in", tmp)
            s_t = sem("weights_turned", tmp)
            s_c = sem("turned_copied", tmp)
            s_a = sem("A_filled", tmp)
            s_v = sem("wv_parts", tmp)
            s_m = sem("mask_steps", tmp)
            s_e = sem("A_copied", tmp)
            TB = BANK // P
            block = tmp.enter_context(nc.Block())

            @block.sync
            def _(sp):
                sp.dma_start(wq_in[:, :], Wq).then_inc(s_w, 16)
                sp.dma_start(mask_i[:, :], mask_in.rearrange("b (q p) -> (b q) p", p=P)).then_inc(s_w, 16)
                sp.dma_start(wkv_in[:, :], Wkv).then_inc(s_w, 16)
                sp.dma_start(w_out[:, :, :], Wout.rearrange("(h p) d -> p h d", p=P)).then_inc(s_w, 16)
                sp.dma_start(b_out[:, :], bout.rearrange("(o d) -> o d", o=1).to_broadcast([P, D])).then_inc(s_w, 16)

            @block.tensor
            def _(pe):
                pe.wait_ge(s_w, 5 * 16)
                for w, x in enumerate((wq_in, wkv_in)):
                    for p in range(HP):
                        mm = nc.tensor.transpose(sbank[2 * w + p // TB][:, p % TB * P:(p % TB + 1) * P],
                                                 x[:, p * P:(p + 1) * P], ident[:, :])
                        if p % TB == TB - 1:
                            mm.then_inc(s_t, 1)
                pe.wait_ge(s_c, 4)
                for i in range(2):
                    half = slice(DH * i, DH * i + DH)
                    for p in range(HP):
                        mm = nc.tensor.matmul(sbank[4 + i * HP // TB + p // TB][:, p % TB * P:(p % TB + 1) * P],
                                              wq_T[half, p, :], wk_T[half, p, :], start=True, stop=True)
                        if p % TB == TB - 1:
                            mm.then_inc(s_a, 1)
                pe.wait_ge(s_m, 2)
                nc.tensor.transpose(sbank[0][:, 0:TT], mask_f[:, :], ident[0:TT, 0:TT]).then_inc(s_t, 1)

            @block.scalar
            def _(act):
                for n in range(4):
                    act.wait_ge(s_t, n + 1)
                    dst = (wq_T, wk_T)[n // 2][:, n % 2 * TB:(n % 2 + 1) * TB, :]
                    nc.scalar.activation(dst, sbank[n][:, :].rearrange("p (h d) -> p h d", h=TB), ACT.Copy,
                                         scale=(-0.125, 1.0)[n // 2]).then_inc(s_c, 1)
                for n in range(H // TB):
                    act.wait_ge(s_a, n + 1)
                    i, k = divmod(n, HP // TB)
                    nc.scalar.activation(A[:, :, :].rearrange("p (h i) d -> p i h d", i=2)[:, i, k * TB:(k + 1) * TB, :],
                                         sbank[4 + n][:, :].rearrange("p (h d) -> p h d", h=TB), ACT.Copy).then_inc(s_e, 1)

            @block.vector
            def _(dve):
                dve.wait_ge(s_w, 5 * 16)
                nc.vector.tensor_scalar(mask_f[:, :], mask_i[:, :], -1.0, 1.0, ALU.mult, ALU.add).then_inc(s_m, 1)
                dve.wait_ge(s_m, 1)
                nc.vector.tensor_scalar(mask_f[:, :], mask_f[:, :], MASK_NEG, None, ALU.mult).then_inc(s_m, 1)
                nc.vector.tensor_copy(wv[0][:, :], wkv_in[:, INNER:]).then_inc(s_v, 1)
                dve.wait_ge(s_v, 1)
                nc.vector.tensor_tensor(wv[1][:, :], wkv_in[:, INNER:], wv[0][:, :], ALU.subtract).then_inc(s_v, 1)
                dve.wait_ge(s_t, 5)
                nc.vector.tensor_copy(mask_fill[:, :], sbank[0][:, 0:TT]).then_inc(s_v, 1)
        nc.all_engine_barrier()

        ctx_rows = sb("ctx_rows", [P, NT, D])
        ctxT = [sb(f"ctxT{i}", [D, SK], F16) for i in range(2)]
        qA = [sb(f"qA{i}", [D, H, SQ], F16) for i in range(2)]
        v = sb("v", [P, NT, INNER])
        SLOTS = 4
        e = [sb(f"e{i}", [P, SK]) for i in range(SLOTS)]
        least2 = [sb(f"least2_{i}", [P, 2]) for i in range(SLOTS)]
        least = [sb(f"least{i}", [P, 1]) for i in range(SLOTS)]
        total = [sb(f"total{i}", [P, 1]) for i in range(SLOTS)]
        recip = [sb(f"recip{i}", [P, 1]) for i in range(SLOTS)]
        eT = [sb(f"eT{i}", [P, NT, SQ]) for i in range(2)]
        outT = sb("outT", [P, HP, SQ])
        yb = sb("yb", [P, QT, D])
        score = ps("score", [P, NC * BANK])
        bank = [ps(f"bank{i}", [P, BANK]) for i in range(3)]
        out_acc = ps("out_acc", [P, BANK])

        s_ctx = sem("ctx_in")
        s_pool = sem("pool_steps_begun")
        s_filled = sem("bank_filled")
        s_emptied = {"act": sem("bank_emptied_act"), "dve": sem("bank_emptied_dve")}
        s_hi = sem("hi_part_ready")
        s_score = sem("scores_ready")
        s_sub = sem("score_halves_taken")
        s_least = sem("least_ready")
        s_exp = sem("exp_done")
        s_rec = sem("recip_ready")
        s_norm = sem("weights_normalised")
        s_pv = sem("pv_done")
        s_out = sem("outT_copied")
        s_y = sem("resid_steps")
        block = ctx.enter_context(nc.Block())

        def after_jobs(eng, last, it):
            for who in ("act", "dve"):
                eng.wait_ge(s_emptied[who], jobs.emptied(who, per.index(last) + 1, it))

        HALVES = (slice(0, 2 * BANK), slice(2 * BANK, SK))

        def unit(u):
            p, r = divmod(u, PU)
            return p, r // 2, r % 2

        @block.sync
        def _(sp):
            def load(b):
                c = ctx_in[ds(b, 1), :, :]
                whole = SK // P
                sp.dma_start(ctx_rows[:, 0:whole, :],
                             c[:, 0:whole * P, :].rearrange("o (t p) d -> p (o t) d", p=P)).then_inc(s_ctx, 16)
                if SK % P:
                    sp.dma_start(ctx_rows[0:SK % P, whole, :],
                                 c[:, whole * P:SK, :].rearrange("o p d -> (o p) d")).then_inc(s_ctx, 16)

            load(0)
            with sp.Fori(0, B) as it:
                sp.wait_ge(s_filled, it * NP + N1)
                load((it + 1) % B)
            sp.wait_ge(s_ctx, 16 * CTX_DMAS * (B + 1))

        @block.tensor
        def _(pe):
            def job(n, j, it=None):
                for who, count in jobs.free(n, it):
                    pe.wait_ge(s_emptied[who], count)
                bk_ = bank[n % 3]
                if j[0] == "ctxT":
                    if it is None:
                        pe.wait_ge(s_ctx, 16 * CTX_DMAS)
                    else:
                        pe.wait_ge(s_ctx, it * (16 * CTX_DMAS) + 32 * CTX_DMAS)
                    for t in range(4 * j[1], min(4 * j[1] + 4, NT)):
                        r = KT[t][1]
                        mm = nc.tensor.transpose(bk_[:, (t % 4) * P:(t % 4) * P + r], ctx_rows[0:r, t, :],
                                                 ident[0:r, 0:r])
                elif j[0] == "q":
                    b = 0 if it is None else (it + 1) % B
                    for i in range(2):
                        mm = nc.tensor.matmul(bk_[:, i * SQ:(i + 1) * SQ], A[:, 2 * j[1] + i, :],
                                              xnT[:, ds(b * SQ, SQ)], start=True, stop=True)
                elif j[0] == "v":
                    if j[1:] == (0, 0):
                        src = first if it is None else per
                        pe.wait_ge(s_emptied["dve"], jobs.emptied("dve", src.index(("ctxT", NC - 1)) + 1, it))
                    s0, r = KT[j[2]]
                    w = slice(j[1] * BANK, (j[1] + 1) * BANK)
                    for i, (a_, b_) in enumerate(((0, 0), (0, 1), (1, 0))):
                        mm = nc.tensor.matmul(bk_[0:r, :], ctxT[a_][:, s0:s0 + r], wv[b_][:, w],
                                              start=(i == 0), stop=(i == 2))
                elif j[0] == "t":
                    u = j[1]
                    if j[2] == 0:
                        pe.wait_ge(s_norm, it * U + u + 1)
                    for t in range(4 * j[2], min(4 * j[2] + 4, NT)):
                        s0, r = KT[t]
                        mm = nc.tensor.transpose(bk_[0:r, (t % 4) * P:(t % 4 + 1) * P], e[u % SLOTS][:, s0:s0 + r],
                                                 ident[:, :])
                elif j[0] == "y":
                    pe.wait_ge(s_out, it * HP + HP)
                    pe.wait_ge(s_emptied["dve"], jobs.emptied("dve", per.index(("q", HP - 1)) + 1, it))
                    for q in range(QT):
                        for p in range(HP):
                            mm = nc.tensor.matmul(bk_[:, q * P:(q + 1) * P], outT[:, p, q * P:(q + 1) * P],
                                                  w_out[:, p, :], start=(q == 0 and p == 0), stop=(p == HP - 1),
                                                  skip_group_check=True)
                mm.then_inc(s_filled, 1)

            def scores(u, it):
                p, q, i = unit(u)
                h = 2 * p + i
                qs = slice(q * P, (q + 1) * P)
                for k, (s0, r) in enumerate(CH):
                    if k % 2 == 0:
                        pe.wait_ge(s_sub, it * (2 * U) + max(2 * u - 1 + k // 2, 0))
                    for n, (a_, b_) in enumerate(((0, 0), (0, 1), (1, 0))):
                        mm = nc.tensor.matmul(score[:, s0:s0 + r], qA[a_][:, h, qs], ctxT[b_][:, s0:s0 + r],
                                              start=(n == 0), stop=(n == 2))
                    if k % 2:
                        mm.then_inc(s_score, 1)

            def pv(p, it):
                pe.wait_ge(s_out, it * HP + p)
                after_jobs(pe, ("t", PU * p + PU - 1, NC - 1), it)
                for t, (_, r) in enumerate(KT):
                    for i in range(2):
                        w = (2 * p + i) * DH
                        mm = nc.tensor.matmul(out_acc[DH * i:DH * i + DH, 0:SQ], v[0:r, t, w:w + DH],
                                              eT[i][0:r, t, :], start=(t == 0), stop=(t == NT - 1))
                mm.then_inc(s_pv, 1)

            for n, j in enumerate(first):
                job(n, j)
            pe.wait_ge(s_emptied["dve"], jobs.emptied("dve", N1))
            with pe.Fori(0, B) as it:
                n = 0
                for s in range(U + LAG):
                    if s < U:
                        scores(s, it)
                    for j, _ in before_pv[s]:
                        job(n, j, it)
                        n += 1
                    if s > LAG and (s - LAG) % PU == 0:
                        pv((s - LAG) // PU - 1, it)
                    for j, _ in steps[s][len(before_pv[s]):]:
                        job(n, j, it)
                        n += 1
                pv(HP - 1, it)
                for j in per[n:]:
                    job(n, j, it)
                    n += 1

        def split(n, j, it):
            bk_ = bank[n % 3]
            if j[0] == "ctxT":
                s0, r = CH[j[1]]
                return [x[:, s0:s0 + r] for x in ctxT], bk_[:, 0:r]
            return [x[:, 2 * j[1]:2 * j[1] + 2, :] for x in qA], bk_[:, :].rearrange("p (h q) -> p h q", h=2)

        def whole(n, j):
            bk_ = bank[n % 3]
            if j[0] == "v":
                r = KT[j[2]][1]
                return v[0:r, j[2], j[1] * BANK:(j[1] + 1) * BANK], bk_[0:r, :]
            _, q, i = unit(j[1])
            lo, hi_ = 4 * j[2], min(4 * j[2] + 4, NT)
            r = KT[hi_ - 1][1]
            return eT[i][0:r, lo:hi_, q * P:(q + 1) * P], bk_[0:r, 0:(hi_ - lo) * P].rearrange("p (t q) -> p t q", q=P)

        def pv_before(j, it):
            return it * HP + (j[1] // PU if j[0] == "t" else 0 if j[1] else HP // 2)

        def scores_before(j, it):
            return it * (2 * U) + 2 * (PU * (j[1] + 1) if j[0] == "q" else U)

        hi_jobs = [[n for n, j in enumerate(x) if j[0] in ("ctxT", "q")] for x in (first, per)]

        @block.scalar
        def _(act):
            def part(n, j, it=None):
                if j[0] in ("ctxT", "q"):
                    act.wait_ge(s_filled, jobs.filled(n, it))
                    if it is not None:
                        act.wait_ge(s_score, scores_before(j, it))
                    (hi_, _), src = split(n, j, it)
                    nc.scalar.activation(hi_, src, ACT.Copy).then_inc(s_hi, 1)
                elif owner[j] == "act":
                    act.wait_ge(s_filled, jobs.filled(n, it))
                    if it is not None:
                        act.wait_ge(s_pv, pv_before(j, it))
                    dst, src = whole(n, j)
                    nc.scalar.activation(dst, src, ACT.Copy).then_inc(s_emptied["act"], 1)

            for n, j in enumerate(first):
                part(n, j)
            with act.Fori(0, B) as it:
                n = 0
                for s in range(U + LAG):
                    for _ in steps[s]:
                        part(n, per[n], it)
                        n += 1
                    if s < U:
                        act.wait_ge(s_least, it * U + s + 1)
                        nc.scalar.activation(e[s % SLOTS][:, :], e[s % SLOTS][:, :], ACT.Exp, bias=least[s % SLOTS][:, 0:1],
                                             scale=-1.0, accum_out=total[s % SLOTS][:, 0:1]).then_inc(s_exp, 1)
                while n < NP:
                    part(n, per[n], it)
                    n += 1

        @block.gpsimd
        def _(pool):
            with pool.Fori(0, B) as it:
                for u in range(U):
                    pool.wait_ge(s_rec, it * U + u + 1)
                    pool.sem_inc(s_pool, 1)
                    x = e[u % SLOTS][:, :]
                    nc.gpsimd.tensor_scalar(x, x, recip[u % SLOTS][:, 0:1], 1.0, ALU.mult, ALU.mult).then_inc(s_norm, 1)

        @block.vector
        def _(dve):
            def part(n, j, it=None):
                if j[0] == "y":
                    dve.wait_ge(s_filled, jobs.filled(n, it))
                    nc.vector.tensor_tensor(yb[:, :, :], bank[n % 3][:, 0:QT * D].rearrange("p (q d) -> p q d", q=QT),
                                            b_out[:, :].unsqueeze(1).to_broadcast([P, QT, D]), ALU.add).then_inc(s_emptied["dve"], 1)
                elif j[0] in ("ctxT", "q"):
                    k = hi_jobs[it is not None].index(n)
                    dve.wait_ge(s_hi, k + 1 if it is None else it * len(hi_jobs[1]) + (len(hi_jobs[0]) + k + 1))
                    (hi_, lo), src = split(n, j, it)
                    nc.vector.tensor_tensor(lo, src, hi_, ALU.subtract).then_inc(s_emptied["dve"], 1)
                elif owner[j] == "dve":
                    dve.wait_ge(s_filled, jobs.filled(n, it))
                    if it is not None:
                        dve.wait_ge(s_pv, pv_before(j, it))
                    dst, src = whole(n, j)
                    nc.vector.tensor_copy(dst, src).then_inc(s_emptied["dve"], 1)

            def reciprocal(u, it):
                dve.wait_ge(s_exp, it * U + u + 1)
                nc.vector.reciprocal(recip[u % SLOTS][:, :], total[u % SLOTS][:, :]).then_inc(s_rec, 1)

            def take(u, half, it):
                _, q, _ = unit(u)
                dve.wait_ge(s_score, it * (2 * U) + 2 * u + half + 1)
                if half == 0:
                    dve.wait_ge(s_filled, jobs.filled(per.index(("t", u - SLOTS, NC - 1)), it) if u >= SLOTS
                                else it * NP + N1)
                w = HALVES[half]
                nc.vector.tensor_scalar(e[u % SLOTS][:, w], score[:, w], mask_fill[:, ds(it * QT + q, 1)], None,
                                        ALU.add, ALU.min, accum_out=least2[u % SLOTS][:, half:half + 1]).then_inc(s_sub, 1)

            def copy_out(p, it):
                dve.wait_ge(s_pv, it * HP + p + 1)
                dve.wait_ge(s_filled, it * NP + N1)
                nc.vector.tensor_copy(outT[:, p, :], out_acc[:, 0:SQ]).then_inc(s_out, 1)

            for n, j in enumerate(first):
                part(n, j)
            with dve.Fori(0, B) as it:
                n = 0
                for s in range(U + LAG):
                    if s < U:
                        take(s, 0, it)
                    if 0 < s <= U:
                        reciprocal(s - 1, it)
                    if s < U:
                        take(s, 1, it)
                        dve.wait_ge(s_sub, it * (2 * U) + 2 * s + 2)
                        x = least2[s % SLOTS]
                        nc.vector.tensor_tensor(least[s % SLOTS][:, :], x[:, 0:1], x[:, 1:2], ALU.min).then_inc(s_least, 1)
                    for _ in before_pv[s]:
                        part(n, per[n], it)
                        n += 1
                    if s > LAG and (s - LAG) % PU == 0:
                        copy_out((s - LAG) // PU - 1, it)
                    for _ in steps[s][len(before_pv[s]):]:
                        part(n, per[n], it)
                        n += 1
                copy_out(HP - 1, it)
                while n < NP:
                    part(n, per[n], it)
                    n += 1
                dve.wait_ge(s_emptied["dve"], jobs.emptied("dve", per.index(("y",)) + 1, it))
                x = resid[:, ds(it * QT, QT), :]
                nc.vector.tensor_tensor(x, x, yb[:, :, :], ALU.add).then_inc(s_y, 1)
                dve.wait_ge(s_y, it * (1 + QT) + 1)
                for q in range(QT):
                    st, x = (a_[:, ds(it * QT + q, 1), :].rearrange("p t d -> p (t d)") for a_ in (stats, resid))
                    nc.vector.bn_stats(st, x).then_inc(s_y, 1)


def moe_ffn_1(nc, resid, xnT, ident, Wr, Wg, Wu, Wd, Sg, Su, Sd, TT):
    D, E = Wr.shape
    F = Wg.shape[2]
    NPAIR = E * F // P
    N = NPAIR + 1
    TG = BANK // P
    PASSES = TT // TG
    SUBS = 2
    M = SUBS * N
    RING = 2
    AHEAD = 2
    TOP = 2
    assert M % RING == 0 and PASSES % SUBS == 0
    assert 2 * F == P and Sg.shape[1] == P and TG * 2 * E == P and TT * E <= BANK
    with ExitStack() as ctx:
        def sb(name, shape, dt=F32):
            return ctx.enter_context(nc.sbuf_tensor("f1_" + name, shape, dt))

        def ps(name):
            return ctx.enter_context(nc.psum_tensor("f1_" + name, [P, BANK], F32))

        def sem(name):
            return ctx.enter_context(nc.semaphore("f1_" + name))

        w_in = sb("w_in", [D, 2, N, P])
        w_gu = [sb(f"w_gu{i}", [D, 2, N, P], F16) for i in range(2)]
        wr_in = sb("wr_in", [D, E])
        w_r = [sb(f"w_r{i}", [D, E], F16) for i in range(2)]
        w_d = sb("w_d", [P, N, D])
        x16 = [sb(f"x16_{i}", [D, TT * P], F16) for i in range(2)]
        ident16 = sb("ident16", [P, P], F16)
        select = sb("select", [P, TG, E, F], F16)
        order = sb("order", [P, E])
        prob = sb("prob", [P, TT, E])
        left = sb("left", [P, TT, E])
        mark = sb("mark", [P, TT, E])
        pick = sb("pick", [P, TT, E])
        cw = sb("cw", [P, TT, E])
        best = sb("best", [P, TT])
        cw16 = sb("cw16", [P, TT, 2, E], F16)
        cwT = sb("cwT", [P, PASSES, P], F16)
        silu = [sb(f"silu{i}", [P, BANK]) for i in range(2)]
        hid = [sb(f"hid{i}", [P, BANK]) for i in range(2)]
        yT = sb("yT", [D, BANK])
        gbank = [ps(f"gbank{i}") for i in range(2)]
        ubank = [ps(f"ubank{i}") for i in range(2)]
        cbank = [ps(f"cbank{i}") for i in range(2)]
        ybank = ps("ybank")
        tbank = ps("tbank")
        s_wr = sem("router_weights_in")
        s_w = sem("weights_in")
        s_whi = sem("w_gu_hi_ready")
        s_split = sem("weight_and_cw_parts")
        s_id = sem("constants_set")
        s_xh = sem("x_hi_ready")
        s_xl = sem("x_lo_ready")
        s_logit = sem("logits_filled")
        s_route = sem("routing_steps")
        s_exp = sem("exp_done")
        s_cwt = sem("cw_turned")
        s_cwc = sem("cwT_written")
        s_fill = sem("pair_filled")
        s_silu = sem("gbanks_free_silu_ready")
        s_gate = sem("gated")
        s_hid = sem("silus_used_hid_ready")
        s_down = sem("hids_used")
        s_yt = sem("yT_copied")
        s_turn = sem("y_turned")
        s_r = sem("resid_added")
        block = ctx.enter_context(nc.Block())
        LOADS = 6

        @block.sync
        def _(sp):
            sp.dma_start(wr_in[:, :], Wr).then_inc(s_wr, 16)
            for i, (w, s) in enumerate(((Wg, Sg), (Wu, Su))):
                sp.dma_start(w_in[:, i, 0:NPAIR, :].rearrange("d n (i f) -> d (n i) f", f=F),
                             w.rearrange("e d f -> d e f")).then_inc(s_w, 16)
                sp.dma_start(w_in[:, i, NPAIR, :], s).then_inc(s_w, 16)
            sp.dma_start(w_d[:, 0:NPAIR, :], Wd.rearrange("(n i) f d -> (i f) n d", i=2)).then_inc(s_w, 16)
            sp.dma_start(w_d[:, NPAIR, :], Sd).then_inc(s_w, 16)
            sp.wait_ge(s_w, 16 * LOADS)

        @block.gpsimd
        def _(pool):
            for s_ in (s_silu, s_hid, s_down):
                pool.sem_inc(s_, RING)
            for e in range(E):
                nc.gpsimd.memset(order[:, e:e + 1], float(E - e)).then_inc(s_id, 1)
            nc.gpsimd.tensor_scalar(ident16[:, :], ident[:, :], 1.0, 1.0, ALU.mult, ALU.mult).then_inc(s_id, 1)
            rows = ident[:, :].rearrange("p (j s e) -> p j s e", j=TG, s=2)
            for j in range(TG):
                hi_, lo = (rows[:, j, s, :].unsqueeze(2).to_broadcast([P, E, F]) for s in range(2))
                nc.gpsimd.tensor_tensor(select[:, j, :, :], hi_, lo, ALU.add).then_inc(s_id, 1)

        @block.tensor
        def _(pe):
            pe.wait_ge(s_split, 2)
            with pe.Fori(0, PASSES) as it:
                pe.wait_ge(s_xl, it + 1)
                for j in range(TG):
                    t = it * TG + j
                    for i, (a_, b_) in enumerate(((0, 0), (0, 1), (1, 0))):
                        mm = nc.tensor.matmul(gbank[0][:, ds(t * E, E)], x16[a_][:, ds(t * P, P)], w_r[b_][:, :],
                                              start=(i == 0), stop=(i == 2))
                mm.then_inc(s_logit, 1)
            pe.wait_ge(s_id, E + 1 + TG)
            pe.wait_ge(s_split, 5)
            turned = cbank[0][:, :].bitcast(F16)
            for i in range(PASSES):
                mm = nc.tensor.transpose(turned[:, i * P:(i + 1) * P],
                                         cw16[:, i * TG:(i + 1) * TG, :, :].rearrange("p t s e -> p (t s e)"),
                                         ident16[:, :])
            mm.then_inc(s_cwt, 1)
            pe.wait_ge(s_w, 16 * LOADS)
            pe.wait_ge(s_cwc, 1)

            def fill(m, it):
                n = m % N
                before = 0 if it is None else it * M
                at_ = 0 if it is None else (it + 1) % (PASSES // SUBS) * SUBS if m >= M else it * SUBS + m // N
                x = [t[:, ds(at_ * BANK, BANK)] for t in x16]
                pe.wait_ge(s_silu, before + m + 1)
                pe.wait_ge(s_hid, before + m + 1)
                for k, dst in enumerate((gbank[m % RING], ubank[m % RING])):
                    for i, (a_, b_) in enumerate(((0, 0), (0, 1), (1, 0))):
                        mm = nc.tensor.matmul(dst[:, :], w_gu[a_][:, k, n, :], x[b_], start=(i == 0), stop=(i == 2))
                if n < NPAIR:
                    for j in range(TG):
                        mm = nc.tensor.matmul(cbank[m % RING][:, j * P:(j + 1) * P],
                                              select[:, j, 2 * n:2 * n + 2, :].rearrange("p e f -> p (e f)"),
                                              cwT[:, ds(at_, 1), :].rearrange("p t d -> p (t d)"), start=True, stop=True)
                mm.then_inc(s_fill, 1)

            def down(m, it):
                n = m % N
                pe.wait_ge(s_hid, it * M + (RING + m + 1))
                if n == 0:
                    pe.wait_ge(s_yt, it * SUBS + m // N)
                nc.tensor.matmul(ybank[:, :], w_d[:, n, :], hid[m % RING][:, :], start=(n == 0),
                                 stop=(n == N - 1)).then_inc(s_down, 1)

            def turn(sub, it):
                pe.wait_ge(s_yt, it * SUBS + (sub + 1))
                pe.wait_ge(s_r, it * SUBS + sub)
                for j in range(TG):
                    mm = nc.tensor.transpose(tbank[:, j * P:(j + 1) * P], yT[:, j * P:(j + 1) * P], ident[:, :])
                mm.then_inc(s_turn, 1)

            for m in range(AHEAD):
                fill(m, None)
            with pe.Fori(0, PASSES // SUBS) as it:
                down(0, it)
                for m in range(AHEAD, M + AHEAD):
                    fill(m, it)
                    if m % N == 1:
                        turn(m // N - 1, it)
                    if m <= M:
                        down(m - 1, it)

        @block.scalar
        def _(act):
            with act.Fori(0, PASSES) as it:
                w = ds(it * BANK, BANK)
                nc.scalar.activation(x16[0][:, w], xnT[:, w], ACT.Copy).then_inc(s_xh, 1)
            act.wait_ge(s_w, 16 * LOADS)
            nc.scalar.activation(w_gu[0][:, :, :, :], w_in[:, :, :, :], ACT.Copy).then_inc(s_whi, 1)
            act.wait_ge(s_route, 2)
            nc.scalar.activation(prob[:, :, :], prob[:, :, :], ACT.Exp).then_inc(s_exp, 1)

            def gate(m, before):
                act.wait_ge(s_fill, before + m + 1)
                act.wait_ge(s_hid, before + m + 1)
                nc.scalar.activation(silu[m % RING][:, :], gbank[m % RING][:, :], ACT.Silu).then_inc(s_silu, 1)

            for m in range(AHEAD):
                gate(m, 0)
            with act.Fori(0, PASSES // SUBS) as it:
                for m in range(AHEAD, M + AHEAD):
                    gate(m, it * M)
                    if m % N == 0:
                        act.wait_ge(s_down, it * M + (RING + m))
                        act.wait_ge(s_turn, it * SUBS + (m // N - 1))
                        nc.scalar.activation(yT[:, :], ybank[:, :], ACT.Copy).then_inc(s_yt, 1)

        @block.vector
        def _(dve):
            tt = nc.vector.tensor_tensor
            dve.wait_ge(s_wr, 16)
            nc.vector.tensor_copy(w_r[0][:, :], wr_in[:, :]).then_inc(s_split, 1)
            dve.wait_ge(s_split, 1)
            tt(w_r[1][:, :], wr_in[:, :], w_r[0][:, :], ALU.subtract).then_inc(s_split, 1)
            with dve.Fori(0, PASSES) as it:
                w = ds(it * BANK, BANK)
                dve.wait_ge(s_xh, it + 1)
                tt(x16[1][:, w], xnT[:, w], x16[0][:, w], ALU.subtract).then_inc(s_xl, 1)
            dve.wait_ge(s_whi, 1)
            tt(w_gu[1][:, :, :, :], w_in[:, :, :, :], w_gu[0][:, :, :, :], ALU.subtract).then_inc(s_split, 1)

            def each(x):
                return x[:, :].unsqueeze(2).to_broadcast([P, TT, E])

            def reduce(dst, src, op):
                return nc.vector.tensor_reduce(dst[:, :], src[:, :, :], AX.X, op)

            c = Steps()
            dve.wait_ge(s_logit, PASSES)
            logits = gbank[0][:, 0:TT * E].rearrange("p (t e) -> p t e", e=E)
            nc.vector.tensor_reduce(best[:, :], logits, AX.X, ALU.max).then_inc(s_route, 1)
            dve.wait_ge(s_route, c.up())
            tt(prob[:, :, :], logits, each(best), ALU.subtract).then_inc(s_route, 1)
            dve.wait_ge(s_route, c.up())
            dve.wait_ge(s_exp, 1)
            reduce(best, prob, ALU.add).then_inc(s_route, 1)
            dve.wait_ge(s_route, c.up())
            nc.vector.reciprocal(best[:, :], best[:, :]).then_inc(s_route, 1)
            dve.wait_ge(s_route, c.up())
            tt(prob[:, :, :], prob[:, :, :], each(best), ALU.mult).then_inc(s_route, 1)
            dve.wait_ge(s_route, c.up())
            dve.wait_ge(s_id, E)
            lower_first = order[:, :].unsqueeze(1).to_broadcast([P, TT, E])
            for k in range(TOP):
                src = left if k else prob
                reduce(best, src, ALU.max).then_inc(s_route, 1)
                dve.wait_ge(s_route, c.up())
                tt(mark[:, :, :], src[:, :, :], each(best), ALU.is_equal).then_inc(s_route, 1)
                dve.wait_ge(s_route, c.up())
                tt(mark[:, :, :], mark[:, :, :], lower_first, ALU.mult).then_inc(s_route, 1)
                dve.wait_ge(s_route, c.up())
                reduce(best, mark, ALU.max).then_inc(s_route, 1)
                dve.wait_ge(s_route, c.up())
                tt(pick[:, :, :], lower_first, each(best), ALU.is_equal).then_inc(s_route, 1)
                dve.wait_ge(s_route, c.up())
                if k == 0:
                    tt(cw[:, :, :], prob[:, :, :], pick[:, :, :], ALU.mult).then_inc(s_route, 1)
                    dve.wait_ge(s_route, c.up())
                    nc.vector.scalar_tensor_tensor(out=left[:, :, :], in0=pick[:, :, :], scalar=-2.0,
                                                   in1=prob[:, :, :], op0=ALU.mult, op1=ALU.add).then_inc(s_route, 1)
                    dve.wait_ge(s_route, c.up())
                else:
                    tt(mark[:, :, :], prob[:, :, :], pick[:, :, :], ALU.mult).then_inc(s_route, 1)
                    dve.wait_ge(s_route, c.up())
                    tt(cw[:, :, :], cw[:, :, :], mark[:, :, :], ALU.add).then_inc(s_route, 1)
                    dve.wait_ge(s_route, c.up())
            nc.vector.tensor_copy(cw16[:, :, 0, :], cw[:, :, :]).then_inc(s_split, 1)
            dve.wait_ge(s_split, 4)
            tt(cw16[:, :, 1, :], cw[:, :, :], cw16[:, :, 0, :], ALU.subtract).then_inc(s_split, 1)
            dve.wait_ge(s_cwt, 1)
            nc.vector.tensor_copy(cwT[:, :, :], cbank[0][:, :].bitcast(F16)[:, 0:PASSES * P].rearrange("p (i d) -> p i d", d=P)).then_inc(s_cwc, 1)

            def hidden(m, it):
                before = 0 if it is None else it * M
                dve.wait_ge(s_silu, before + (RING + m + 1))
                dve.wait_ge(s_down, before + m + 1)
                h = hid[m % RING]
                gated = tt(h[:, :], ubank[m % RING][:, :], silu[m % RING][:, :], ALU.mult)
                if m % N == NPAIR:
                    gated.then_inc(s_hid, 1)
                else:
                    gated.then_inc(s_gate, 1)
                    dve.wait_ge(s_gate, (0 if it is None else it * (SUBS * NPAIR)) + m + 1 - (m + 1) // N)
                    tt(h[:, :], cbank[m % RING][:, :], h[:, :], ALU.mult).then_inc(s_hid, 1)

            for m in range(AHEAD):
                hidden(m, None)
            with dve.Fori(0, PASSES // SUBS) as it:
                for m in range(AHEAD, M + AHEAD):
                    hidden(m, it)
                    if m % N == 1:
                        sub = m // N - 1
                        dve.wait_ge(s_turn, it * SUBS + (sub + 1))
                        x = resid[:, ds(it * (SUBS * TG) + sub * TG, TG), :]
                        tt(x, tbank[:, :].rearrange("p (t d) -> p t d", d=D), x, ALU.add).then_inc(s_r, 1)


def program(nc, a, out):
    B, SQ, D = a["x"].shape
    TT = B * SQ // P
    with ExitStack() as ctx:
        resid = ctx.enter_context(nc.sbuf_tensor("resid", [P, TT, D], F32))
        xnT = ctx.enter_context(nc.sbuf_tensor("xnT", [D, B * SQ], F32))
        stats = ctx.enter_context(nc.sbuf_tensor("stats", [P, TT, 6], F32))
        ident = ctx.enter_context(nc.sbuf_tensor("ident", [P, P], F32))
        s_in = ctx.enter_context(nc.semaphore("x_in"))
        s_id = ctx.enter_context(nc.semaphore("ident_steps"))
        s_out = ctx.enter_context(nc.semaphore("out_written"))
        x_tiles = a["x"].rearrange("b (q p) d -> p (b q) d", p=P)
        out_tiles = out.rearrange("b (q p) d -> p (b q) d", p=P)

        with nc.Block() as block:
            @block.sync
            def _(sp):
                sp.dma_start(resid[:, :, :], x_tiles).then_inc(s_in, 16)
                sp.wait_ge(s_in, 16)

            @block.gpsimd
            def _(pool):
                nc.gpsimd.memset(ident[:, :], 0.0).then_inc(s_id, 1)
                pool.wait_ge(s_id, 1)
                nc.gpsimd.affine_select(out=ident[:, :], in_=ident[:, :], compare_op=ALU.not_equal, fill=1.0,
                                        base=0, pattern=[[-1, P]], channel_multiplier=1).then_inc(s_id, 1)
                pool.wait_ge(s_id, 2)
        nc.all_engine_barrier()
        layernorm(nc, resid, xnT, ident, stats, TT, "ln0", first=True)
        nc.all_engine_barrier()
        cross_attention_0(nc, resid, stats, xnT, ident, a["ctx_1024"], a["mask_BxSxS2_ik1"],
                          *(a["L0_xattn_" + n] for n in ("Wq", "bq", "Wk", "bk", "Wv", "bv", "Wo", "bo")), B, SQ)
        nc.all_engine_barrier()
        layernorm(nc, resid, xnT, ident, stats, TT, "ln1")
        nc.all_engine_barrier()
        moe_ffn_0(nc, resid, stats, xnT, ident, *(a["L0_ffn_" + n] for n in (
            "gate_w", "gate_b", "dp_w1", "dp_b1", "dp_w2", "dp_b2", "ew1", "eb1", "ew2", "eb2")), TT)
        nc.all_engine_barrier()
        layernorm(nc, resid, xnT, ident, stats, TT, "ln2")
        nc.all_engine_barrier()
        cross_attention_1(nc, resid, stats, xnT, ident, a["ctx_1024"], a["mask_BxS_ik0"],
                          *(a["L1_xattn_" + n] for n in ("Wq", "Wkv", "Wout", "bout")), B, SQ)
        nc.all_engine_barrier()
        layernorm(nc, resid, xnT, ident, stats, TT, "ln3")
        nc.all_engine_barrier()
        moe_ffn_1(nc, resid, xnT, ident, *(a["L1_ffn_" + n] for n in ("Wr", "Wg", "Wu", "Wd", "Sg", "Su", "Sd")), TT)
        nc.all_engine_barrier()
        with nc.Block() as block:
            @block.sync
            def _(sp):
                sp.dma_start(out_tiles, resid[:, :, :]).then_inc(s_out, 16)
                sp.wait_ge(s_out, 16)


_INS = ("x", "ctx_1024", "mask_BxSxS2_ik1", "mask_BxS_ik0",
        "L0_xattn_Wq", "L0_xattn_bq", "L0_xattn_Wk", "L0_xattn_bk", "L0_xattn_Wv", "L0_xattn_bv",
        "L0_xattn_Wo", "L0_xattn_bo", "L0_ffn_gate_w", "L0_ffn_gate_b", "L0_ffn_dp_w1", "L0_ffn_dp_b1",
        "L0_ffn_dp_w2", "L0_ffn_dp_b2", "L0_ffn_ew1", "L0_ffn_eb1", "L0_ffn_ew2", "L0_ffn_eb2",
        "L1_xattn_Wq", "L1_xattn_Wkv", "L1_xattn_Wout", "L1_xattn_bout", "L1_ffn_Wr", "L1_ffn_Wg",
        "L1_ffn_Wu", "L1_ffn_Wd", "L1_ffn_Sg", "L1_ffn_Su", "L1_ffn_Sd")


def kernel(**inputs):
    import numpy as _np
    import concourse.bacc as _bacc
    from concourse import mybir as _mybir
    from concourse.bass_utils import run_bass_kernel_spmd as _run

    nc = _bacc.Bacc("TRN2", target_bir_lowering=False, num_devices=1)
    arrays, a = {}, {}
    for name in _INS:
        arr = _np.ascontiguousarray(inputs[name])
        arrays["in_" + name + "_dram"] = arr
        a[name] = nc.dram_tensor("in_" + name + "_dram", arr.shape, _mybir.dt.from_np(arr.dtype),
                                 kind="ExternalInput").ap()
    out = nc.dram_tensor("out_0_dram", inputs["x"].shape, _mybir.dt.float32, kind="ExternalOutput").ap()
    program(nc, a, out)
    return _run(nc, [arrays], core_ids=[0]).results[0]["out_0_dram"]
```
